# Optimizing a Trainium2 kernel written in Bass

```python
import numpy as np
import jax
import jax.numpy as jnp

def _softmax(x, axis=-1):
    return jax.nn.softmax(x, axis=axis)

def _gelu(x):
    return jax.nn.gelu(x, approximate=True)

def _silu(x):
    return jax.nn.silu(x)

def _sigmoid(x):
    return jax.nn.sigmoid(x)

def _layernorm(x, axis=-1, eps=1e-05):
    m = jnp.mean(x, axis=axis, keepdims=True)
    v = jnp.var(x, axis=axis, keepdims=True)
    return (x - m) / jnp.sqrt(v + eps)

def _scatter_add(tgt, idx, src, axis=0):
    return tgt.at[idx].add(src)

def _segment_sum(src, seg, n):
    return jax.ops.segment_sum(src, seg, n)
kernel_name = 'mk_adj_ffn_d2_adj_r2_f9a2c1'

def setup_inputs(seed: int=0):
    np.random.seed(seed)
    _w = jnp.asarray

    def _rec_inputs():
        import jax
        import jax.numpy as jnp
        _gk = jax.random.key(seed)
        x = -0.0002928 + 1 * jax.random.normal(jax.random.fold_in(_gk, 1), (1354, 256), jnp.float32)
        _a = jax.random.bernoulli(jax.random.fold_in(_gk, 2), 0.00295421, (1354, 1354))
        _a = jnp.logical_or(_a, jnp.eye(1354, dtype=bool))
        _af = _a.astype(jnp.float32)
        _af = _af * jax.random.uniform(jax.random.fold_in(_gk, 3), (1354, 1354), jnp.float32, 0.05, 1)
        adj = _af
        return (x, adj)
    x, adj = _rec_inputs()

    def _L0_gnn_setup():
        import jax, jax.numpy as jnp
        import numpy as np
        N = 4096
        DIN = 256
        DOUT = 256
        TAU = 1.0
        EPS = 1e-08
        NORM_EPS = 1e-08
        key = jax.random.key(seed)
        k1, k2, k3 = jax.random.split(key, 3)
        x = jax.random.normal(k1, (N, DIN), dtype=jnp.float32)
        adj = jax.random.uniform(k2, (N, N), dtype=jnp.float32)
        limit = float(np.sqrt(6.0 / (DIN + DOUT)))
        weight = jax.random.uniform(k3, (DIN, DOUT), dtype=jnp.float32, minval=-limit, maxval=limit)
        bias = jnp.zeros((DOUT,), dtype=jnp.float32)
        return {'x': x, 'adj': adj, 'weight': weight, 'bias': bias}
    _L0_gnn_all = _L0_gnn_setup()
    _L0_gnn_in = {k: v for k, v in _L0_gnn_all.items() if k in ('weight', 'bias')}
    del _L0_gnn_all

    def _L0_ffn_setup():
        import jax, jax.numpy as jnp
        import numpy as np
        B, S, H, E, K, DF, SH = (8, 2048, 256, 8, 2, 128, 256)
        key = jax.random.key(seed)
        ks = jax.random.split(key, 10)
        n = lambda i, shape, sc: jax.random.normal(ks[i], shape, jnp.float32) * sc
        return {'hidden_states': n(0, (B, S, H), 1.0), 'gate_w': n(1, (E, H), 0.05), 'w1': n(2, (E, H, DF), 0.05), 'b1': n(3, (E, DF), 0.01), 'w2': n(4, (E, DF, H), 0.05), 'b2': n(5, (E, H), 0.01), 'sw1': n(6, (H, SH), 0.05), 'sb1': n(7, (SH,), 0.01), 'sw2': n(8, (SH, H), 0.05), 'sb2': n(9, (H,), 0.01)}
    _L0_ffn_all = _L0_ffn_setup()
    _L0_ffn_in = {k: v for k, v in _L0_ffn_all.items() if k in ('gate_w', 'w1', 'b1', 'w2', 'b2', 'sw1', 'sb1', 'sw2', 'sb2')}
    del _L0_ffn_all

    def _L1_gnn_setup():
        import jax, jax.numpy as jnp
        import numpy as np
        N = 2048
        D_IN = 256
        D_OUT = 256
        key = jax.random.key(seed)
        k1, k2, k3 = jax.random.split(key, 3)
        X = jax.random.normal(k1, (N, D_IN), dtype=jnp.float32)
        A = jax.random.uniform(k2, (N, N), dtype=jnp.float32)
        W = jax.random.normal(k3, (D_OUT, D_IN), dtype=jnp.float32) * (1.0 / np.sqrt(D_IN))
        return {'X': X, 'A': A, 'W': W}
    _L1_gnn_all = _L1_gnn_setup()
    _L1_gnn_in = {k: v for k, v in _L1_gnn_all.items() if k in ('W',)}
    del _L1_gnn_all

    def _L1_ffn_setup():
        import jax, jax.numpy as jnp
        import numpy as np
        D, NH, HID, E = (256, 8, 1024, 8)
        EPS = 1e-05

        def _layernorm(x, g, b):
            mu = jnp.mean(x, axis=-1, keepdims=True)
            var = jnp.mean(jnp.square(x - mu), axis=-1, keepdims=True)
            return (x - mu) * jax.lax.rsqrt(var + EPS) * g + b
        key = jax.random.key(seed)
        ks = jax.random.split(key, 20)
        s = 0.02
        inp = {'x': jax.random.normal(ks[0], (4, 512, D), jnp.float32), 'Wq': jax.random.normal(ks[1], (D, D), jnp.float32) * s, 'bq': jnp.zeros((D,), jnp.float32), 'Wk': jax.random.normal(ks[2], (D, D), jnp.float32) * s, 'bk': jnp.zeros((D,), jnp.float32), 'Wv': jax.random.normal(ks[3], (D, D), jnp.float32) * s, 'bv': jnp.zeros((D,), jnp.float32), 'Wo': jax.random.normal(ks[4], (D, D), jnp.float32) * s, 'bo': jnp.zeros((D,), jnp.float32), 'g1': jnp.ones((D,), jnp.float32), 'beta1': jnp.zeros((D,), jnp.float32), 'g2': jnp.ones((D,), jnp.float32), 'beta2': jnp.zeros((D,), jnp.float32), 'Wg': jax.random.normal(ks[5], (D, E), jnp.float32) * s, 'bg': jnp.zeros((E,), jnp.float32), 'W1': jax.random.normal(ks[6], (E, D, HID), jnp.float32) * s, 'b1': jnp.zeros((E, HID), jnp.float32), 'W2': jax.random.normal(ks[7], (E, HID, D), jnp.float32) * s, 'b2': jnp.zeros((E, D), jnp.float32)}
        return inp
    _L1_ffn_all = _L1_ffn_setup()
    _L1_ffn_in = {k: v for k, v in _L1_ffn_all.items() if k in ('Wq', 'bq', 'Wk', 'bk', 'Wv', 'bv', 'Wo', 'bo', 'g1', 'beta1', 'g2', 'beta2', 'Wg', 'bg', 'W1', 'b1', 'W2', 'b2')}
    del _L1_ffn_all
    return {'x': x, 'adj': adj, 'L0_gnn_weight': _L0_gnn_in['weight'], 'L0_gnn_bias': _L0_gnn_in['bias'], 'L0_ffn_gate_w': _L0_ffn_in['gate_w'], 'L0_ffn_w1': _L0_ffn_in['w1'], 'L0_ffn_b1': _L0_ffn_in['b1'], 'L0_ffn_w2': _L0_ffn_in['w2'], 'L0_ffn_b2': _L0_ffn_in['b2'], 'L0_ffn_sw1': _L0_ffn_in['sw1'], 'L0_ffn_sb1': _L0_ffn_in['sb1'], 'L0_ffn_sw2': _L0_ffn_in['sw2'], 'L0_ffn_sb2': _L0_ffn_in['sb2'], 'L1_gnn_W': _L1_gnn_in['W'], 'L1_ffn_Wq': _L1_ffn_in['Wq'], 'L1_ffn_bq': _L1_ffn_in['bq'], 'L1_ffn_Wk': _L1_ffn_in['Wk'], 'L1_ffn_bk': _L1_ffn_in['bk'], 'L1_ffn_Wv': _L1_ffn_in['Wv'], 'L1_ffn_bv': _L1_ffn_in['bv'], 'L1_ffn_Wo': _L1_ffn_in['Wo'], 'L1_ffn_bo': _L1_ffn_in['bo'], 'L1_ffn_g1': _L1_ffn_in['g1'], 'L1_ffn_beta1': _L1_ffn_in['beta1'], 'L1_ffn_g2': _L1_ffn_in['g2'], 'L1_ffn_beta2': _L1_ffn_in['beta2'], 'L1_ffn_Wg': _L1_ffn_in['Wg'], 'L1_ffn_bg': _L1_ffn_in['bg'], 'L1_ffn_W1': _L1_ffn_in['W1'], 'L1_ffn_b1': _L1_ffn_in['b1'], 'L1_ffn_W2': _L1_ffn_in['W2'], 'L1_ffn_b2': _L1_ffn_in['b2']}

def reference(x, adj, L0_gnn_weight, L0_gnn_bias, L0_ffn_gate_w, L0_ffn_w1, L0_ffn_b1, L0_ffn_w2, L0_ffn_b2, L0_ffn_sw1, L0_ffn_sb1, L0_ffn_sw2, L0_ffn_sb2, L1_gnn_W, L1_ffn_Wq, L1_ffn_bq, L1_ffn_Wk, L1_ffn_bk, L1_ffn_Wv, L1_ffn_bv, L1_ffn_Wo, L1_ffn_bo, L1_ffn_g1, L1_ffn_beta1, L1_ffn_g2, L1_ffn_beta2, L1_ffn_Wg, L1_ffn_bg, L1_ffn_W1, L1_ffn_b1, L1_ffn_W2, L1_ffn_b2):
    import jax
    import jax.numpy as jnp

    def _L0_gnn_ref(x, adj, weight, bias):
        import jax, jax.numpy as jnp
        import numpy as np
        N = 4096
        DIN = 256
        DOUT = 256
        TAU = 1.0
        EPS = 1e-08
        NORM_EPS = 1e-08
        h = x @ weight
        norm = jnp.linalg.norm(h, axis=1, keepdims=True)
        h_norm = h / jnp.maximum(norm, NORM_EPS)
        sim = h_norm @ h_norm.T
        attn_logits = sim / TAU + jnp.log(adj + EPS)
        attn = jax.nn.softmax(attn_logits, axis=1)
        out = attn @ h + bias
        return out

    def _L0_ffn_ref(hidden_states, gate_w, w1, b1, w2, b2, sw1, sb1, sw2, sb2):
        import jax, jax.numpy as jnp
        import numpy as np
        B, S, H, E, K, DF, SH = (8, 2048, 256, 8, 2, 128, 256)
        x = hidden_states
        xf = x.reshape(-1, x.shape[-1])
        T = xf.shape[0]
        scores = jax.nn.softmax(xf @ gate_w.T, axis=-1)
        topk_w, topk_i = jax.lax.top_k(scores, K)
        topk_w = topk_w / (topk_w.sum(-1, keepdims=True) + 1e-20)
        combine = jnp.zeros((T, E), xf.dtype).at[jnp.arange(T)[:, None], topk_i].add(topk_w)
        h1 = jax.nn.relu(jnp.einsum('th,ehf->tef', xf, w1) + b1)
        eo = jnp.einsum('tef,efh->teh', h1, w2) + b2
        y = jnp.einsum('te,teh->th', combine, eo)
        shared = jax.nn.relu(xf @ sw1 + sb1) @ sw2 + sb2
        return (y + shared).reshape(x.shape)

    def _L1_gnn_ref(X, A, W):
        import jax, jax.numpy as jnp
        import numpy as np
        N = 2048
        D_IN = 256
        D_OUT = 256
        A2 = A + jnp.eye(A.shape[0], dtype=A.dtype)
        dscale = jnp.diagonal(A2) ** (-0.5)
        temp = A2 @ X @ W.T
        A_norm = dscale[:, None] * A2 * dscale[None, :]
        return jax.nn.relu(A_norm @ temp)

    def _L1_ffn_ref(x, Wq, bq, Wk, bk, Wv, bv, Wo, bo, g1, beta1, g2, beta2, Wg, bg, W1, b1, W2, b2):
        import jax, jax.numpy as jnp
        import numpy as np
        D, NH, HID, E = (256, 8, 1024, 8)
        EPS = 1e-05

        def _layernorm(x, g, b):
            mu = jnp.mean(x, axis=-1, keepdims=True)
            var = jnp.mean(jnp.square(x - mu), axis=-1, keepdims=True)
            return (x - mu) * jax.lax.rsqrt(var + EPS) * g + b
        B, S, _ = x.shape
        dh = D // NH
        q = (x @ Wq + bq).reshape(B, S, NH, dh)
        k = (x @ Wk + bk).reshape(B, S, NH, dh)
        v = (x @ Wv + bv).reshape(B, S, NH, dh)
        scores = jnp.einsum('bqhd,bkhd->bhqk', q, k) / jnp.sqrt(jnp.float32(dh)).astype(x.dtype)
        attn = jax.nn.softmax(scores, axis=-1)
        ctx = jnp.einsum('bhqk,bkhd->bqhd', attn, v).reshape(B, S, D)
        sa = ctx @ Wo + bo
        x = _layernorm(x + sa, g1, beta1)
        t = x.reshape(-1, D)
        logits = t @ Wg + bg
        idx = jnp.argmax(logits, axis=-1)
        h = jax.nn.gelu(jnp.einsum('td,edh->teh', t, W1) + b1, approximate=False)
        y = jnp.einsum('teh,ehd->ted', h, W2) + b2
        onehot = jax.nn.one_hot(idx, E, dtype=t.dtype)
        moe = jnp.einsum('ted,te->td', y, onehot).reshape(B, S, D)
        return _layernorm(x + moe, g2, beta2)
    x = x + _L0_gnn_ref(_layernorm(x, axis=-1), adj, L0_gnn_weight, L0_gnn_bias)
    x = x + _L0_ffn_ref(_layernorm(x, axis=-1)[None], L0_ffn_gate_w, L0_ffn_w1, L0_ffn_b1, L0_ffn_w2, L0_ffn_b2, L0_ffn_sw1, L0_ffn_sb1, L0_ffn_sw2, L0_ffn_sb2)[0]
    x = x + _L1_gnn_ref(_layernorm(x, axis=-1), adj, L1_gnn_W)
    x = x + _L1_ffn_ref(_layernorm(x, axis=-1)[None], L1_ffn_Wq, L1_ffn_bq, L1_ffn_Wk, L1_ffn_bk, L1_ffn_Wv, L1_ffn_bv, L1_ffn_Wo, L1_ffn_bo, L1_ffn_g1, L1_ffn_beta1, L1_ffn_g2, L1_ffn_beta2, L1_ffn_Wg, L1_ffn_bg, L1_ffn_W1, L1_ffn_b1, L1_ffn_W2, L1_ffn_b2)[0]
    return x

_drawn_inputs = setup_inputs


def setup_inputs(seed=0):
    import zlib

    import numpy as np

    out = dict(_drawn_inputs(seed))
    spreads = {'L0_gnn_bias': (0.0, 0.1),
     'L1_ffn_bq': (0.0, 0.8),
     'L1_ffn_bk': (0.0, 0.8),
     'L1_ffn_bv': (0.0, 0.8),
     'L1_ffn_bo': (0.0, 0.283),
     'L1_ffn_g1': (1.0, 0.2),
     'L1_ffn_beta1': (0.0, 0.286),
     'L1_ffn_g2': (1.0, 0.2),
     'L1_ffn_beta2': (0.0, 0.323),
     'L1_ffn_bg': (0.0, 0.344),
     'L1_ffn_b1': (0.0, 0.8),
     'L1_ffn_b2': (0.0, 0.328)}
    factors = {'L0_ffn_b1': 8.0,
     'L0_ffn_b2': 6.813,
     'L0_ffn_sb1': 7.669,
     'L0_ffn_sb2': 3.026,
     'L1_ffn_Wq': 8.0,
     'L1_ffn_Wk': 8.0,
     'L1_ffn_Wv': 5.309,
     'L1_ffn_Wo': 3.714}
    for name, (base, spread) in spreads.items():
        noise = np.random.default_rng([zlib.crc32(name.encode()), seed]).standard_normal(out[name].shape)
        drawn = base * np.exp(spread * noise) if base else spread * noise
        out[name] = jnp.asarray(drawn.astype(out[name].dtype))
    for name, factor in factors.items():
        out[name] = (out[name] * factor).astype(out[name].dtype)
    return out
```

```python
import numpy as np
import concourse.bass as bass
from concourse import mybir
from contextlib import ExitStack

F32 = mybir.dt.float32
F32R = mybir.dt.float32r
BF16 = mybir.dt.bfloat16
I32 = mybir.dt.int32
U32 = mybir.dt.uint32
ALU = mybir.AluOpType
ACT = mybir.ActivationFunctionType
AX = mybir.AxisListType

P = 128
R = 1354
D = 256
H2 = D // P
T = (R + P - 1) // P
LAST = R - (T - 1) * P
NC = 3
CW = 452
RW = NC * CW
G = (T + 1) // 2
E0, F0, S0 = 8, 128, 256
HEADS, DH = 8, 32
PAIRS = HEADS // 2
KA = 3 * DH
E1, HID = 8, 1024
FC = HID // P
SLOTS = (R + E1 * (P - 1)) // P
BLOB = 2 * H2 * HID + FC + D
NORM_EPS = 1e-8
LN_EPS = 1e-5


def rows(t):
    return P if t < T - 1 else LAST


def cols(t):
    return slice(t * P, t * P + rows(t))


def chunk(c):
    return slice(c * CW, (c + 1) * CW)


def build(nc, x, adjT, w_gnn, b_gnn, gate_wT, w1, b1T, w2, b2, sw1, sb1T, sw2, sb2, w_gnn1T,
          wq, bqT, wk, bkT, wv, bv, wo, bo, g1, beta1, g2, beta2, wg, bg, blob, out):
    ctx = ExitStack()
    with ctx:
        def sb(name, shape, dt=F32):
            return ctx.enter_context(nc.sbuf_tensor(name, shape, dt))

        def sem(name):
            return ctx.enter_context(nc.semaphore(name))

        ps = ctx.enter_context(nc.psum_tensor("ps", [P, 8, 512], F32))

        ident = sb("ident", [P, P])
        ones2 = sb("ones2", [P, 2])
        xt = sb("xt", [P, T, D])
        xn = sb("xn", [P, T, D])
        xT = sb("xT", [P, H2, RW])
        st = sb("st", [P, T, 6])
        mv = sb("mv", [P, T, 2])
        rstd = sb("rstd", [P, T])
        std = sb("std", [P, T])
        eps_s = sb("eps_s", [P, 1])

        w_gnn_s = sb("w_gnn_s", [P, H2, D])
        b_gnn_s = sb("b_gnn_s", [P, D])

        ht = sb("ht", [P, T, D])
        zero = sb("zero", [P, D])
        lg = sb("lg", [P, T, E0])
        top = sb("top", [P, T, 8])
        topi = sb("topi", [P, T, 8], U32)
        iota8 = sb("iota8", [P, E0])

        phase = ctx.enter_context(ExitStack())

        def sbp(name, shape, dt=F32):
            return phase.enter_context(nc.sbuf_tensor(name, shape, dt))

        adj = sbp("adj", [P, T, RW])
        hn = sbp("hn", [P, T, D])
        hT = sbp("hT", [P, H2, RW])
        sq = sbp("sq", [P, D])
        ss = sbp("ss", [P, T])
        norm = sbp("norm", [P, T])
        rnorm = sbp("rnorm", [P, T])
        NE = 2
        ex = sbp("ex", [P, NE, RW])
        ee = sbp("ee", [P, NE, RW])
        esum = sbp("esum", [P, RW])
        rden = sbp("rden", [P, T])

        EX = E0 + S0 // F0
        gate_s = sbp("gate_s", [P, H2, E0])
        w1_s = sbp("w1_s", [P, EX, H2, F0])
        w2_s = sbp("w2_s", [P, EX, D])
        b1_s = sbp("b1_s", [P, EX])
        b2_s = sbp("b2_s", [E0 + 1, D])
        mx = sbp("mx", [P, T])
        z = sbp("z", [P, T])
        topf = sbp("topf", [P, T, 2])
        pick = sbp("pick", [P, T, E0])
        comb = sbp("comb", [P, T, EX])
        combT = sbp("combT", [E0 + 1, RW])
        w_gnn1_s = sbp("w_gnn1_s", [P, H2, D])
        dg = sbp("dg", [P, T])
        dgs = sbp("dgs", [P, T])
        dscale = sbp("dscale", [P, T])

        phase.close()
        wq_s, wk_s, wv_s, wo_s = (sbp(f"w{n}_s", [P, H2, D]) for n in "qkvo")
        bq_s, bk_s = (sbp(f"b{n}_s", [P, H2]) for n in "qk")
        bv_s, bo_s, g1_s, beta1_s = (sbp(f"{n}_s", [P, D]) for n in ("bv", "bo", "g1", "beta1"))
        pr32 = sbp("pr32", [P, 2, RW])
        hi = [sbp(f"{n}_hi", [P, H2, RW], F32R) for n in "qk"]
        lo = [sbp(f"{n}_lo", [P, H2, RW], F32R) for n in "qk"]
        aug = [sbp(f"{n}_aug", [KA + 1, 2, 2, RW], F32R) for n in "qk"]
        va = sbp("va", [P, T, HEADS, 2 * DH])
        NPT = 2
        pt = sbp("pt", [P, NPT, 2, CW])
        acc = sbp("acc", [P, 2, CW])
        rec = sbp("rec", [P, CW])
        mxp = sbp("mxp", [P, 2, T, 2])
        nm = sbp("nm", [P, 2, T])
        mT = sbp("mT", [T, 2, P], F32R)
        cT = xT
        phase.close()
        wg_s = sbp("wg_s", [P, H2, E1])
        bg_s = sbp("bg_s", [P, E1])
        g2_s, beta2_s = (sbp(f"{n}_s", [P, D]) for n in ("g2", "beta2"))
        valid = sbp("valid", [P, T])
        before = sbp("before", [P, P], BF16)
        onesb = sbp("onesb", [P, P], BF16)
        lower = sbp("lower", [P, E1, E1])
        starts = sbp("starts", [P, SLOTS])
        oh = sbp("oh", [P, T, E1])
        ohb = sbp("ohb", [P, T, E1], BF16)
        best = sbp("best", [P, T])
        rank = sbp("rank", [P, T + 1, E1])
        cnt = sbp("cnt", [P, E1], I32)
        padded = sbp("padded", [P, E1])
        prod = sbp("prod", [P, E1, E1])
        base = sbp("base", [P, E1])
        ends = sbp("ends", [P, E1])
        pos = sbp("pos", [P, T])
        posi = sbp("posi", [P, T], U32)
        past = sbp("past", [P, SLOTS, E1])
        slotf = sbp("slotf", [P, SLOTS])
        sloti = sbp("sloti", [P, SLOTS], I32)
        NW = 3
        wexp = sbp("wexp", [P, NW, BLOB])
        xg = sbp("xg", [P, 2, D])
        xgT = sbp("xgT", [P, 2, H2, P])
        hid = sbp("hid", [P, 2, FC, P])
        yg = sbp("yg", [P, 2, D])
        moe = sbp("moe", [P, T, D])
        xs_d = nc.dram_tensor("xs_scratch", [SLOTS * P, D], F32).ap()
        ys_d = nc.dram_tensor("ys_scratch", [SLOTS * P, D], F32).ap()

        s_x = sem("x_loaded")
        s_wgnn = sem("gnn_weights_loaded")
        s_adj = [sem(f"adj_loaded_{n}") for n in range(2)]
        s_pad = sem("pads_cleared")
        s_id = sem("identity_ready")
        s_xb = sem("x_bias_added")

        ln_stats, ln_mean, ln_dev, ln_inv, ln_done = (
            sem(f"layernorm_{s}") for s in ("stats", "mean", "deviation", "inverse", "done"))
        turn_turned, turn_even, turn_odd = (sem(f"transposes_{s}") for s in ("turned", "even_copied", "odd_copied"))

        class LN:
            def __init__(self, n):
                self.n, self.tiles = n, n * T

            def wait_tile(self, eng, t):
                eng.wait_ge(ln_done, self.tiles + t + 1)

        class Turn:
            def __init__(self, n):
                self.n, self.groups, self.half = n, n * G, n * G // 2

            def wait_group(self, eng, g):
                eng.wait_ge(turn_even, self.half + g // 2 + 1)
                if g:
                    eng.wait_ge(turn_odd, self.half + (g + 1) // 2)

        ln0 = LN(0)
        tx = Turn(0)
        s_h = sem("h_projected")
        s_hc = sem("h_copied")
        s_ss = sem("h_squares_summed")
        s_nm = sem("h_norm_ready")
        s_rn = sem("h_norm_inverted")
        s_hn = sem("h_normalised")
        th = Turn(1)
        s_sim = sem("sim_ready")
        s_exp = sem("sim_exp_ready")
        s_e = sem("edge_weights_ready")
        s_agg = sem("aggregated")
        s_es = sem("edge_sums_added")
        s_den = sem("denominators_ready")
        s_rd = sem("denominators_inverted")
        s_x1 = sem("x1_ready")
        ln1 = LN(1)
        tx1 = Turn(2)
        s_w0 = sem("layer0_expert_weights_loaded")
        s_init = sem("stage_b_constants_ready")
        s_lg = sem("gate_logits_ready")
        s_r = sem("routing_steps")
        s_er = sem("routing_exp_ready")
        s_top = sem("top_scores_ready")
        s_comb = sem("combine_weights_ready")
        s_ct = sem("combine_turned")
        s_cc = sem("combineT_copied")
        s_up = sem("expert_up_ready")
        s_hid = sem("expert_hidden_ready")
        s_dn = sem("expert_down_ready")
        s_x2 = sem("x2_parts_added")
        ln2 = LN(2)
        s_self = sem("self_loops_added")
        s_dg = sem("diagonal_ready")
        s_dgs = sem("diagonal_root_ready")
        s_ds = sem("degree_scale_ready")
        s_g = sem("graph_product_ready")
        s_ga = sem("graph_product_even_copied")
        s_gv = sem("graph_product_odd_copied")
        s_t1 = sem("temp_ready")
        s_ts = sem("temp_scaled")
        s_p2 = sem("second_product_ready")
        s_rl = sem("second_product_rectified")
        s_x3 = sem("x3_ready")
        s_aw = sem("attention_weights_loaded")
        s_c3 = sem("stage_d_constants_ready")
        ln3 = LN(3)
        tx3 = Turn(3)
        s_dup = sem("pad_columns_doubled")
        s_pr = sem("projection_ready")
        s_pb = sem("projection_biased")
        s_hi = sem("hi_part_ready")
        s_lo = sem("lo_part_ready")
        s_v = sem("v_projected")
        s_vb = sem("v_biased")
        s_aug = [sem(f"pair_operands_{n}") for n in range(2)]
        s_s1 = sem("scores_for_max_ready")
        s_mx = sem("score_maxima_ready")
        s_neg = sem("negated_maxima_ready")
        s_mt = sem("maxima_turned")
        s_mc = sem("maxima_copied")
        s_mr = [sem(f"maxima_row_{n}") for n in range(2)]
        s_s2 = sem("scores_ready")
        s_p = sem("probabilities_ready")
        s_pv = sem("values_weighted")
        s_ac = sem("head_outputs_copied")
        s_rc = sem("row_sums_inverted")
        s_cx = sem("head_outputs_normalised")
        s_xo = sem("attention_residual_biased")
        s_o = sem("output_projected")
        s_u = sem("attention_added")
        ln4 = LN(4)
        s_gain = sem("ln4_gain_applied")
        s_t = sem("moe_input_ready")
        s_ew = sem("moe_small_weights_loaded")
        s_c4 = sem("stage_e_constants_ready")
        s_zd = sem("slots_zeroed")
        tx4 = Turn(4)
        s_l1 = sem("moe_logits_ready")
        s_k = sem("dispatch_steps")
        s_k2 = sem("best_expert_steps")
        s_oh = sem("choices_ready")
        s_rank = sem("ranks_ready")
        s_pos = sem("positions_ready")
        s_sl = sem("slot_experts_ready")
        s_sc = sem("tokens_scattered")
        s_w = [sem(f"expert_loaded_{n}") for n in range(NW)]
        s_xg = [sem(f"slot_tokens_loaded_{n}") for n in range(2)]
        s_gt = sem("slot_tokens_turned")
        s_gc = sem("slot_tokens_copied")
        s_f1 = sem("slot_up_ready")
        s_fg = sem("slot_gelu_ready")
        s_f2 = sem("slot_down_ready")
        s_y = sem("slot_output_ready")
        s_ys = [sem(f"slot_output_stored_{n}") for n in range(2)]
        s_ga2 = sem("outputs_gathered")
        s_u2 = sem("moe_added")
        ln5 = LN(5)
        s_gain2 = sem("ln5_gain_applied")
        s_x4 = sem("x4_parts")
        s_out = sem("output_stored")

        block = ctx.enter_context(nc.Block())

        def ln_std(act, s, eps=LN_EPS):
            act.wait_ge(ln_mean, s.tiles + T)
            act.activation(std[:], mv[:, :, 1], ACT.Sqrt, bias=eps_s[:]).then_inc(ln_dev, 1)

        def ln_steps(v, s, src, dst, before=None):
            for t in range(T + 1):
                if t < T:
                    if before:
                        before(t)
                    v.bn_stats(st[:, t, :], src[:, t, :]).then_inc(ln_stats, 1)
                if t:
                    v.wait_ge(ln_stats, s.tiles + t)
                    v.bn_aggr(mv[:, t - 1, :], st[:, t - 1, :]).then_inc(ln_mean, 1)
            v.wait_ge(ln_dev, s.n + 1)
            v.reciprocal(rstd[:], std[:]).then_inc(ln_inv, 1)
            v.wait_ge(ln_inv, s.n + 1)
            for t in range(T):
                v.tensor_scalar(dst[:, t, :], src[:, t, :], mv[:, t, 0:1], rstd[:, t:t + 1],
                                ALU.subtract, ALU.mult).then_inc(ln_done, 1)

        def turn_pe(pe, s, src, ready, banks, before=0):
            for g in range(G):
                pe.wait_ge(ready, before + min(2 * g + 2, T))
                if g >= len(banks):
                    s.wait_group(pe, g - len(banks))
                b = ps[:, banks[g % len(banks)], :].rearrange("p (k c) -> p k c", k=H2)
                for t in range(2 * g, min(2 * g + 2, T)):
                    for k in range(H2):
                        m = pe.transpose(b[:, k, (t - 2 * g) * P:(t - 2 * g) * P + rows(t)],
                                         src[0:rows(t), t, k * P:(k + 1) * P], ident[0:rows(t), 0:rows(t)])
                m.then_inc(turn_turned, 1)

        def turn_copy(eng, s, dst, banks, odd):
            for g in range(odd, G, 2):
                n = sum(rows(t) for t in range(2 * g, min(2 * g + 2, T)))
                eng.wait_ge(turn_turned, s.groups + g + 1)
                b = ps[:, banks[g % len(banks)], :].rearrange("p (k c) -> p k c", k=H2)
                o = dst[:, :, 2 * g * P:2 * g * P + n]
                if odd:
                    eng.tensor_copy(o, b[:, :, 0:n]).then_inc(turn_odd, 1)
                else:
                    eng.activation(o, b[:, :, 0:n], ACT.Copy).then_inc(turn_even, 1)

        def group(g):
            return range(2 * g, min(2 * g + 2, T))

        def gshape(ap, g):
            return ap.rearrange("p (t d) -> p t d", t=2)[0:rows(2 * g), 0:len(group(g)), :]

        def project(pe, src, wait_group, w, done, banks, freed):
            for g in range(G):
                wait_group(pe, g)
                if g >= len(banks):
                    pe.wait_ge(freed, 2 * (g - len(banks) + 1))
                for t in group(g):
                    for k in range(H2):
                        m = pe.matmul(half(banks[g % len(banks)], t)[0:rows(t), :], src[:, k, cols(t)], w[:, k, :],
                                      start=(k == 0), stop=(k == H2 - 1))
                m.then_inc(done, 1)

        def half(bank, t):
            return ps[:, bank, (t % 2) * D:(t % 2 + 1) * D]

        def route(v):
            v.wait_ge(s_lg, 1)
            v.wait_ge(s_init, 5)
            d = ps[:, 4, 0:E0 * T].rearrange("p (t e) -> p t e", e=E0)
            v.tensor_copy(lg[:, 0:T - 1, :], d[:, 0:T - 1, :])
            v.tensor_copy(lg[0:LAST, T - 1, :], d[0:LAST, T - 1, :]).then_inc(s_r, 1)
            v.wait_ge(s_r, 1)
            v.tensor_reduce(mx[:], lg[:], AX.X, ALU.max).then_inc(s_r, 1)
            v.wait_ge(s_r, 2)
            v.tensor_tensor(lg[:], lg[:], mx[:].unsqueeze(2).to_broadcast([P, T, E0]), ALU.subtract).then_inc(s_r, 1)
            v.wait_ge(s_er, 1)
            v.tensor_reduce(z[:], lg[:], AX.X, ALU.add).then_inc(s_r, 1)
            v.wait_ge(s_r, 4)
            v.reciprocal(z[:], z[:]).then_inc(s_r, 1)
            v.wait_ge(s_r, 5)
            v.tensor_tensor(lg[:], lg[:], z[:].unsqueeze(2).to_broadcast([P, T, E0]), ALU.mult).then_inc(s_r, 1)
            v.wait_ge(s_r, 6)
            for t in range(T):
                v.max(top[:, t, :], lg[:, t, :]).then_inc(s_top, 1)
            for t in range(T):
                v.wait_ge(s_top, t + 1)
                v.max_index(topi[:, t, :], top[:, t, :], lg[:, t, :]).then_inc(s_top, 1)
            v.tensor_reduce(z[:], top[:, :, 0:2], AX.X, ALU.add).then_inc(s_r, 1)
            v.wait_ge(s_r, 7)
            v.tensor_scalar(z[:], z[:], 1e-20, None, ALU.add).then_inc(s_r, 1)
            v.wait_ge(s_r, 8)
            v.reciprocal(z[:], z[:]).then_inc(s_r, 1)
            v.wait_ge(s_r, 9)
            v.tensor_tensor(top[:, :, 0:2], top[:, :, 0:2], z[:].unsqueeze(2).to_broadcast([P, T, 2]), ALU.mult).then_inc(s_r, 1)
            v.wait_ge(s_top, 2 * T)
            v.tensor_copy(topf[:], topi[:, :, 0:2]).then_inc(s_r, 1)
            v.wait_ge(s_r, 11)
            io = iota8[:].unsqueeze(1).to_broadcast([P, T, E0])
            first, second = (topf[:, :, a:a + 1].to_broadcast([P, T, E0]) for a in range(2))
            share1, share2 = (top[:, :, a:a + 1].to_broadcast([P, T, E0]) for a in range(2))
            cw = comb[:, :, 0:E0]
            v.tensor_tensor(cw, io, first, ALU.is_equal).then_inc(s_r, 1)
            v.tensor_tensor(pick[:], io, second, ALU.is_equal).then_inc(s_r, 1)
            v.wait_ge(s_r, 13)
            v.tensor_tensor(cw, cw, share1, ALU.mult).then_inc(s_r, 1)
            v.tensor_tensor(pick[:], pick[:], share2, ALU.mult).then_inc(s_r, 1)
            v.wait_ge(s_r, 15)
            v.tensor_tensor(cw, cw, pick[:], ALU.add).then_inc(s_comb, 1)
            v.wait_ge(s_comb, 1)

        @block.sync
        def _(sp):
            sp.wait_ge(s_pad, 4)
            sp.dma_start(xt[:, 0:T - 1, :], x[0:(T - 1) * P, :].rearrange("(t p) d -> p t d", p=P)).then_inc(s_x, 16)
            sp.dma_start(xt[0:LAST, T - 1, :], x[(T - 1) * P:R, :]).then_inc(s_x, 16)
            sp.dma_start(w_gnn_s[:], w_gnn.rearrange("(k p) o -> p k o", p=P)).then_inc(s_wgnn, 16)
            sp.dma_start(b_gnn_s[:], b_gnn.to_broadcast([P, D])).then_inc(s_wgnn, 16)
            for t in range(T):
                sp.dma_start(adj[0:rows(t), t, 0:R], adjT[t * P:t * P + rows(t), :]).then_inc(s_adj[t >= 2], 16)

            for e in range(E0):
                sp.dma_start(w1_s[:, e, :, :], w1[e].rearrange("(k p) f -> p k f", p=P)).then_inc(s_w0, 16)
            for e in range(E0, EX):
                sp.dma_start(w1_s[:, e, :, :], sw1[:, (e - E0) * F0:(e - E0 + 1) * F0].rearrange("(k p) f -> p k f", p=P)).then_inc(s_w0, 16)
            sp.dma_start(w2_s[:, 0:E0, :], w2.rearrange("e f h -> f e h")).then_inc(s_w0, 16)
            sp.dma_start(w2_s[:, E0:EX, :], sw2.rearrange("(c p) h -> p c h", p=P)).then_inc(s_w0, 16)
            sp.dma_start(b1_s[:, 0:E0], b1T).then_inc(s_w0, 16)
            sp.dma_start(b1_s[:, E0:EX], sb1T).then_inc(s_w0, 16)
            sp.dma_start(b2_s[0:E0, :], b2).then_inc(s_w0, 16)
            sp.dma_start(b2_s[E0:E0 + 1, :], sb2).then_inc(s_w0, 16)
            sp.dma_start(gate_s[:], gate_wT.rearrange("(k p) e -> p k e", p=P)).then_inc(s_w0, 16)
            sp.dma_start(w_gnn1_s[:], w_gnn1T.rearrange("(k p) o -> p k o", p=P)).then_inc(s_w0, 16)

            sp.wait_ge(s_p2, 1)
            for w_s, w in ((wq_s, wq), (wk_s, wk), (wv_s, wv), (wo_s, wo)):
                sp.dma_start(w_s[:], w.rearrange("(k p) o -> p k o", p=P)).then_inc(s_aw, 16)
            for b_s, b in ((bq_s, bqT), (bk_s, bkT)):
                sp.dma_start(b_s[:], b).then_inc(s_aw, 16)
            for b_s, b in ((bv_s, bv), (bo_s, bo), (g1_s, g1), (beta1_s, beta1)):
                sp.dma_start(b_s[:], b.to_broadcast([P, D])).then_inc(s_aw, 16)
            sp.wait_ge(s_c4, 1)
            sp.dma_start(xs_d.rearrange("(s p) d -> p s d", p=P), zero[:].unsqueeze(1).to_broadcast([P, SLOTS, D])).then_inc(s_zd, 16)

            def pair_operands(p):
                for h in range(2):
                    own = slice((2 * p + h) % 4 * DH, ((2 * p + h) % 4 + 1) * DH)
                    for a, (src, dst) in enumerate((((hi[0], hi[0], lo[0]), aug[0]), ((hi[1], lo[1], hi[1]), aug[1]))):
                        for r in range(3):
                            sp.dma_start(dst[r * DH:(r + 1) * DH, p % 2, h, :].bitcast(F32), src[r][own, p // 2, :].bitcast(F32)).then_inc(s_aug[p % 2], 16)

            def maxima_row(n):
                p, h = n // 2, n % 2
                sp.wait_ge(s_mc, n + 1)
                row = aug[0][KA:KA + 1, p % 2, h, :].bitcast(F32)
                sp.dma_start(row[:, 0:(T - 1) * P].rearrange("a (t c) -> a t c", c=P), mT[0:T - 1, h, :].bitcast(F32)).then_inc(s_mr[p % 2], 16)
                sp.dma_start(row[:, (T - 1) * P:RW], mT[T - 1:T, h, 0:RW - (T - 1) * P].bitcast(F32)).then_inc(s_mr[p % 2], 16)

            sp.wait_ge(s_hi, 4)
            sp.wait_ge(s_lo, 4)
            for p in range(PAIRS):
                if p >= 2:
                    sp.wait_ge(s_pv, NC * T * (p - 1))
                pair_operands(p)
                maxima_row(2 * p)
                maxima_row(2 * p + 1)

            sp.wait_ge(s_o, G)
            sp.dma_start(wg_s[:], wg.rearrange("(k p) e -> p k e", p=P)).then_inc(s_ew, 16)
            sp.dma_start(bg_s[:], bg.to_broadcast([P, E1])).then_inc(s_ew, 16)
            sp.dma_start(g2_s[:], g2.to_broadcast([P, D])).then_inc(s_ew, 16)
            sp.dma_start(beta2_s[:], beta2.to_broadcast([P, D])).then_inc(s_ew, 16)
            sp.wait_ge(s_sl, 1)

            def expert(n):
                if n >= NW:
                    sp.wait_ge(s_y, n - NW + 1)
                e = sp.value_load(sloti[0:1, n:n + 1], min_val=0, max_val=E1 - 1)
                sp.dma_start(wexp[:, n % NW, :], blob[bass.ds(e, 1), :, :].rearrange("a p n -> (a p) n")).then_inc(s_w[n % NW], 16)

            for n in range(NW):
                expert(n)
            sp.wait_ge(s_sc, 16 * T)
            def tokens(n):
                if n >= 2:
                    sp.wait_ge(s_gt, n - 1)
                sp.dma_start(xg[:, n % 2, :], xs_d[n * P:(n + 1) * P, :]).then_inc(s_xg[n % 2], 16)

            tokens(0)
            tokens(1)
            for n in range(SLOTS):
                if n + 2 < SLOTS:
                    tokens(n + 2)
                sp.wait_ge(s_y, n + 1)
                sp.dma_start(ys_d[n * P:(n + 1) * P, :], yg[:, n % 2, :]).then_inc(s_ys[n % 2], 16)
                if n + NW < SLOTS:
                    expert(n + NW)
            sp.wait_ge(s_x4, T)
            sp.dma_start(out[0:(T - 1) * P, :].rearrange("(t p) d -> p t d", p=P), xt[:, 0:T - 1, :]).then_inc(s_out, 16)
            sp.dma_start(out[(T - 1) * P:R, :], xt[0:LAST, T - 1, :]).then_inc(s_out, 16)
            sp.wait_ge(s_out, 32)

        @block.gpsimd
        def _(pool):
            pool.memset(xt[:, T - 1, :], 0.0).then_inc(s_pad, 1)
            pool.memset(xT[:, :, R:RW], 0.0).then_inc(s_pad, 1)
            pool.memset(hT[:, :, R:RW], 0.0).then_inc(s_pad, 1)
            pool.memset(adj[:, :, R:RW], 0.0).then_inc(s_pad, 1)
            pool.memset(ht[:, T - 1, :], 0.0).then_inc(s_pad, 1)
            pool.memset(ss[:, :], 0.0).then_inc(s_pad, 1)
            pool.memset(ones2[:], 1.0).then_inc(s_pad, 1)
            pool.memset(eps_s[:], LN_EPS).then_inc(s_pad, 1)
            pool.memset(lg[:, T - 1, :], 0.0).then_inc(s_init, 1)
            pool.memset(comb[:, :, E0:EX], 1.0).then_inc(s_init, 1)
            pool.memset(combT[:], 1.0).then_inc(s_init, 1)
            pool.memset(dg[:], 1.0).then_inc(s_init, 1)
            pool.iota(iota8[:], [[1, E0]], base=0, channel_multiplier=0, allow_small_or_imprecise_dtypes=True).then_inc(s_init, 1)
            pool.memset(zero[:], 0.0).then_inc(s_c4, 1)
            pool.memset(ident[:], 0.0).then_inc(s_id, 1)
            pool.wait_ge(s_id, 1)
            pool.affine_select(out=ident[:], in_=ident[:], compare_op=ALU.not_equal, fill=1.0, base=0,
                               pattern=[[-1, P]], channel_multiplier=1).then_inc(s_id, 1)
            pool.wait_ge(s_wgnn, 32)
            for t in range(T):
                ln0.wait_tile(pool, t)
                pool.tensor_tensor(xt[0:rows(t), t, :], xt[0:rows(t), t, :], b_gnn_s[0:rows(t), :], ALU.add).then_inc(s_xb, 1)
            for j in range(T - 1):
                pool.wait_ge(s_e, NC * (j + 1))
                if j == 0:
                    pool.tensor_copy(esum[:], ee[:, 0, :]).then_inc(s_es, 1)
                else:
                    pool.wait_ge(s_es, j)
                    pool.tensor_tensor(esum[:], esum[:], ee[:, j % NE, :], ALU.add).then_inc(s_es, 1)
            pool.wait_ge(s_e, NC * T)
            for t in range(T):
                a = adj[0:rows(t), t, cols(t)]
                pool.tensor_tensor(a, a, ident[0:rows(t), 0:rows(t)], ALU.add).then_inc(s_self, 1)

            pool.wait_ge(s_p2, 1)
            pool.wait_ge(s_rl, T)
            pool.memset(va[:, :, :, DH:2 * DH], 1.0).then_inc(s_c3, 1)
            pool.wait_ge(s_c3, 1)
            pool.memset(aug[1][KA:KA + 1, :, :, :].bitcast(F32), 1.0).then_inc(s_c3, 1)
            pool.wait_ge(s_c3, 2)
            pool.memset(mxp[:, :, T - 1, :], 0.0).then_inc(s_c3, 1)
            pool.wait_ge(s_aw, 16 * 10)
            for t in range(T):
                ln3.wait_tile(pool, t)
                pool.tensor_tensor(ht[:, t, :], xn[:, t, :], bo_s[:], ALU.add).then_inc(s_xo, 1)
            for t in range(T):
                pool.wait_ge(s_gain, t + 1)
                pool.tensor_tensor(xn[:, t, :], xn[:, t, :], beta1_s[:], ALU.add).then_inc(s_t, 1)

            pool.memset(valid[:], 1.0).then_inc(s_c4, 1)
            pool.memset(before[:], 1.0).then_inc(s_c4, 1)
            pool.memset(onesb[:], 1.0).then_inc(s_c4, 1)
            pool.memset(lower[:], 1.0).then_inc(s_c4, 1)
            pool.iota(starts[:], [[P, SLOTS]], base=0, channel_multiplier=0, allow_small_or_imprecise_dtypes=True).then_inc(s_c4, 1)
            pool.wait_ge(s_c4, 5)
            pool.affine_select(out=valid[:], in_=valid[:], compare_op=ALU.is_ge, fill=0.0, base=R - 1, pattern=[[-P, T]],
                               channel_multiplier=-1).then_inc(s_c4, 1)
            pool.affine_select(out=before[:], in_=before[:], compare_op=ALU.is_ge, fill=0.0, base=-1, pattern=[[1, P]],
                               channel_multiplier=-1).then_inc(s_c4, 1)
            pool.affine_select(out=lower[:], in_=lower[:], compare_op=ALU.is_ge, fill=0.0, base=-1, pattern=[[1, E1], [-1, E1]],
                               channel_multiplier=0).then_inc(s_c4, 1)
            pool.wait_ge(s_zd, 16)
            pool.wait_ge(s_pos, 1)
            pool.wait_ge(s_t, T)
            for t in range(T):
                pool.indirect_dma_start(xs_d, bass.IndirectOffsetOnAxis(ap=posi[0:rows(t), t:t + 1], axis=0),
                                        xn[0:rows(t), t, :], None).then_inc(s_sc, 16)
            for q in range(2):
                pool.wait_ge(s_ys[q], 16 * (SLOTS // 2))
            for t in range(T):
                pool.indirect_dma_start(moe[0:rows(t), t, :], None, ys_d,
                                        bass.IndirectOffsetOnAxis(ap=posi[0:rows(t), t:t + 1], axis=0)).then_inc(s_ga2, 16)
            for t in range(T):
                pool.wait_ge(s_gain2, 2 * t + 2)
                pool.tensor_tensor(xt[0:rows(t), t, :], xt[0:rows(t), t, :], ht[0:rows(t), t, :], ALU.add).then_inc(s_x4, 1)

        HB = (4, 5, 6, 7)
        SIMB = (6, 7)

        @block.tensor
        def _(pe):
            pe.wait_ge(s_id, 2)
            turn_pe(pe, tx, xn, ln_done, (0, 1, 2, 3), ln0.tiles)
            pe.wait_ge(s_wgnn, 32)
            project(pe, xT, tx.wait_group, w_gnn_s, s_h, HB, s_ss)
            turn_pe(pe, th, hn, s_hn, (0, 1, 2, 3))

            def sim(j):
                for c in range(NC):
                    n = NC * j + c
                    if n >= 2:
                        pe.wait_ge(s_exp, n - 1)
                    else:
                        pe.wait_ge(s_ss, T)
                    for k in range(H2):
                        m = pe.matmul(ps[0:rows(j), SIMB[n % 2], 0:CW], hT[:, k, cols(j)], hT[:, k, chunk(c)],
                                      start=(k == 0), stop=(k == H2 - 1))
                    m.then_inc(s_sim, 1)

            th.wait_group(pe, G - 1)
            pe.wait_ge(s_pad, 8)
            sim(0)
            for j in range(T):
                if j + 1 < T:
                    sim(j + 1)
                pe.wait_ge(s_e, NC * (j + 1))
                for i in range(T):
                    m = pe.matmul(half(i // 2, i)[0:rows(i), :], ee[0:rows(j), j % NE, cols(i)], ht[0:rows(j), j, :],
                                  start=(j == 0 and i % 2 == 0), stop=(j == T - 1), skip_group_check=True)
                m.then_inc(s_agg, 1)
            pe.wait_ge(s_es, T - 1)
            pe.wait_ge(s_exp, NC * T)
            for i in range(T):
                o = ps[0:rows(i), SIMB[0], 2 * i:2 * i + 2]
                pe.matmul(o, esum[:, cols(i)], ones2[:], start=(i == 0), stop=False, skip_group_check=True)
                m = pe.matmul(o, ee[0:LAST, (T - 1) % NE, cols(i)], ones2[0:LAST, :], start=False, stop=True, skip_group_check=True)
            m.then_inc(s_den, 1)

            turn_pe(pe, tx1, xn, ln_done, (0, 1, 2, 3), ln1.tiles)
            tx1.wait_group(pe, G - 1)
            pe.wait_ge(s_w0, 16 * (EX + 8))
            for t in range(T):
                for k in range(H2):
                    m = pe.matmul(ps[0:rows(t), 4, E0 * t:E0 * (t + 1)], xT[:, k, cols(t)], gate_s[:, k, :],
                                  start=(k == 0), stop=(k == H2 - 1))
            m.then_inc(s_lg, 1)

            def up(e):
                for c in range(NC):
                    if e:
                        pe.wait_ge(s_hid, NC * (e - 1) + c + 1)
                    for k in range(H2):
                        m = pe.matmul(ps[:, c, 0:CW], w1_s[:, e, k, :], xT[:, k, chunk(c)], start=(k == 0), stop=(k == H2 - 1))
                    m.then_inc(s_up, 1)

            def down(e):
                pe.wait_ge(s_hid, NC * (e + 1))
                for g in range(G):
                    n = G * e + g
                    if n >= 4:
                        pe.wait_ge(s_x2, T * ((n - 4) // G) + min(2 * ((n - 4) % G) + 2, T))
                    else:
                        pe.wait_ge(s_r, 1)
                    for t in group(g):
                        m = pe.matmul(half(4 + n % 4, t)[0:rows(t), :], ee[:, e % 2, cols(t)], w2_s[:, e, :],
                                      start=True, stop=(e < EX - 1))
                        if e == EX - 1:
                            m = pe.matmul(half(4 + n % 4, t)[0:rows(t), :], combT[:, cols(t)], b2_s[:], start=False, stop=True)
                    m.then_inc(s_dn, 1)

            up(0)
            for e in range(EX - 1):
                up(e + 1)
                down(e)
            pe.wait_ge(s_comb, 1)
            pe.wait_ge(s_hid, NC * EX)
            for t in range(T):
                m = pe.transpose(ps[0:E0, t // 4, t % 4 * P:t % 4 * P + rows(t)], comb[0:rows(t), t, 0:E0], ident[0:rows(t), 0:rows(t)])
            m.then_inc(s_ct, 1)
            pe.wait_ge(s_cc, NC)
            down(EX - 1)

            pe.wait_ge(s_self, T)
            for j in range(T):
                ln2.wait_tile(pe, j)
                for k in range(H2):
                    for c in range(NC):
                        m = pe.matmul(ps[:, NC * k + c, 0:CW], xn[0:rows(j), j, k * P:(k + 1) * P], adj[0:rows(j), j, chunk(c)],
                                      start=(j == 0), stop=(j == T - 1))
            m.then_inc(s_g, 1)

            def both_copied(eng, g):
                eng.wait_ge(s_ga, 1)
                eng.wait_ge(s_gv, 1)
            project(pe, hT, both_copied, w_gnn1_s, s_t1, (6, 7), s_ts)
            for j in range(T):
                pe.wait_ge(s_ts, j + 1)
                for i in range(T):
                    m = pe.matmul(half(i // 2, i)[0:rows(i), :], adj[0:rows(j), j, cols(i)], ht[0:rows(j), j, :],
                                  start=(j == 0 and i % 2 == 0), stop=(j == T - 1), skip_group_check=True)
            m.then_inc(s_p2, 1)

            turn_pe(pe, tx3, xn, ln_done, (6, 7), ln3.tiles)
            pe.wait_ge(s_aw, 16 * 10)
            tx3.wait_group(pe, G - 1)
            pe.wait_ge(s_dup, 1)
            pe.wait_ge(s_rl, T)
            for u, (w_s, k2) in enumerate(((wq_s, 0), (wq_s, 1), (wk_s, 0), (wk_s, 1))):
                if u >= 2:
                    pe.wait_ge(s_pb, u - 1)
                for c in range(NC):
                    for k in range(H2):
                        m = pe.matmul(ps[:, 3 * (u % 2) + c, 0:CW], w_s[:, k, k2 * P:(k2 + 1) * P], xT[:, k, chunk(c)],
                                      start=(k == 0), stop=(k == H2 - 1))
                m.then_inc(s_pr, 1)
            project(pe, xT, tx3.wait_group, wv_s, s_v, (6, 7), s_vb)

            def rows2(i):
                return slice(i * P, min((i + 1) * P, RW))

            def max_scores(u):
                n, i = u // T, u % T
                p, h = n // 2, n % 2
                if i == 0:
                    pe.wait_ge(s_aug[p % 2], 16 * 12 * (p // 2 + 1))
                    if n:
                        pe.wait_ge(s_mc, n)
                    else:
                        pe.wait_ge(s_vb, T)
                        pe.wait_ge(s_pb, 4)
                w = rows2(i)
                for c in range(NC):
                    if u and c == 0:
                        pe.wait_ge(s_mx, 2 * (u - 1) + 1)
                    if u and c == 2:
                        pe.wait_ge(s_mx, 2 * u)
                    m = pe.matmul(ps[0:w.stop - w.start, 5 + c, 0:CW], aug[0][0:KA, p % 2, h, w], aug[1][0:KA, p % 2, h, chunk(c)],
                                  start=True, stop=True)
                    if c:
                        m.then_inc(s_s1, 1)
                if i == T - 1:
                    pe.wait_ge(s_neg, n + 1)
                    pe.transpose(ps[0:T, 5, 0:P], nm[:, h, :], ident[:]).then_inc(s_mt, 1)

            def scores(n):
                p, c, k = n // (NC * T), n // T % NC, n % T
                if n % (NC * T) == 0:
                    pe.wait_ge(s_mr[p % 2], 64 * (p // 2 + 1))
                    pe.wait_ge(s_c3, 3)
                    if n == 0:
                        pe.wait_ge(s_pb, 4)
                if n >= 2:
                    pe.wait_ge(s_p, n - 1)
                for h in range(2):
                    m = pe.matmul(ps[0:rows(k), 1 + 2 * (n % 2) + h, 0:CW], aug[1][:, p % 2, h, cols(k)], aug[0][:, p % 2, h, chunk(c)],
                                  start=True, stop=True)
                m.then_inc(s_s2, 1)

            def values(n):
                p, k = n // (NC * T), n % T
                pe.wait_ge(s_p, n + 1)
                if k == 0 and n:
                    pe.wait_ge(s_ac, n // T)
                for h in range(2):
                    m = pe.matmul(ps[2 * DH * h:2 * DH * (h + 1), 0, 0:CW], va[0:rows(k), k, 2 * p + h, :], pt[0:rows(k), n % NPT, h, :],
                                  start=(k == 0), stop=(k == T - 1))
                m.then_inc(s_pv, 1)

            for u in range(2 * T):
                max_scores(u)
            u, N = 2 * T, PAIRS * NC * T
            scores(0)
            for n in range(N):
                p = n // (NC * T)
                while u < HEADS * T and u < 2 * T * (p + 1) + (n % (NC * T) + 2) * 2 // 3:
                    max_scores(u)
                    u += 1
                if n + 1 < N:
                    scores(n + 1)
                values(n)

            def heads_ready(eng, g):
                eng.wait_ge(s_cx, 2 * NC * PAIRS)
            project(pe, cT, heads_ready, wo_s, s_o, (1, 2, 3, 4, 5, 6), s_u)

            turn_pe(pe, tx4, xn, s_t, (0, 1))
            tx4.wait_group(pe, G - 1)
            pe.wait_ge(s_ew, 64)
            pe.wait_ge(s_u, T)
            for t in range(T):
                for k in range(H2):
                    m = pe.matmul(ps[0:rows(t), 4, E1 * t:E1 * (t + 1)], xT[:, k, cols(t)], wg_s[:, k, :],
                                  start=(k == 0), stop=(k == H2 - 1))
            m.then_inc(s_l1, 1)
            pe.wait_ge(s_oh, 1)
            pe.wait_ge(s_c4, 9)
            for t in range(T + 1):
                o = ps[:, 5, E1 * t:E1 * (t + 1)]
                for j in range(t):
                    m = pe.matmul(o, onesb[:], ohb[:, j, :], start=(j == 0), stop=(t == T and j == T - 1))
                if t < T:
                    m = pe.matmul(o, before[:], ohb[:, t, :], start=(t == 0), stop=True)
            m.then_inc(s_rank, 1)

            def slot_turn(n):
                pe.wait_ge(s_xg[n % 2], 16 * (n // 2 + 1))
                if n >= 2:
                    pe.wait_ge(s_gc, n - 1)
                for k in range(H2):
                    m = pe.transpose(ps[:, n % 2, k * P:(k + 1) * P], xg[:, n % 2, k * P:(k + 1) * P], ident[:])
                m.then_inc(s_gt, 1)

            def slot_up(n):
                pe.wait_ge(s_w[n % NW], 16 * (n // NW + 1))
                pe.wait_ge(s_gc, n + 1)
                w = wexp[:, n % NW, 0:H2 * HID].rearrange("p (k f) -> p k f", k=H2)
                for b in range(2):
                    if n >= 2:
                        pe.wait_ge(s_fg, FC * (n - 2) + FC // 2 * (b + 1))
                    for f in range(FC // 2):
                        for k in range(H2):
                            fc = b * FC // 2 + f
                            m = pe.matmul(ps[:, 2 + 2 * (n % 2) + b, f * P:(f + 1) * P], w[:, k, fc * P:(fc + 1) * P],
                                          xgT[:, n % 2, k, :], start=(k == 0), stop=(k == H2 - 1))
                    m.then_inc(s_f1, 1)

            def slot_down(n):
                if n >= 2:
                    pe.wait_ge(s_y, n - 1)
                w = wexp[:, n % NW, H2 * HID:2 * H2 * HID].rearrange("p (c d) -> p c d", c=FC)
                for f in range(FC):
                    pe.wait_ge(s_fg, FC * n + f + 1)
                    m = pe.matmul(ps[:, 6 + n % 2, 0:D], hid[:, n % 2, f, :], w[:, f, :], start=(f == 0), stop=(f == FC - 1))
                m.then_inc(s_f2, 1)

            slot_turn(0)
            slot_turn(1)
            slot_up(0)
            for n in range(SLOTS):
                if n + 2 < SLOTS:
                    slot_turn(n + 2)
                if n + 1 < SLOTS:
                    slot_up(n + 1)
                slot_down(n)

        @block.scalar
        def _(act):
            act.wait_ge(s_pad, 8)
            ln_std(act, ln0)
            turn_copy(act, tx, xT, (0, 1, 2, 3), 0)
            for g in range(G):
                act.wait_ge(s_h, g + 1)
                bank = ps[:, HB[g % 4], :]
                act.activation(ht[0:rows(2 * g), 2 * g:2 * g + len(group(g)), :], gshape(bank, g), ACT.Copy).then_inc(s_hc, 1)
                for t in group(g):
                    if t:
                        act.wait_ge(s_ss, t)
                    act.activation(sq[0:rows(t), :], half(HB[g % 4], t)[0:rows(t), :], ACT.Square,
                                   accum_out=ss[0:rows(t), t:t + 1]).then_inc(s_ss, 1)
            act.wait_ge(s_ss, T)
            act.activation(norm[:], ss[:], ACT.Sqrt).then_inc(s_nm, 1)
            turn_copy(act, th, hT, (0, 1, 2, 3), 0)
            for j in range(T):
                for c in range(NC):
                    n = NC * j + c
                    act.wait_ge(s_sim, n + 1)
                    if j >= NE:
                        act.wait_ge(s_e, NC * (j - NE) + c + 1)
                    act.activation(ex[0:rows(j), j % NE, chunk(c)], ps[0:rows(j), SIMB[n % 2], 0:CW], ACT.Exp)\
                        .then_inc(s_exp, 1)

            ln_std(act, ln1)
            turn_copy(act, tx1, xT, (0, 1, 2, 3), 0)
            act.wait_ge(s_r, 3)
            act.activation(lg[:], lg[:], ACT.Exp).then_inc(s_er, 1)
            for e in range(EX):
                for c in range(NC):
                    act.wait_ge(s_up, NC * e + c + 1)
                    if e >= 2:
                        act.wait_ge(s_dn, G * (e - 1))
                    act.activation(ee[:, e % 2, chunk(c)], ps[:, c, 0:CW], ACT.Relu, bias=b1_s[:, e:e + 1]).then_inc(s_hid, 1)
            act.wait_ge(s_init, 5)
            act.wait_ge(s_ct, 1)
            for c in range(NC):
                n = min(512, R - 512 * c)
                act.activation(combT[0:E0, 512 * c:512 * c + n], ps[0:E0, c, 0:n], ACT.Copy).then_inc(s_cc, 1)

            act.wait_ge(s_dg, T)
            act.activation(dgs[:], dg[:], ACT.Sqrt).then_inc(s_dgs, 1)
            ln_std(act, ln2)
            act.wait_ge(s_g, 1)
            act.activation(hT[:, 0, :].rearrange("p (c w) -> p c w", c=NC), ps[:, 0:NC, 0:CW], ACT.Copy).then_inc(s_ga, 1)
            act.wait_ge(s_ds, 1)
            for t in range(T):
                act.wait_ge(s_t1, t // 2 + 1)
                act.activation(ht[0:rows(t), t, :], half(6 + t // 2 % 2, t)[0:rows(t), :], ACT.Copy,
                               scale=dscale[0:rows(t), t:t + 1]).then_inc(s_ts, 1)
            act.wait_ge(s_p2, 1)
            for t in range(T):
                act.activation(hn[0:rows(t), t, :], half(t // 2, t)[0:rows(t), :], ACT.Relu,
                               scale=dscale[0:rows(t), t:t + 1]).then_inc(s_rl, 1)

            ln_std(act, ln3)
            turn_copy(act, tx3, xT, (6, 7), 0)
            for u in range(4):
                act.wait_ge(s_pr, u + 1)
                if u >= 2:
                    act.wait_ge(s_lo, u - 1)
                act.activation(pr32[:, u % 2, :].rearrange("p (c w) -> p c w", c=NC), ps[:, 3 * (u % 2):3 * (u % 2) + 3, 0:CW],
                               ACT.Identity, bias=(bq_s, bk_s)[u // 2][:, u % 2:u % 2 + 1]).then_inc(s_pb, 1)
            N = PAIRS * NC * T
            for n in range(N + 1):
                if n < N:
                    act.wait_ge(s_s2, n + 1)
                    if n >= NPT:
                        act.wait_ge(s_pv, n - NPT + 1)
                    k = n % T
                    b = 1 + 2 * (n % 2)
                    act.activation(pt[0:rows(k), n % NPT, :, :], ps[0:rows(k), b:b + 2, 0:CW], ACT.Exp, scale=DH ** -0.5).then_inc(s_p, 1)
                if n and n % T == 0:
                    m = n // T - 1
                    act.wait_ge(s_pv, n)
                    if m >= 2:
                        act.wait_ge(s_cx, 2 * (m - 1))
                    act.activation(acc[:, m % 2, :], ps[:, 0, 0:CW], ACT.Copy).then_inc(s_ac, 1)
            ln_std(act, ln4)

            turn_copy(act, tx4, xT, (0, 1), 0)
            for n in range(SLOTS):
                bias = wexp[:, n % NW, 2 * H2 * HID:2 * H2 * HID + FC]
                for f in range(FC):
                    if f % (FC // 2) == 0:
                        act.wait_ge(s_f1, 2 * n + f // (FC // 2) + 1)
                        if n >= 2:
                            act.wait_ge(s_f2, n - 1)
                    act.activation(hid[:, n % 2, f, :], ps[:, 2 + 2 * (n % 2) + f // (FC // 2), f % (FC // 2) * P:(f % (FC // 2) + 1) * P],
                                   ACT.Gelu, bias=bias[:, f:f + 1]).then_inc(s_fg, 1)
            ln_std(act, ln5)

        @block.vector
        def _(v):
            v.wait_ge(s_x, 32)
            ln_steps(v, ln0, xt, xn)
            turn_copy(v, tx, xT, (0, 1, 2, 3), 1)
            v.wait_ge(s_nm, 1)
            v.tensor_scalar(norm[:], norm[:], NORM_EPS, None, ALU.max).then_inc(s_rn, 1)
            v.wait_ge(s_rn, 1)
            v.reciprocal(rnorm[:], norm[:]).then_inc(s_rn, 1)
            v.wait_ge(s_rn, 2)
            for t in range(T):
                v.tensor_scalar(hn[:, t, :], ht[:, t, :], rnorm[:, t:t + 1], None, ALU.mult).then_inc(s_hn, 1)
            turn_copy(v, th, hT, (0, 1, 2, 3), 1)
            for j in range(T):
                if j < 3:
                    v.wait_ge(s_adj[j >= 2], 16 * (T - 2) if j >= 2 else 32)
                if j >= NE:
                    v.wait_ge(s_agg, j - NE + 1)
                    v.wait_ge(s_es, j - NE + 1)
                for c in range(NC):
                    v.wait_ge(s_exp, NC * j + c + 1)
                    v.scalar_tensor_tensor(out=ee[0:rows(j), j % NE, chunk(c)], in0=adj[0:rows(j), j, chunk(c)], scalar=NORM_EPS,
                                           in1=ex[0:rows(j), j % NE, chunk(c)], op0=ALU.add, op1=ALU.mult).then_inc(s_e, 1)
            v.wait_ge(s_den, 1)
            d = ps[:, SIMB[0], 0:2 * T].rearrange("p (t a) -> p t a", a=2)
            v.reciprocal(rden[:, 0:T - 1], d[:, 0:T - 1, 0]).then_inc(s_rd, 1)
            v.reciprocal(rden[0:LAST, T - 1:T], d[0:LAST, T - 1, 0:1]).then_inc(s_rd, 1)
            v.wait_ge(s_rd, 2)
            v.wait_ge(s_xb, T)
            v.wait_ge(s_agg, T)
            for t in range(T):
                v.scalar_tensor_tensor(out=xt[0:rows(t), t, :], in0=half(t // 2, t)[0:rows(t), :], scalar=rden[0:rows(t), t:t + 1],
                                       in1=xt[0:rows(t), t, :], op0=ALU.mult, op1=ALU.add).then_inc(s_x1, 1)

            ln_steps(v, ln1, xt, xn, before=lambda t: v.wait_ge(s_x1, t + 1))
            turn_copy(v, tx1, xT, (0, 1, 2, 3), 1)
            route(v)
            for e in range(EX):
                for g in range(G):
                    v.wait_ge(s_dn, G * e + g + 1)
                    for t in group(g):
                        if e:
                            v.wait_ge(s_x2, T * (e - 1) + t + 1)
                        v.scalar_tensor_tensor(out=xt[0:rows(t), t, :], in0=half(4 + (G * e + g) % 4, t)[0:rows(t), :],
                                               scalar=comb[0:rows(t), t, e:e + 1], in1=xt[0:rows(t), t, :],
                                               op0=ALU.mult, op1=ALU.add).then_inc(s_x2, 1)

            v.wait_ge(s_self, T)
            for t in range(T):
                v.tensor_tensor_reduce(hn[0:rows(t), t, 0:rows(t)], adj[0:rows(t), t, cols(t)], ident[0:rows(t), 0:rows(t)],
                                       1.0, 0.0, ALU.mult, ALU.add, dg[0:rows(t), t:t + 1]).then_inc(s_dg, 1)
            ln_steps(v, ln2, xt, xn, before=lambda t: v.wait_ge(s_x2, T * (EX - 1) + t + 1))
            v.wait_ge(s_dgs, 1)
            v.reciprocal(dscale[:], dgs[:]).then_inc(s_ds, 1)
            v.wait_ge(s_g, 1)
            v.tensor_copy(hT[:, 1, :].rearrange("p (c w) -> p c w", c=NC), ps[:, NC:2 * NC, 0:CW]).then_inc(s_gv, 1)
            for t in range(T):
                v.wait_ge(s_rl, t + 1)
                v.tensor_tensor(xt[0:rows(t), t, :], xt[0:rows(t), t, :], hn[0:rows(t), t, :], ALU.add).then_inc(s_x3, 1)


            ln_steps(v, ln3, xt, xn, before=lambda t: v.wait_ge(s_x3, t + 1))
            turn_copy(v, tx3, xT, (6, 7), 1)
            v.wait_ge(turn_odd, tx3.half + G // 2)
            v.tensor_copy(xT[:, :, R:RW], xT[:, :, R - 1:R].to_broadcast([P, H2, RW - R])).then_inc(s_dup, 1)
            for u in range(4):
                v.wait_ge(s_pb, u + 1)
                v.tensor_copy(hi[u // 2][:, u % 2, :], pr32[:, u % 2, :]).then_inc(s_hi, 1)
                v.wait_ge(s_hi, u + 1)
                v.tensor_tensor(lo[u // 2][:, u % 2, :], pr32[:, u % 2, :], hi[u // 2][:, u % 2, :].bitcast(F32), ALU.subtract)\
                    .then_inc(s_lo, 1)
            for t in range(T):
                v.wait_ge(s_v, t // 2 + 1)
                v.tensor_tensor(va[0:rows(t), t, :, 0:DH], half(6 + t // 2 % 2, t)[0:rows(t), :].rearrange("p (h d) -> p h d", d=DH),
                                bv_s[0:rows(t), :].rearrange("p (h d) -> p h d", d=DH), ALU.add).then_inc(s_vb, 1)

            def maxima(u):
                n, i = u // T, u % T
                w = min((i + 1) * P, RW) - i * P
                if u == 0:
                    v.wait_ge(s_c3, 3)
                if i == 0 and n >= 2:
                    v.wait_ge(s_neg, n - 1)
                v.wait_ge(s_s1, 2 * u + 1)
                v.tensor_reduce(mxp[0:w, n % 2, i, 0:1], ps[0:w, 5:7, 0:CW], AX.XY, ALU.max).then_inc(s_mx, 1)
                v.wait_ge(s_s1, 2 * u + 2)
                v.tensor_reduce(mxp[0:w, n % 2, i, 1:2], ps[0:w, 7, 0:CW], AX.X, ALU.max).then_inc(s_mx, 1)
                if i == T - 1:
                    v.wait_ge(s_mx, 2 * u + 2)
                    if n >= 2:
                        v.wait_ge(s_mt, n - 1)
                    v.tensor_reduce(nm[:, n % 2, :], mxp[:, n % 2, :, :], AX.X, ALU.max, negate=True).then_inc(s_neg, 1)
                    v.wait_ge(s_mt, n + 1)
                    if n >= 2:
                        v.wait_ge(s_mr[n // 2 % 2 ^ 1], 64 * ((n // 2 - 1) // 2 + 1))
                    v.tensor_copy(mT[:, n % 2, :], ps[0:T, 5, 0:P]).then_inc(s_mc, 1)

            def normalise(m):
                p, c = m // NC, m % NC
                v.wait_ge(s_ac, m + 1)
                if m:
                    v.wait_ge(s_cx, 2 * m)
                for h in range(2):
                    a = slice(2 * DH * h, 2 * DH * h + DH)
                    ones = slice(2 * DH * h + DH, 2 * DH * (h + 1))
                    v.reciprocal(rec[a, :], acc[ones, m % 2, :]).then_inc(s_rc, 1)
                for h in range(2):
                    a = slice(2 * DH * h, 2 * DH * h + DH)
                    o = ((2 * p + h) % 4) * DH
                    v.wait_ge(s_rc, 2 * m + h + 1)
                    v.tensor_tensor(cT[o:o + DH, p // 2, chunk(c)], acc[a, m % 2, :], rec[a, :], ALU.mult).then_inc(s_cx, 1)

            for u in range(2 * T):
                maxima(u)
            u, N = 2 * T, PAIRS * NC * T
            for n in range(N):
                p = n // (NC * T)
                while u < HEADS * T and u < 2 * T * (p + 1) + (n % (NC * T) + 2) * 2 // 3:
                    maxima(u)
                    u += 1
                if n % T == 2 and n > T:
                    normalise(n // T - 1)
            normalise(N // T - 1)

            def add_attention(t):
                if t % 2 == 0:
                    v.wait_ge(s_o, t // 2 + 1)
                    v.wait_ge(s_xo, T)
                v.tensor_tensor(ht[0:rows(t), t, :], half(1 + t // 2, t)[0:rows(t), :], ht[0:rows(t), t, :], ALU.add).then_inc(s_u, 1)
                v.wait_ge(s_u, t + 1)
            ln_steps(v, ln4, ht, xn, before=add_attention)
            for t in range(T):
                ln4.wait_tile(v, t)
                v.tensor_tensor(xn[:, t, :], xn[:, t, :], g1_s[:], ALU.mult).then_inc(s_gain, 1)

            turn_copy(v, tx4, xT, (0, 1), 1)
            v.wait_ge(s_l1, 1)
            v.wait_ge(s_ew, 64)
            d = ps[:, 4, 0:E1 * T].rearrange("p (t e) -> p t e", e=E1)
            v.tensor_tensor(lg[:, 0:T - 1, :], d[:, 0:T - 1, :], bg_s[:].unsqueeze(1).to_broadcast([P, T - 1, E1]), ALU.add).then_inc(s_k, 1)
            v.tensor_tensor(lg[0:LAST, T - 1, :], d[0:LAST, T - 1, :], bg_s[0:LAST, :], ALU.add).then_inc(s_k, 1)
            v.wait_ge(s_k, 2)
            for t in range(T):
                v.max(top[:, t, :], lg[:, t, :]).then_inc(s_k2, 1)
            for t in range(T):
                v.wait_ge(s_k2, t + 1)
                v.max_index(topi[:, t, :], top[:, t, :], lg[:, t, :]).then_inc(s_k2, 1)
            v.wait_ge(s_k2, 2 * T)
            v.tensor_copy(best[:], topi[:, :, 0]).then_inc(s_k, 1)
            v.wait_ge(s_k, 3)
            v.wait_ge(s_c4, 9)
            v.tensor_tensor(oh[:], iota8[:].unsqueeze(1).to_broadcast([P, T, E1]), best[:].unsqueeze(2).to_broadcast([P, T, E1]),
                            ALU.is_equal).then_inc(s_k, 1)
            v.wait_ge(s_k, 4)
            v.tensor_tensor(oh[:], oh[:], valid[:].unsqueeze(2).to_broadcast([P, T, E1]), ALU.mult).then_inc(s_k, 1)
            v.wait_ge(s_k, 5)
            v.tensor_copy(ohb[:], oh[:]).then_inc(s_oh, 1)
            v.wait_ge(s_rank, 1)
            v.tensor_copy(rank[:], ps[:, 5, 0:E1 * (T + 1)].rearrange("p (t e) -> p t e", e=E1)).then_inc(s_k, 1)
            v.wait_ge(s_k, 6)
            v.tensor_scalar(cnt[:], rank[:, T, :], float(P - 1), None, ALU.add).then_inc(s_k, 1)
            v.wait_ge(s_k, 7)
            v.tensor_scalar(cnt[:], cnt[:], 7, 7, ALU.arith_shift_right, ALU.logical_shift_left).then_inc(s_k, 1)
            v.wait_ge(s_k, 8)
            v.tensor_copy(padded[:], cnt[:]).then_inc(s_k, 1)
            v.wait_ge(s_k, 9)
            v.tensor_tensor(prod[:], lower[:], padded[:].unsqueeze(1).to_broadcast([P, E1, E1]), ALU.mult).then_inc(s_k, 1)
            v.wait_ge(s_k, 10)
            v.tensor_reduce(base[:], prod[:], AX.X, ALU.add).then_inc(s_k, 1)
            v.wait_ge(s_k, 11)
            v.tensor_tensor(ends[:], base[:], padded[:], ALU.add).then_inc(s_k, 1)
            v.wait_ge(s_k, 12)
            v.tensor_tensor(past[:], ends[:].unsqueeze(1).to_broadcast([P, SLOTS, E1]),
                            starts[:].unsqueeze(2).to_broadcast([P, SLOTS, E1]), ALU.is_le).then_inc(s_k, 1)
            v.wait_ge(s_k, 13)
            v.tensor_reduce(slotf[:], past[:], AX.X, ALU.add).then_inc(s_k, 1)
            v.wait_ge(s_k, 14)
            v.tensor_scalar(sloti[:], slotf[:], float(E1 - 1), None, ALU.min).then_inc(s_sl, 1)
            v.tensor_tensor(rank[:, 0:T, :], rank[:, 0:T, :], base[:].unsqueeze(1).to_broadcast([P, T, E1]), ALU.add).then_inc(s_k, 1)
            v.wait_ge(s_k, 15)
            v.tensor_tensor(rank[:, 0:T, :], rank[:, 0:T, :], oh[:], ALU.mult).then_inc(s_k, 1)
            v.wait_ge(s_k, 16)
            v.tensor_reduce(pos[:], rank[:, 0:T, :], AX.X, ALU.add).then_inc(s_k, 1)
            v.wait_ge(s_k, 17)
            v.tensor_copy(posi[:], pos[:]).then_inc(s_pos, 1)

            for n in range(SLOTS + 1):
                if n < SLOTS:
                    v.wait_ge(s_gt, n + 1)
                    if n >= 2:
                        v.wait_ge(s_f1, 2 * (n - 1))
                    v.tensor_copy(xgT[:, n % 2, :, :], ps[:, n % 2, 0:D].rearrange("p (k c) -> p k c", k=H2)).then_inc(s_gc, 1)
                if n:
                    v.wait_ge(s_f2, n)
                    if n >= 3:
                        v.wait_ge(s_ys[(n - 1) % 2], 16 * ((n - 1) // 2))
                    v.tensor_tensor(yg[:, (n - 1) % 2, :], ps[:, 6 + (n - 1) % 2, 0:D], wexp[:, (n - 1) % NW, BLOB - D:BLOB], ALU.add)\
                        .then_inc(s_y, 1)

            def add_moe(t):
                v.wait_ge(s_ga2, 16 * T)
                v.tensor_tensor(ht[0:rows(t), t, :], moe[0:rows(t), t, :], xn[0:rows(t), t, :], ALU.add).then_inc(s_u2, 1)
                v.wait_ge(s_u2, t + 1)
            ln_steps(v, ln5, ht, ht, before=add_moe)
            for t in range(T):
                ln5.wait_tile(v, t)
                v.tensor_tensor(ht[:, t, :], ht[:, t, :], g2_s[:], ALU.mult).then_inc(s_gain2, 1)
                v.tensor_tensor(xt[0:rows(t), t, :], xt[0:rows(t), t, :], beta2_s[0:rows(t), :], ALU.add).then_inc(s_gain2, 1)



def layout(i):
    c = np.ascontiguousarray
    row = lambda a: c(a.reshape(1, -1))
    e1, d, hid = i["L1_ffn_W1"].shape
    w1 = i["L1_ffn_W1"].reshape(e1, H2, P, hid).transpose(0, 2, 1, 3).reshape(e1, P, -1)
    w2 = i["L1_ffn_W2"].reshape(e1, hid // P, P, d).transpose(0, 2, 1, 3).reshape(e1, P, -1)
    b1 = i["L1_ffn_b1"].reshape(e1, hid // P, P).transpose(0, 2, 1)
    b2 = np.broadcast_to(i["L1_ffn_b2"][:, None, :], (e1, P, d))
    return dict(
        x=c(i["x"]), adjT=c(i["adj"].T), w_gnn=c(i["L0_gnn_weight"]), b_gnn=row(i["L0_gnn_bias"]),
        gate_wT=c(i["L0_ffn_gate_w"].T), w1=c(i["L0_ffn_w1"]), b1T=c(i["L0_ffn_b1"].T), w2=c(i["L0_ffn_w2"]), b2=c(i["L0_ffn_b2"]),
        sw1=c(i["L0_ffn_sw1"]), sb1T=c(i["L0_ffn_sb1"].reshape(-1, P).T), sw2=c(i["L0_ffn_sw2"]), sb2=row(i["L0_ffn_sb2"]),
        w_gnn1T=c(i["L1_gnn_W"].T),
        wq=c(i["L1_ffn_Wq"]), bqT=c(i["L1_ffn_bq"].reshape(-1, P).T), wk=c(i["L1_ffn_Wk"]), bkT=c(i["L1_ffn_bk"].reshape(-1, P).T),
        wv=c(i["L1_ffn_Wv"]), bv=row(i["L1_ffn_bv"]), wo=c(i["L1_ffn_Wo"]), bo=row(i["L1_ffn_bo"]),
        g1=row(i["L1_ffn_g1"]), beta1=row(i["L1_ffn_beta1"]), g2=row(i["L1_ffn_g2"]), beta2=row(i["L1_ffn_beta2"]),
        wg=c(i["L1_ffn_Wg"]), bg=row(i["L1_ffn_bg"]),
        blob=c(np.concatenate([w1, w2, b1, b2], axis=2)),
    )


def kernel(**inputs):
    import concourse.bacc as bacc
    from concourse.bass_utils import run_bass_kernel_spmd

    nc = bacc.Bacc("TRN2", target_bir_lowering=False, num_devices=1)
    arrays, args = {}, []
    for name, a in layout({k: np.asarray(v) for k, v in inputs.items()}).items():
        arrays[f"in_{name}"] = a
        args.append(nc.dram_tensor(f"in_{name}", a.shape, mybir.dt.from_np(a.dtype), kind="ExternalInput").ap())
    args.append(nc.dram_tensor("out_x", (R, D), F32, kind="ExternalOutput").ap())
    build(nc, *args)
    r = run_bass_kernel_spmd(nc, [arrays], core_ids=[0])
    return r.results[0]["out_x"]
```

```python
import numpy as np
import concourse.bass as bass
from concourse import mybir
from contextlib import ExitStack

F32 = mybir.dt.float32
F32R = mybir.dt.float32r
BF16 = mybir.dt.bfloat16
I32 = mybir.dt.int32
U32 = mybir.dt.uint32
ALU = mybir.AluOpType
ACT = mybir.ActivationFunctionType
AX = mybir.AxisListType

P = 128
R = 1354
D = 256
H2 = D // P
T = (R + P - 1) // P
LAST = R - (T - 1) * P
NC = 3
CW = 452
RW = NC * CW
G = (T + 1) // 2
E0, F0, S0 = 8, 128, 256
HEADS, DH = 8, 32
PAIRS = HEADS // 2
KA = 3 * DH
E1, HID = 8, 1024
FC = HID // P
SLOTS = (R + E1 * (P - 1)) // P
BLOB = 2 * H2 * HID + FC + D
NORM_EPS = 1e-8
LN_EPS = 1e-5


def rows(t):
    return P if t < T - 1 else LAST


def cols(t):
    return slice(t * P, t * P + rows(t))


def chunk(c):
    return slice(c * CW, (c + 1) * CW)


def build(nc, x, adjT, w_gnn, b_gnn, gate_wT, w1, b1T, w2, b2, sw1, sb1T, sw2, sb2, w_gnn1T,
          wq, bqT, wk, bkT, wv, bv, wo, bo, g1, beta1, g2, beta2, wg, bg, blob, out):
    ctx = ExitStack()
    with ctx:
        def sb(name, shape, dt=F32):
            return ctx.enter_context(nc.sbuf_tensor(name, shape, dt))

        def sem(name):
            return ctx.enter_context(nc.semaphore(name))

        ps = ctx.enter_context(nc.psum_tensor("ps", [P, 8, 512], F32))

        ident = sb("ident", [P, P])
        ones2 = sb("ones2", [P, 2])
        xt = sb("xt", [P, T, D])
        xn = sb("xn", [P, T, D])
        xT = sb("xT", [P, H2, RW])
        st = sb("st", [P, T, 6])
        mv = sb("mv", [P, T, 2])
        rstd = sb("rstd", [P, T])
        std = sb("std", [P, T])
        eps_s = sb("eps_s", [P, 1])

        w_gnn_s = sb("w_gnn_s", [P, H2, D])
        b_gnn_s = sb("b_gnn_s", [P, D])

        ht = sb("ht", [P, T, D])
        zero = sb("zero", [P, D])
        lg = sb("lg", [P, T, E0])
        top = sb("top", [P, T, 8])
        topi = sb("topi", [P, T, 8], U32)
        iota8 = sb("iota8", [P, E0])

        phase = ctx.enter_context(ExitStack())

        def sbp(name, shape, dt=F32):
            return phase.enter_context(nc.sbuf_tensor(name, shape, dt))

        adj = sbp("adj", [P, T, RW])
        hn = sbp("hn", [P, T, D])
        hT = sbp("hT", [P, H2, RW])
        sq = sbp("sq", [P, D])
        ss = sbp("ss", [P, T])
        norm = sbp("norm", [P, T])
        rnorm = sbp("rnorm", [P, T])
        NE = 2
        ex = sbp("ex", [P, NE, RW])
        ee = sbp("ee", [P, NE, RW])
        esum = sbp("esum", [P, RW])
        rden = sbp("rden", [P, T])

        EX = E0 + S0 // F0
        gate_s = sbp("gate_s", [P, H2, E0])
        w1_s = sbp("w1_s", [P, EX, H2, F0])
        w2_s = sbp("w2_s", [P, EX, D])
        b1_s = sbp("b1_s", [P, EX])
        b2_s = sbp("b2_s", [E0 + 1, D])
        mx = sbp("mx", [P, T])
        z = sbp("z", [P, T])
        topf = sbp("topf", [P, T, 2])
        pick = sbp("pick", [P, T, E0])
        comb = sbp("comb", [P, T, EX])
        combT = sbp("combT", [E0 + 1, RW])
        w_gnn1_s = sbp("w_gnn1_s", [P, H2, D])
        dg = sbp("dg", [P, T])
        dgs = sbp("dgs", [P, T])
        dscale = sbp("dscale", [P, T])

        phase.close()
        wq_s, wk_s, wv_s, wo_s = (sbp(f"w{n}_s", [P, H2, D]) for n in "qkvo")
        bq_s, bk_s = (sbp(f"b{n}_s", [P, H2]) for n in "qk")
        bv_s, bo_s, g1_s, beta1_s = (sbp(f"{n}_s", [P, D]) for n in ("bv", "bo", "g1", "beta1"))
        pr32 = sbp("pr32", [P, 2, RW])
        hi = [sbp(f"{n}_hi", [P, H2, RW], F32R) for n in "qk"]
        lo = [sbp(f"{n}_lo", [P, H2, RW], F32R) for n in "qk"]
        NA = 3
        aug = [sbp(f"{n}_aug", [KA + 1, NA, 2, RW], F32R) for n in "qk"]
        va = sbp("va", [P, T, D])
        ones32 = sbp("ones32", [P, DH])
        NPT = 2
        pt = sbp("pt", [P, NPT, 2, CW])
        acc = sbp("acc", [P, 2, CW])
        rec = sbp("rec", [2 * DH, CW])
        mxp = sbp("mxp", [P, 2, T, 2])
        nm = sbp("nm", [P, 2, T])
        mT = sbp("mT", [T, 2, P], F32R)
        cT = xT
        phase.close()
        wg_s = sbp("wg_s", [P, H2, E1])
        bg_s = sbp("bg_s", [P, E1])
        g2_s, beta2_s = (sbp(f"{n}_s", [P, D]) for n in ("g2", "beta2"))
        valid = sbp("valid", [P, T])
        before = sbp("before", [P, P], BF16)
        onesb = sbp("onesb", [P, P], BF16)
        lower = sbp("lower", [P, E1, E1])
        starts = sbp("starts", [P, SLOTS])
        oh = sbp("oh", [P, T, E1])
        ohb = sbp("ohb", [P, T, E1], BF16)
        best = sbp("best", [P, T])
        rank = sbp("rank", [P, T + 1, E1])
        cnt = sbp("cnt", [P, E1], I32)
        padded = sbp("padded", [P, E1])
        prod = sbp("prod", [P, E1, E1])
        base = sbp("base", [P, E1])
        ends = sbp("ends", [P, E1])
        pos = sbp("pos", [P, T])
        posi = sbp("posi", [P, T], U32)
        past = sbp("past", [P, SLOTS, E1])
        slotf = sbp("slotf", [P, SLOTS])
        sloti = sbp("sloti", [P, SLOTS], I32)
        NW = 4
        TL = 3
        wexp = sbp("wexp", [P, NW, BLOB])
        xg = sbp("xg", [P, SLOTS, D])
        xgT = sbp("xgT", [P, 2, H2, P])
        hid = sbp("hid", [P, 2, FC, P])
        yg = sbp("yg", [P, 2, D])
        moe = sbp("moe", [P, T, D])
        xs_d = nc.dram_tensor("xs_scratch", [SLOTS * P, D], F32).ap()
        ys_d = nc.dram_tensor("ys_scratch", [SLOTS * P, D], F32).ap()

        s_x = sem("x_loaded")
        s_wgnn = sem("gnn_weights_loaded")
        s_adj = [sem(f"adj_loaded_{n}") for n in range(2)]
        s_pad = sem("pads_cleared")
        s_id = sem("identity_ready")
        s_xb = sem("x_bias_added")

        ln_stats, ln_mean, ln_dev, ln_inv, ln_done = (
            sem(f"layernorm_{s}") for s in ("stats", "mean", "deviation", "inverse", "done"))
        turn_turned, turn_even, turn_odd = (sem(f"transposes_{s}") for s in ("turned", "even_copied", "odd_copied"))

        class LN:
            def __init__(self, n):
                self.n, self.tiles = n, n * T

            def wait_tile(self, eng, t):
                eng.wait_ge(ln_done, self.tiles + t + 1)

        class Turn:
            def __init__(self, n):
                self.n, self.groups, self.half = n, n * G, n * G // 2

            def wait_group(self, eng, g):
                eng.wait_ge(turn_even, self.half + g // 2 + 1)
                if g:
                    eng.wait_ge(turn_odd, self.half + (g + 1) // 2)

        ln0 = LN(0)
        tx = Turn(0)
        s_h = sem("h_projected")
        s_hc = sem("h_copied")
        s_ss = sem("h_squares_summed")
        s_nm = sem("h_norm_ready")
        s_rn = sem("h_norm_inverted")
        s_hn = sem("h_normalised")
        th = Turn(1)
        s_sim = sem("sim_ready")
        s_exp = sem("sim_exp_ready")
        s_e = sem("edge_weights_ready")
        s_agg = sem("aggregated")
        s_es = sem("edge_sums_added")
        s_den = sem("denominators_ready")
        s_rd = sem("denominators_inverted")
        s_x1 = sem("x1_ready")
        ln1 = LN(1)
        tx1 = Turn(2)
        s_w0 = sem("layer0_expert_weights_loaded")
        s_init = sem("stage_b_constants_ready")
        s_lg = sem("gate_logits_ready")
        s_r = sem("routing_steps")
        s_er = sem("routing_exp_ready")
        s_top = sem("top_scores_ready")
        s_comb = sem("combine_weights_ready")
        s_ct = sem("combine_turned")
        s_cc = sem("combineT_copied")
        s_up = sem("expert_up_ready")
        s_hid = sem("expert_hidden_ready")
        s_dn = sem("expert_down_ready")
        s_x2 = sem("x2_parts_added")
        ln2 = LN(2)
        s_self = sem("self_loops_added")
        s_dg = sem("diagonal_ready")
        s_dgs = sem("diagonal_root_ready")
        s_ds = sem("degree_scale_ready")
        s_g = sem("graph_product_ready")
        s_ga = sem("graph_product_even_copied")
        s_gv = sem("graph_product_odd_copied")
        s_t1 = sem("temp_ready")
        s_ts = sem("temp_scaled")
        s_p2 = sem("second_product_ready")
        s_rl = sem("second_product_rectified")
        s_x3 = sem("x3_ready")
        s_aw = sem("attention_weights_loaded")
        s_c3 = sem("stage_d_constants_ready")
        ln3 = LN(3)
        tx3 = Turn(3)
        s_dup = sem("pad_columns_doubled")
        s_pr = sem("projection_ready")
        s_pb = sem("projection_biased")
        s_hi = sem("hi_part_ready")
        s_lo = sem("lo_part_ready")
        s_v = sem("v_projected")
        s_vc = sem("v_copied")
        s_vb = sem("v_biased")
        s_aug = [sem(f"pair_operands_{n}") for n in range(NA)]
        s_s1 = sem("scores_for_max_ready")
        s_mx = sem("score_maxima_ready")
        s_neg = sem("negated_maxima_ready")
        s_mt = sem("maxima_turned")
        s_mc = sem("maxima_copied")
        s_mr = [sem(f"maxima_row_{n}") for n in range(NA)]
        s_s2 = sem("scores_ready")
        s_p = sem("probabilities_ready")
        s_pv = sem("values_weighted")
        s_ac = sem("head_outputs_copied")
        s_rc = sem("row_sums_inverted")
        s_cx = sem("head_outputs_normalised")
        s_xo = sem("attention_residual_biased")
        s_o = sem("output_projected")
        s_u = sem("attention_added")
        ln4 = LN(4)
        s_gain = sem("ln4_gain_applied")
        s_t = sem("moe_input_ready")
        s_ew = sem("moe_small_weights_loaded")
        s_c4 = sem("stage_e_constants_ready")
        s_zd = sem("slots_zeroed")
        tx4 = Turn(4)
        s_l1 = sem("moe_logits_ready")
        s_k = sem("dispatch_steps")
        s_k2 = sem("best_expert_steps")
        s_oh = sem("choices_ready")
        s_rank = sem("ranks_ready")
        s_pos = sem("positions_ready")
        s_sl = sem("slot_experts_ready")
        s_sc = sem("tokens_scattered")
        s_w = [sem(f"expert_loaded_{n}") for n in range(NW)]
        s_xg = [sem(f"slot_tokens_loaded_{n}") for n in range(TL)]
        s_gt = sem("slot_tokens_turned")
        s_gc = sem("slot_tokens_copied")
        s_f1 = sem("slot_up_ready")
        s_fg = sem("slot_gelu_ready")
        s_f2 = sem("slot_down_ready")
        s_y = sem("slot_output_ready")
        s_ys = [sem(f"slot_output_stored_{n}") for n in range(2)]
        s_ga2 = sem("outputs_gathered")
        s_u2 = sem("moe_added")
        ln5 = LN(5)
        s_gain2 = sem("ln5_gain_applied")
        s_x4 = sem("x4_parts")
        s_out = sem("output_stored")

        block = ctx.enter_context(nc.Block())

        def ln_std(act, s, eps=LN_EPS):
            act.wait_ge(ln_mean, s.tiles + T)
            act.activation(std[:], mv[:, :, 1], ACT.Sqrt, bias=eps_s[:]).then_inc(ln_dev, 1)

        def ln_steps(v, s, src, dst, before=None):
            for t in range(T + 1):
                if t < T:
                    if before:
                        before(t)
                    v.bn_stats(st[:, t, :], src[:, t, :]).then_inc(ln_stats, 1)
                if t:
                    v.wait_ge(ln_stats, s.tiles + t)
                    v.bn_aggr(mv[:, t - 1, :], st[:, t - 1, :]).then_inc(ln_mean, 1)
            v.wait_ge(ln_dev, s.n + 1)
            v.reciprocal(rstd[:], std[:]).then_inc(ln_inv, 1)
            v.wait_ge(ln_inv, s.n + 1)
            for t in range(T):
                v.tensor_scalar(dst[:, t, :], src[:, t, :], mv[:, t, 0:1], rstd[:, t:t + 1],
                                ALU.subtract, ALU.mult).then_inc(ln_done, 1)

        def turn_pe(pe, s, src, ready, banks, before=0, after=None):
            for g in range(G):
                pe.wait_ge(ready, before + min(2 * g + 2, T))
                if g >= len(banks):
                    s.wait_group(pe, g - len(banks))
                b = ps[:, banks[g % len(banks)], :].rearrange("p (k c) -> p k c", k=H2)
                for t in range(2 * g, min(2 * g + 2, T)):
                    for k in range(H2):
                        m = pe.transpose(b[:, k, (t - 2 * g) * P:(t - 2 * g) * P + rows(t)],
                                         src[0:rows(t), t, k * P:(k + 1) * P], ident[0:rows(t), 0:rows(t)])
                m.then_inc(turn_turned, 1)
                if after:
                    after(g)

        def turn_copy(eng, s, dst, banks, odd):
            for g in range(odd, G, 2):
                n = sum(rows(t) for t in range(2 * g, min(2 * g + 2, T)))
                eng.wait_ge(turn_turned, s.groups + g + 1)
                b = ps[:, banks[g % len(banks)], :].rearrange("p (k c) -> p k c", k=H2)
                o = dst[:, :, 2 * g * P:2 * g * P + n]
                if odd:
                    eng.tensor_copy(o, b[:, :, 0:n]).then_inc(turn_odd, 1)
                else:
                    eng.activation(o, b[:, :, 0:n], ACT.Copy).then_inc(turn_even, 1)

        def group(g):
            return range(2 * g, min(2 * g + 2, T))

        def gshape(ap, g):
            return ap.rearrange("p (t d) -> p t d", t=2)[0:rows(2 * g), 0:len(group(g)), :]

        def project(pe, src, wait_group, w, done, banks, freed, per=2):
            for g in range(G):
                wait_group(pe, g)
                if g >= len(banks):
                    pe.wait_ge(freed, per * (g - len(banks) + 1))
                for t in group(g):
                    for k in range(H2):
                        m = pe.matmul(half(banks[g % len(banks)], t)[0:rows(t), :], src[:, k, cols(t)], w[:, k, :],
                                      start=(k == 0), stop=(k == H2 - 1))
                m.then_inc(done, 1)

        def half(bank, t):
            return ps[:, bank, (t % 2) * D:(t % 2 + 1) * D]

        STEPS = PAIRS * NC * T

        HALVES = 2 * (NC * T - 4)

        def max_item(q):
            p, r = q // (2 * NC * T), q % (2 * NC * T)
            return [(2 * T * (p + 1) + k // 2, k % 2) for k in range(4 * T) if p + 1 < PAIRS and k * HALVES // (4 * T) == r]

        def route(v):
            v.wait_ge(s_lg, 1)
            v.wait_ge(s_init, 5)
            d = ps[:, 4, 0:E0 * T].rearrange("p (t e) -> p t e", e=E0)
            v.tensor_copy(lg[:, 0:T - 1, :], d[:, 0:T - 1, :])
            v.tensor_copy(lg[0:LAST, T - 1, :], d[0:LAST, T - 1, :]).then_inc(s_r, 1)
            v.wait_ge(s_r, 1)
            v.tensor_reduce(mx[:], lg[:], AX.X, ALU.max).then_inc(s_r, 1)
            v.wait_ge(s_r, 2)
            v.tensor_tensor(lg[:], lg[:], mx[:].unsqueeze(2).to_broadcast([P, T, E0]), ALU.subtract).then_inc(s_r, 1)
            v.wait_ge(s_er, 1)
            v.tensor_reduce(z[:], lg[:], AX.X, ALU.add).then_inc(s_r, 1)
            v.wait_ge(s_r, 4)
            v.reciprocal(z[:], z[:]).then_inc(s_r, 1)
            v.wait_ge(s_r, 5)
            v.tensor_tensor(lg[:], lg[:], z[:].unsqueeze(2).to_broadcast([P, T, E0]), ALU.mult).then_inc(s_r, 1)
            v.wait_ge(s_r, 6)
            for t in range(T):
                v.max(top[:, t, :], lg[:, t, :]).then_inc(s_top, 1)
            for t in range(T):
                v.wait_ge(s_top, t + 1)
                v.max_index(topi[:, t, :], top[:, t, :], lg[:, t, :]).then_inc(s_top, 1)
            v.tensor_reduce(z[:], top[:, :, 0:2], AX.X, ALU.add).then_inc(s_r, 1)
            v.wait_ge(s_r, 7)
            v.tensor_scalar(z[:], z[:], 1e-20, None, ALU.add).then_inc(s_r, 1)
            v.wait_ge(s_r, 8)
            v.reciprocal(z[:], z[:]).then_inc(s_r, 1)
            v.wait_ge(s_r, 9)
            v.tensor_tensor(top[:, :, 0:2], top[:, :, 0:2], z[:].unsqueeze(2).to_broadcast([P, T, 2]), ALU.mult).then_inc(s_r, 1)
            v.wait_ge(s_top, 2 * T)
            v.tensor_copy(topf[:], topi[:, :, 0:2]).then_inc(s_r, 1)
            v.wait_ge(s_r, 11)
            io = iota8[:].unsqueeze(1).to_broadcast([P, T, E0])
            first, second = (topf[:, :, a:a + 1].to_broadcast([P, T, E0]) for a in range(2))
            share1, share2 = (top[:, :, a:a + 1].to_broadcast([P, T, E0]) for a in range(2))
            cw = comb[:, :, 0:E0]
            v.tensor_tensor(cw, io, first, ALU.is_equal).then_inc(s_r, 1)
            v.tensor_tensor(pick[:], io, second, ALU.is_equal).then_inc(s_r, 1)
            v.wait_ge(s_r, 13)
            v.tensor_tensor(cw, cw, share1, ALU.mult).then_inc(s_r, 1)
            v.tensor_tensor(pick[:], pick[:], share2, ALU.mult).then_inc(s_r, 1)
            v.wait_ge(s_r, 15)
            v.tensor_tensor(cw, cw, pick[:], ALU.add).then_inc(s_comb, 1)
            v.wait_ge(s_comb, 1)

        @block.sync
        def _(sp):
            sp.wait_ge(s_pad, 4)
            sp.dma_start(xt[:, 0:T - 1, :], x[0:(T - 1) * P, :].rearrange("(t p) d -> p t d", p=P)).then_inc(s_x, 16)
            sp.dma_start(xt[0:LAST, T - 1, :], x[(T - 1) * P:R, :]).then_inc(s_x, 16)
            sp.dma_start(w_gnn_s[:], w_gnn.rearrange("(k p) o -> p k o", p=P)).then_inc(s_wgnn, 16)
            sp.dma_start(b_gnn_s[:], b_gnn.to_broadcast([P, D])).then_inc(s_wgnn, 16)
            for t in range(T):
                sp.dma_start(adj[0:rows(t), t, 0:R], adjT[t * P:t * P + rows(t), :]).then_inc(s_adj[t >= 2], 16)

            for e in range(E0):
                sp.dma_start(w1_s[:, e, :, :], w1[e].rearrange("(k p) f -> p k f", p=P)).then_inc(s_w0, 16)
            for e in range(E0, EX):
                sp.dma_start(w1_s[:, e, :, :], sw1[:, (e - E0) * F0:(e - E0 + 1) * F0].rearrange("(k p) f -> p k f", p=P)).then_inc(s_w0, 16)
            sp.dma_start(w2_s[:, 0:E0, :], w2.rearrange("e f h -> f e h")).then_inc(s_w0, 16)
            sp.dma_start(w2_s[:, E0:EX, :], sw2.rearrange("(c p) h -> p c h", p=P)).then_inc(s_w0, 16)
            sp.dma_start(b1_s[:, 0:E0], b1T).then_inc(s_w0, 16)
            sp.dma_start(b1_s[:, E0:EX], sb1T).then_inc(s_w0, 16)
            sp.dma_start(b2_s[0:E0, :], b2).then_inc(s_w0, 16)
            sp.dma_start(b2_s[E0:E0 + 1, :], sb2).then_inc(s_w0, 16)
            sp.dma_start(gate_s[:], gate_wT.rearrange("(k p) e -> p k e", p=P)).then_inc(s_w0, 16)
            sp.dma_start(w_gnn1_s[:], w_gnn1T.rearrange("(k p) o -> p k o", p=P)).then_inc(s_w0, 16)

            sp.wait_ge(s_p2, 1)
            for w_s, w in ((wq_s, wq), (wk_s, wk), (wv_s, wv), (wo_s, wo)):
                sp.dma_start(w_s[:], w.rearrange("(k p) o -> p k o", p=P)).then_inc(s_aw, 16)
            for b_s, b in ((bq_s, bqT), (bk_s, bkT)):
                sp.dma_start(b_s[:], b).then_inc(s_aw, 16)
            for b_s, b in ((bv_s, bv), (bo_s, bo), (g1_s, g1), (beta1_s, beta1)):
                sp.dma_start(b_s[:], b.to_broadcast([P, D])).then_inc(s_aw, 16)
            sp.wait_ge(s_c4, 1)
            sp.dma_start(xs_d.rearrange("(s p) d -> p s d", p=P), zero[:].unsqueeze(1).to_broadcast([P, SLOTS, D])).then_inc(s_zd, 16)

            def pair_operands(p, which=(0, 1)):
                own = slice(p * DH, (p + 1) * DH)
                for a in which:
                    src = ((hi[0], hi[0], lo[0]), (hi[1], lo[1], hi[1]))[a]
                    for r in range(3):
                        sp.dma_start(aug[a][r * DH:(r + 1) * DH, p % NA, :, :].bitcast(F32), src[r][own, :, :].bitcast(F32))\
                            .then_inc(s_aug[p % NA], 16)

            def maxima_row(n):
                p, h = n // 2, n % 2
                sp.wait_ge(s_mc, n + 1)
                row = aug[0][KA:KA + 1, p % NA, h, :].bitcast(F32)
                sp.dma_start(row[:, 0:(T - 1) * P].rearrange("a (t c) -> a t c", c=P), mT[0:T - 1, h, :].bitcast(F32)).then_inc(s_mr[p % NA], 16)
                sp.dma_start(row[:, (T - 1) * P:RW], mT[T - 1:T, h, 0:RW - (T - 1) * P].bitcast(F32)).then_inc(s_mr[p % NA], 16)

            for a in range(2):
                sp.wait_ge(s_hi, 2 * (a + 1))
                sp.wait_ge(s_lo, 2 * (a + 1))
                pair_operands(0, (a,))
            for p in range(1, NA):
                pair_operands(p)
            for n in range(4):
                maxima_row(n)
            for p in range(NA, PAIRS):
                sp.wait_ge(s_pv, NC * T * (p - NA + 1))
                pair_operands(p)
            for n in range(4, HEADS):
                maxima_row(n)

            sp.wait_ge(s_o, G)
            sp.dma_start(wg_s[:], wg.rearrange("(k p) e -> p k e", p=P)).then_inc(s_ew, 16)
            sp.dma_start(bg_s[:], bg.to_broadcast([P, E1])).then_inc(s_ew, 16)
            sp.dma_start(g2_s[:], g2.to_broadcast([P, D])).then_inc(s_ew, 16)
            sp.dma_start(beta2_s[:], beta2.to_broadcast([P, D])).then_inc(s_ew, 16)
            sp.wait_ge(s_sl, 1)

            def expert(n):
                if n >= NW:
                    sp.wait_ge(s_y, n - NW + 1)
                e = sp.value_load(sloti[0:1, n:n + 1], min_val=0, max_val=E1 - 1)
                sp.dma_start(wexp[:, n % NW, :], blob[bass.ds(e, 1), :, :].rearrange("a p n -> (a p) n")).then_inc(s_w[n % NW], 16)

            expert(0)
            sp.wait_ge(s_sc, 16 * T)
            for n in range(TL):
                own = slice(n * SLOTS // TL, (n + 1) * SLOTS // TL)
                sp.dma_start(xg[:, own, :], xs_d.rearrange("(s p) d -> p s d", p=P)[:, own, :]).then_inc(s_xg[n], 16)
                if n == 0:
                    expert(1)
            for n in range(2, SLOTS):
                expert(n)
            sp.wait_ge(s_x4, T)
            sp.dma_start(out[0:(T - 1) * P, :].rearrange("(t p) d -> p t d", p=P), xt[:, 0:T - 1, :]).then_inc(s_out, 16)
            sp.dma_start(out[(T - 1) * P:R, :], xt[0:LAST, T - 1, :]).then_inc(s_out, 16)
            sp.wait_ge(s_out, 32)

        @block.gpsimd
        def _(pool):
            pool.memset(xt[:, T - 1, :], 0.0).then_inc(s_pad, 1)
            pool.memset(xT[:, :, R:RW], 0.0).then_inc(s_pad, 1)
            pool.memset(hT[:, :, R:RW], 0.0).then_inc(s_pad, 1)
            pool.memset(adj[:, :, R:RW], 0.0).then_inc(s_pad, 1)
            pool.memset(ht[:, T - 1, :], 0.0).then_inc(s_pad, 1)
            pool.memset(ss[:, :], 0.0).then_inc(s_pad, 1)
            pool.memset(ones2[:], 1.0).then_inc(s_pad, 1)
            pool.memset(eps_s[:], LN_EPS).then_inc(s_pad, 1)
            pool.memset(lg[:, T - 1, :], 0.0).then_inc(s_init, 1)
            pool.memset(comb[:, :, E0:EX], 1.0).then_inc(s_init, 1)
            pool.memset(combT[:], 1.0).then_inc(s_init, 1)
            pool.memset(dg[:], 1.0).then_inc(s_init, 1)
            pool.iota(iota8[:], [[1, E0]], base=0, channel_multiplier=0, allow_small_or_imprecise_dtypes=True).then_inc(s_init, 1)
            pool.memset(zero[:], 0.0).then_inc(s_c4, 1)
            pool.memset(ident[:], 0.0).then_inc(s_id, 1)
            pool.wait_ge(s_id, 1)
            pool.affine_select(out=ident[:], in_=ident[:], compare_op=ALU.not_equal, fill=1.0, base=0,
                               pattern=[[-1, P]], channel_multiplier=1).then_inc(s_id, 1)
            pool.wait_ge(s_wgnn, 32)
            for t in range(T):
                ln0.wait_tile(pool, t)
                pool.tensor_tensor(xt[0:rows(t), t, :], xt[0:rows(t), t, :], b_gnn_s[0:rows(t), :], ALU.add).then_inc(s_xb, 1)
            for j in range(T - 1):
                pool.wait_ge(s_e, NC * (j + 1))
                if j == 0:
                    pool.tensor_copy(esum[:], ee[:, 0, :]).then_inc(s_es, 1)
                else:
                    pool.wait_ge(s_es, j)
                    pool.tensor_tensor(esum[:], esum[:], ee[:, j % NE, :], ALU.add).then_inc(s_es, 1)
            pool.wait_ge(s_e, NC * T)
            for t in range(T):
                a = adj[0:rows(t), t, cols(t)]
                pool.tensor_tensor(a, a, ident[0:rows(t), 0:rows(t)], ALU.add).then_inc(s_self, 1)

            pool.wait_ge(s_p2, 1)
            pool.wait_ge(s_rl, T)
            pool.memset(ones32[:], 1.0).then_inc(s_c3, 1)
            pool.wait_ge(s_c3, 1)
            pool.memset(aug[1][KA:KA + 1, :, :, :].bitcast(F32), 1.0).then_inc(s_c3, 1)
            pool.wait_ge(s_c3, 2)
            pool.memset(mxp[:, :, T - 1, :], 0.0).then_inc(s_c3, 1)
            pool.wait_ge(s_aw, 16 * 10)
            for t in range(T):
                ln3.wait_tile(pool, t)
                pool.tensor_tensor(ht[:, t, :], xn[:, t, :], bo_s[:], ALU.add).then_inc(s_xo, 1)
            for t in range(T):
                pool.wait_ge(s_vc, t // 2 + 1)
                pool.tensor_tensor(va[0:rows(t), t, :], va[0:rows(t), t, :], bv_s[0:rows(t), :], ALU.add).then_inc(s_vb, 1)
            for t in range(T):
                pool.wait_ge(s_gain, t + 1)
                pool.tensor_tensor(xn[:, t, :], xn[:, t, :], beta1_s[:], ALU.add).then_inc(s_t, 1)

            pool.memset(valid[:], 1.0).then_inc(s_c4, 1)
            pool.memset(before[:], 1.0).then_inc(s_c4, 1)
            pool.memset(onesb[:], 1.0).then_inc(s_c4, 1)
            pool.memset(lower[:], 1.0).then_inc(s_c4, 1)
            pool.iota(starts[:], [[P, SLOTS]], base=0, channel_multiplier=0, allow_small_or_imprecise_dtypes=True).then_inc(s_c4, 1)
            pool.wait_ge(s_c4, 5)
            pool.affine_select(out=valid[:], in_=valid[:], compare_op=ALU.is_ge, fill=0.0, base=R - 1, pattern=[[-P, T]],
                               channel_multiplier=-1).then_inc(s_c4, 1)
            pool.affine_select(out=before[:], in_=before[:], compare_op=ALU.is_ge, fill=0.0, base=-1, pattern=[[1, P]],
                               channel_multiplier=-1).then_inc(s_c4, 1)
            pool.affine_select(out=lower[:], in_=lower[:], compare_op=ALU.is_ge, fill=0.0, base=-1, pattern=[[1, E1], [-1, E1]],
                               channel_multiplier=0).then_inc(s_c4, 1)
            pool.wait_ge(s_zd, 16)
            pool.wait_ge(s_pos, 1)
            pool.wait_ge(s_t, T)
            for t in range(T):
                pool.indirect_dma_start(xs_d, bass.IndirectOffsetOnAxis(ap=posi[0:rows(t), t:t + 1], axis=0),
                                        xn[0:rows(t), t, :], None).then_inc(s_sc, 16)
            for n in range(SLOTS):
                pool.wait_ge(s_y, n + 1)
                pool.dma_start(ys_d[n * P:(n + 1) * P, :], yg[:, n % 2, :]).then_inc(s_ys[n % 2], 16)
            for q in range(2):
                pool.wait_ge(s_ys[q], 16 * (SLOTS // 2))
            for t in range(T):
                pool.indirect_dma_start(moe[0:rows(t), t, :], None, ys_d,
                                        bass.IndirectOffsetOnAxis(ap=posi[0:rows(t), t:t + 1], axis=0)).then_inc(s_ga2, 16)
            for t in range(T):
                pool.wait_ge(s_gain2, 2 * t + 2)
                pool.tensor_tensor(xt[0:rows(t), t, :], xt[0:rows(t), t, :], ht[0:rows(t), t, :], ALU.add).then_inc(s_x4, 1)

        HB = (4, 5, 6, 7)
        SIMB = (6, 7)

        @block.tensor
        def _(pe):
            pe.wait_ge(s_id, 2)
            turn_pe(pe, tx, xn, ln_done, (0, 1, 2, 3), ln0.tiles)
            pe.wait_ge(s_wgnn, 32)
            project(pe, xT, tx.wait_group, w_gnn_s, s_h, HB, s_ss)
            turn_pe(pe, th, hn, s_hn, (0, 1, 2, 3))

            def sim(j):
                for c in range(NC):
                    n = NC * j + c
                    if n >= 2:
                        pe.wait_ge(s_exp, n - 1)
                    else:
                        pe.wait_ge(s_ss, T)
                    for k in range(H2):
                        m = pe.matmul(ps[0:rows(j), SIMB[n % 2], 0:CW], hT[:, k, cols(j)], hT[:, k, chunk(c)],
                                      start=(k == 0), stop=(k == H2 - 1))
                    m.then_inc(s_sim, 1)

            th.wait_group(pe, G - 1)
            pe.wait_ge(s_pad, 8)
            sim(0)
            for j in range(T):
                if j + 1 < T:
                    sim(j + 1)
                pe.wait_ge(s_e, NC * (j + 1))
                for i in range(T):
                    m = pe.matmul(half(i // 2, i)[0:rows(i), :], ee[0:rows(j), j % NE, cols(i)], ht[0:rows(j), j, :],
                                  start=(j == 0 and i % 2 == 0), stop=(j == T - 1), skip_group_check=True)
                m.then_inc(s_agg, 1)
            pe.wait_ge(s_es, T - 1)
            pe.wait_ge(s_exp, NC * T)
            for i in range(T):
                o = ps[0:rows(i), SIMB[0], 2 * i:2 * i + 2]
                pe.matmul(o, esum[:, cols(i)], ones2[:], start=(i == 0), stop=False, skip_group_check=True)
                m = pe.matmul(o, ee[0:LAST, (T - 1) % NE, cols(i)], ones2[0:LAST, :], start=False, stop=True, skip_group_check=True)
            m.then_inc(s_den, 1)

            turn_pe(pe, tx1, xn, ln_done, (0, 1, 2, 3), ln1.tiles)
            tx1.wait_group(pe, G - 1)
            pe.wait_ge(s_w0, 16 * (EX + 8))
            for t in range(T):
                for k in range(H2):
                    m = pe.matmul(ps[0:rows(t), 4, E0 * t:E0 * (t + 1)], xT[:, k, cols(t)], gate_s[:, k, :],
                                  start=(k == 0), stop=(k == H2 - 1))
            m.then_inc(s_lg, 1)

            def up(e):
                for c in range(NC):
                    if e:
                        pe.wait_ge(s_hid, NC * (e - 1) + c + 1)
                    for k in range(H2):
                        m = pe.matmul(ps[:, c, 0:CW], w1_s[:, e, k, :], xT[:, k, chunk(c)], start=(k == 0), stop=(k == H2 - 1))
                    m.then_inc(s_up, 1)

            def down(e):
                pe.wait_ge(s_hid, NC * (e + 1))
                for g in range(G):
                    n = G * e + g
                    if n >= 4:
                        pe.wait_ge(s_x2, T * ((n - 4) // G) + min(2 * ((n - 4) % G) + 2, T))
                    else:
                        pe.wait_ge(s_r, 1)
                    for t in group(g):
                        m = pe.matmul(half(4 + n % 4, t)[0:rows(t), :], ee[:, e % 2, cols(t)], w2_s[:, e, :],
                                      start=True, stop=(e < EX - 1))
                        if e == EX - 1:
                            m = pe.matmul(half(4 + n % 4, t)[0:rows(t), :], combT[:, cols(t)], b2_s[:], start=False, stop=True)
                    m.then_inc(s_dn, 1)

            up(0)
            for e in range(EX - 1):
                up(e + 1)
                down(e)
            pe.wait_ge(s_comb, 1)
            pe.wait_ge(s_hid, NC * EX)
            for t in range(T):
                m = pe.transpose(ps[0:E0, t // 4, t % 4 * P:t % 4 * P + rows(t)], comb[0:rows(t), t, 0:E0], ident[0:rows(t), 0:rows(t)])
            m.then_inc(s_ct, 1)
            pe.wait_ge(s_cc, NC)
            down(EX - 1)

            pe.wait_ge(s_self, T)
            for j in range(T):
                ln2.wait_tile(pe, j)
                for k in range(H2):
                    for c in range(NC):
                        m = pe.matmul(ps[:, NC * k + c, 0:CW], xn[0:rows(j), j, k * P:(k + 1) * P], adj[0:rows(j), j, chunk(c)],
                                      start=(j == 0), stop=(j == T - 1))
            m.then_inc(s_g, 1)

            def both_copied(eng, g):
                eng.wait_ge(s_ga, 1)
                eng.wait_ge(s_gv, 1)
            project(pe, hT, both_copied, w_gnn1_s, s_t1, (6, 7), s_ts)
            for j in range(T):
                pe.wait_ge(s_ts, j + 1)
                for i in range(T):
                    m = pe.matmul(half(i // 2, i)[0:rows(i), :], adj[0:rows(j), j, cols(i)], ht[0:rows(j), j, :],
                                  start=(j == 0 and i % 2 == 0), stop=(j == T - 1), skip_group_check=True)
            m.then_inc(s_p2, 1)

            turn_pe(pe, tx3, xn, ln_done, (6, 7), ln3.tiles)
            pe.wait_ge(s_aw, 16 * 10)
            tx3.wait_group(pe, G - 1)
            pe.wait_ge(s_dup, 1)
            pe.wait_ge(s_rl, T)
            for u, (w_s, k2) in enumerate(((wq_s, 0), (wq_s, 1), (wk_s, 0), (wk_s, 1))):
                if u >= 2:
                    pe.wait_ge(s_pb, u - 1)
                for c in range(NC):
                    for k in range(H2):
                        m = pe.matmul(ps[:, 3 * (u % 2) + c, 0:CW], w_s[:, k, k2 * P:(k2 + 1) * P], xT[:, k, chunk(c)],
                                      start=(k == 0), stop=(k == H2 - 1))
                m.then_inc(s_pr, 1)
            project(pe, xT, tx3.wait_group, wv_s, s_v, (6, 7), s_vc, 1)

            def rows2(i):
                return slice(i * P, min((i + 1) * P, RW))

            def max_scores(u, part):
                n, i = u // T, u % T
                p, h = n // 2, n % 2
                if i == 0 and part == 0:
                    pe.wait_ge(s_aug[p % NA], 16 * 6 * (p // NA + 1))
                    if n:
                        pe.wait_ge(s_mc, n)
                    else:
                        pe.wait_ge(s_vc, G)
                        pe.wait_ge(s_pb, 4)
                w = rows2(i)
                if u:
                    pe.wait_ge(s_mx, 2 * (u - 1) + part + 1)
                for c in ((0, 1), (2,))[part]:
                    m = pe.matmul(ps[0:w.stop - w.start, 5 + c, 0:CW], aug[0][0:KA, p % NA, h, w], aug[1][0:KA, p % NA, h, chunk(c)],
                                  start=True, stop=True)
                m.then_inc(s_s1, 1)
                if i == T - 1 and part == 1:
                    pe.wait_ge(s_neg, n + 1)
                    pe.transpose(ps[0:T, 5, 0:P], nm[:, h, :], ident[:]).then_inc(s_mt, 1)

            def scores(n):
                p, c, k = n // (NC * T), n // T % NC, n % T
                if n % (NC * T) == 0:
                    pe.wait_ge(s_mr[p % NA], 64 * (p // NA + 1))
                    pe.wait_ge(s_c3, 3)
                    if n == 0:
                        pe.wait_ge(s_pb, 4)
                if n >= 2:
                    pe.wait_ge(s_p, n - 1)
                for h in range(2):
                    m = pe.matmul(ps[0:rows(k), 1 + 2 * (n % 2) + h, 0:CW], aug[1][:, p % NA, h, cols(k)], aug[0][:, p % NA, h, chunk(c)],
                                  start=True, stop=True)
                m.then_inc(s_s2, 1)

            def values(n):
                p, k = n // (NC * T), n % T
                if n == 0:
                    pe.wait_ge(s_vb, T)
                pe.wait_ge(s_p, n + 1)
                if k == 0 and n:
                    pe.wait_ge(s_ac, n // T)
                for a in range(4):
                    w = va[0:rows(k), k, (2 * p + a) * DH:(2 * p + a + 1) * DH] if a < 2 else ones32[0:rows(k), :]
                    m = pe.matmul(ps[DH * a:DH * (a + 1), 0, 0:CW], w, pt[0:rows(k), n % NPT, a % 2, :],
                                  start=(k == 0), stop=(k == T - 1))
                m.then_inc(s_pv, 1)

            for u in range(2 * T):
                max_scores(u, 0)
                max_scores(u, 1)
            scores(0)
            for n in range(STEPS):
                if n + 1 < STEPS:
                    scores(n + 1)
                for item in max_item(2 * n):
                    max_scores(*item)
                values(n)
                for item in max_item(2 * n + 1):
                    max_scores(*item)

            def heads_ready(eng, g):
                eng.wait_ge(s_cx, NC * PAIRS)
            project(pe, cT, heads_ready, wo_s, s_o, (1, 2, 3, 4, 5, 6), s_u)

            def gate(g):
                tx4.wait_group(pe, g)
                for t in group(g):
                    for k in range(H2):
                        m = pe.matmul(ps[0:rows(t), 4, E1 * t:E1 * (t + 1)], xT[:, k, cols(t)], wg_s[:, k, :],
                                      start=(k == 0), stop=(k == H2 - 1))
                if g == G - 1:
                    m.then_inc(s_l1, 1)

            pe.wait_ge(s_ew, 64)
            pe.wait_ge(s_u, T)
            turn_pe(pe, tx4, xn, s_t, (0, 1, 2, 3), after=lambda g: gate(g - 1) if g else None)
            gate(G - 1)
            pe.wait_ge(s_oh, 1)
            pe.wait_ge(s_c4, 9)
            for t in range(T + 1):
                o = ps[:, 5, E1 * t:E1 * (t + 1)]
                for j in range(t):
                    m = pe.matmul(o, onesb[:], ohb[:, j, :], start=(j == 0), stop=(t == T and j == T - 1))
                if t < T:
                    m = pe.matmul(o, before[:], ohb[:, t, :], start=(t == 0), stop=True)
            m.then_inc(s_rank, 1)

            def slot_turn(n):
                pe.wait_ge(s_xg[n * TL // SLOTS], 16)
                if n >= 2:
                    pe.wait_ge(s_gc, n - 1)
                for k in range(H2):
                    m = pe.transpose(ps[:, n % 2, k * P:(k + 1) * P], xg[:, n, k * P:(k + 1) * P], ident[:])
                m.then_inc(s_gt, 1)

            def slot_up(n):
                pe.wait_ge(s_w[n % NW], 16 * (n // NW + 1))
                pe.wait_ge(s_gc, n + 1)
                w = wexp[:, n % NW, 0:H2 * HID].rearrange("p (k f) -> p k f", k=H2)
                for b in range(2):
                    if n >= 2:
                        pe.wait_ge(s_fg, FC * (n - 2) + FC // 2 * (b + 1))
                    for f in range(FC // 2):
                        for k in range(H2):
                            fc = b * FC // 2 + f
                            m = pe.matmul(ps[:, 2 + 2 * (n % 2) + b, f * P:(f + 1) * P], w[:, k, fc * P:(fc + 1) * P],
                                          xgT[:, n % 2, k, :], start=(k == 0), stop=(k == H2 - 1))
                    m.then_inc(s_f1, 1)

            def slot_down(n):
                if n >= 2:
                    pe.wait_ge(s_y, n - 1)
                w = wexp[:, n % NW, H2 * HID:2 * H2 * HID].rearrange("p (c d) -> p c d", c=FC)
                for f in range(FC):
                    pe.wait_ge(s_fg, FC * n + f + 1)
                    m = pe.matmul(ps[:, 6 + n % 2, 0:D], hid[:, n % 2, f, :], w[:, f, :], start=(f == 0), stop=(f == FC - 1))
                m.then_inc(s_f2, 1)

            slot_turn(0)
            slot_turn(1)
            slot_up(0)
            for n in range(SLOTS):
                if n + 2 < SLOTS:
                    slot_turn(n + 2)
                if n + 1 < SLOTS:
                    slot_up(n + 1)
                slot_down(n)

        @block.scalar
        def _(act):
            act.wait_ge(s_pad, 8)
            ln_std(act, ln0)
            turn_copy(act, tx, xT, (0, 1, 2, 3), 0)
            for g in range(G):
                act.wait_ge(s_h, g + 1)
                bank = ps[:, HB[g % 4], :]
                act.activation(ht[0:rows(2 * g), 2 * g:2 * g + len(group(g)), :], gshape(bank, g), ACT.Copy).then_inc(s_hc, 1)
                for t in group(g):
                    if t:
                        act.wait_ge(s_ss, t)
                    act.activation(sq[0:rows(t), :], half(HB[g % 4], t)[0:rows(t), :], ACT.Square,
                                   accum_out=ss[0:rows(t), t:t + 1]).then_inc(s_ss, 1)
            act.wait_ge(s_ss, T)
            act.activation(norm[:], ss[:], ACT.Sqrt).then_inc(s_nm, 1)
            turn_copy(act, th, hT, (0, 1, 2, 3), 0)
            for j in range(T):
                for c in range(NC):
                    n = NC * j + c
                    act.wait_ge(s_sim, n + 1)
                    if j >= NE:
                        act.wait_ge(s_e, NC * (j - NE) + c + 1)
                    act.activation(ex[0:rows(j), j % NE, chunk(c)], ps[0:rows(j), SIMB[n % 2], 0:CW], ACT.Exp)\
                        .then_inc(s_exp, 1)

            ln_std(act, ln1)
            turn_copy(act, tx1, xT, (0, 1, 2, 3), 0)
            act.wait_ge(s_r, 3)
            act.activation(lg[:], lg[:], ACT.Exp).then_inc(s_er, 1)
            for e in range(EX):
                for c in range(NC):
                    act.wait_ge(s_up, NC * e + c + 1)
                    if e >= 2:
                        act.wait_ge(s_dn, G * (e - 1))
                    act.activation(ee[:, e % 2, chunk(c)], ps[:, c, 0:CW], ACT.Relu, bias=b1_s[:, e:e + 1]).then_inc(s_hid, 1)
            act.wait_ge(s_init, 5)
            act.wait_ge(s_ct, 1)
            for c in range(NC):
                n = min(512, R - 512 * c)
                act.activation(combT[0:E0, 512 * c:512 * c + n], ps[0:E0, c, 0:n], ACT.Copy).then_inc(s_cc, 1)

            act.wait_ge(s_dg, T)
            act.activation(dgs[:], dg[:], ACT.Sqrt).then_inc(s_dgs, 1)
            ln_std(act, ln2)
            act.wait_ge(s_g, 1)
            act.activation(hT[:, 0, :].rearrange("p (c w) -> p c w", c=NC), ps[:, 0:NC, 0:CW], ACT.Copy).then_inc(s_ga, 1)
            act.wait_ge(s_ds, 1)
            for t in range(T):
                act.wait_ge(s_t1, t // 2 + 1)
                act.activation(ht[0:rows(t), t, :], half(6 + t // 2 % 2, t)[0:rows(t), :], ACT.Copy,
                               scale=dscale[0:rows(t), t:t + 1]).then_inc(s_ts, 1)
            act.wait_ge(s_p2, 1)
            for t in range(T):
                act.activation(hn[0:rows(t), t, :], half(t // 2, t)[0:rows(t), :], ACT.Relu,
                               scale=dscale[0:rows(t), t:t + 1]).then_inc(s_rl, 1)

            ln_std(act, ln3)
            turn_copy(act, tx3, xT, (6, 7), 0)
            for u in range(4):
                act.wait_ge(s_pr, u + 1)
                if u >= 2:
                    act.wait_ge(s_lo, u - 1)
                act.activation(pr32[:, u % 2, :].rearrange("p (c w) -> p c w", c=NC), ps[:, 3 * (u % 2):3 * (u % 2) + 3, 0:CW],
                               ACT.Identity, bias=(bq_s, bk_s)[u // 2][:, u % 2:u % 2 + 1]).then_inc(s_pb, 1)
            for g in range(G):
                act.wait_ge(s_v, g + 1)
                act.activation(va[0:rows(2 * g), 2 * g:2 * g + len(group(g)), :], gshape(ps[:, 6 + g % 2, :], g), ACT.Copy).then_inc(s_vc, 1)
            for n in range(STEPS + 1):
                if n < STEPS:
                    act.wait_ge(s_s2, n + 1)
                    if n >= NPT:
                        act.wait_ge(s_pv, n - NPT + 1)
                    k = n % T
                    b = 1 + 2 * (n % 2)
                    act.activation(pt[0:rows(k), n % NPT, :, :], ps[0:rows(k), b:b + 2, 0:CW], ACT.Exp, scale=DH ** -0.5).then_inc(s_p, 1)
                if n and n % T == 0:
                    m = n // T - 1
                    act.wait_ge(s_pv, n)
                    if m >= 2:
                        act.wait_ge(s_cx, m - 1)
                    act.activation(acc[:, m % 2, :], ps[:, 0, 0:CW], ACT.Copy).then_inc(s_ac, 1)
            ln_std(act, ln4)

            turn_copy(act, tx4, xT, (0, 1, 2, 3), 0)
            for n in range(SLOTS):
                bias = wexp[:, n % NW, 2 * H2 * HID:2 * H2 * HID + FC]
                for f in range(FC):
                    if f % (FC // 2) == 0:
                        act.wait_ge(s_f1, 2 * n + f // (FC // 2) + 1)
                        if n >= 2:
                            act.wait_ge(s_f2, n - 1)
                    act.activation(hid[:, n % 2, f, :], ps[:, 2 + 2 * (n % 2) + f // (FC // 2), f % (FC // 2) * P:(f % (FC // 2) + 1) * P],
                                   ACT.Gelu, bias=bias[:, f:f + 1]).then_inc(s_fg, 1)
            ln_std(act, ln5)

        @block.vector
        def _(v):
            v.wait_ge(s_x, 32)
            ln_steps(v, ln0, xt, xn)
            turn_copy(v, tx, xT, (0, 1, 2, 3), 1)
            v.wait_ge(s_nm, 1)
            v.tensor_scalar(norm[:], norm[:], NORM_EPS, None, ALU.max).then_inc(s_rn, 1)
            v.wait_ge(s_rn, 1)
            v.reciprocal(rnorm[:], norm[:]).then_inc(s_rn, 1)
            v.wait_ge(s_rn, 2)
            for t in range(T):
                v.tensor_scalar(hn[:, t, :], ht[:, t, :], rnorm[:, t:t + 1], None, ALU.mult).then_inc(s_hn, 1)
            turn_copy(v, th, hT, (0, 1, 2, 3), 1)
            for j in range(T):
                if j < 3:
                    v.wait_ge(s_adj[j >= 2], 16 * (T - 2) if j >= 2 else 32)
                if j >= NE:
                    v.wait_ge(s_agg, j - NE + 1)
                    v.wait_ge(s_es, j - NE + 1)
                for c in range(NC):
                    v.wait_ge(s_exp, NC * j + c + 1)
                    v.scalar_tensor_tensor(out=ee[0:rows(j), j % NE, chunk(c)], in0=adj[0:rows(j), j, chunk(c)], scalar=NORM_EPS,
                                           in1=ex[0:rows(j), j % NE, chunk(c)], op0=ALU.add, op1=ALU.mult).then_inc(s_e, 1)
            v.wait_ge(s_den, 1)
            d = ps[:, SIMB[0], 0:2 * T].rearrange("p (t a) -> p t a", a=2)
            v.reciprocal(rden[:, 0:T - 1], d[:, 0:T - 1, 0]).then_inc(s_rd, 1)
            v.reciprocal(rden[0:LAST, T - 1:T], d[0:LAST, T - 1, 0:1]).then_inc(s_rd, 1)
            v.wait_ge(s_rd, 2)
            v.wait_ge(s_xb, T)
            v.wait_ge(s_agg, T)
            for t in range(T):
                v.scalar_tensor_tensor(out=xt[0:rows(t), t, :], in0=half(t // 2, t)[0:rows(t), :], scalar=rden[0:rows(t), t:t + 1],
                                       in1=xt[0:rows(t), t, :], op0=ALU.mult, op1=ALU.add).then_inc(s_x1, 1)

            ln_steps(v, ln1, xt, xn, before=lambda t: v.wait_ge(s_x1, t + 1))
            turn_copy(v, tx1, xT, (0, 1, 2, 3), 1)
            route(v)
            for e in range(EX):
                for g in range(G):
                    v.wait_ge(s_dn, G * e + g + 1)
                    for t in group(g):
                        if e:
                            v.wait_ge(s_x2, T * (e - 1) + t + 1)
                        v.scalar_tensor_tensor(out=xt[0:rows(t), t, :], in0=half(4 + (G * e + g) % 4, t)[0:rows(t), :],
                                               scalar=comb[0:rows(t), t, e:e + 1], in1=xt[0:rows(t), t, :],
                                               op0=ALU.mult, op1=ALU.add).then_inc(s_x2, 1)

            v.wait_ge(s_self, T)
            for t in range(T):
                v.tensor_tensor_reduce(hn[0:rows(t), t, 0:rows(t)], adj[0:rows(t), t, cols(t)], ident[0:rows(t), 0:rows(t)],
                                       1.0, 0.0, ALU.mult, ALU.add, dg[0:rows(t), t:t + 1]).then_inc(s_dg, 1)
            ln_steps(v, ln2, xt, xn, before=lambda t: v.wait_ge(s_x2, T * (EX - 1) + t + 1))
            v.wait_ge(s_dgs, 1)
            v.reciprocal(dscale[:], dgs[:]).then_inc(s_ds, 1)
            v.wait_ge(s_g, 1)
            v.tensor_copy(hT[:, 1, :].rearrange("p (c w) -> p c w", c=NC), ps[:, NC:2 * NC, 0:CW]).then_inc(s_gv, 1)
            for t in range(T):
                v.wait_ge(s_rl, t + 1)
                v.tensor_tensor(xt[0:rows(t), t, :], xt[0:rows(t), t, :], hn[0:rows(t), t, :], ALU.add).then_inc(s_x3, 1)


            ln_steps(v, ln3, xt, xn, before=lambda t: v.wait_ge(s_x3, t + 1))
            turn_copy(v, tx3, xT, (6, 7), 1)
            v.wait_ge(turn_odd, tx3.half + G // 2)
            v.tensor_copy(xT[:, :, R:RW], xT[:, :, R - 1:R].to_broadcast([P, H2, RW - R])).then_inc(s_dup, 1)
            for u in range(4):
                v.wait_ge(s_pb, u + 1)
                v.tensor_copy(hi[u // 2][:, u % 2, :], pr32[:, u % 2, :]).then_inc(s_hi, 1)
                v.wait_ge(s_hi, u + 1)
                v.tensor_tensor(lo[u // 2][:, u % 2, :], pr32[:, u % 2, :], hi[u // 2][:, u % 2, :].bitcast(F32), ALU.subtract)\
                    .then_inc(s_lo, 1)

            def maxima(u, part):
                n, i = u // T, u % T
                w = min((i + 1) * P, RW) - i * P
                if u == 0 and part == 0:
                    v.wait_ge(s_c3, 3)
                if i == 0 and part == 0 and n >= 2:
                    v.wait_ge(s_neg, n - 1)
                v.wait_ge(s_s1, 2 * u + part + 1)
                if part == 0:
                    v.tensor_reduce(mxp[0:w, n % 2, i, 0:1], ps[0:w, 5:7, 0:CW], AX.XY, ALU.max).then_inc(s_mx, 1)
                    return
                v.tensor_reduce(mxp[0:w, n % 2, i, 1:2], ps[0:w, 7, 0:CW], AX.X, ALU.max).then_inc(s_mx, 1)
                if i == T - 1:
                    v.wait_ge(s_mx, 2 * u + 2)
                    if n >= 2:
                        v.wait_ge(s_mt, n - 1)
                    v.tensor_reduce(nm[:, n % 2, :], mxp[:, n % 2, :, :], AX.X, ALU.max, negate=True).then_inc(s_neg, 1)
                    v.wait_ge(s_mt, n + 1)
                    if n >= 2:
                        q = n // 2 - 1
                        v.wait_ge(s_mr[q % NA], 64 * (q // NA + 1))
                    v.tensor_copy(mT[:, n % 2, :], ps[0:T, 5, 0:P]).then_inc(s_mc, 1)

            NR = 4

            def invert(m, r):
                own = slice(r * CW // NR, (r + 1) * CW // NR)
                if r == 0:
                    v.wait_ge(s_ac, m + 1)
                    if m:
                        v.wait_ge(s_cx, m)
                v.reciprocal(rec[:, own], acc[2 * DH:4 * DH, m % 2, own]).then_inc(s_rc, 1)

            def normalise(m):
                p, c = m // NC, m % NC
                v.wait_ge(s_rc, NR * (m + 1))
                o = p % 2 * 2 * DH
                v.tensor_tensor(cT[o:o + 2 * DH, p // 2, chunk(c)], acc[0:2 * DH, m % 2, :], rec[:], ALU.mult).then_inc(s_cx, 1)

            for u in range(2 * T):
                maxima(u, 0)
                maxima(u, 1)
            for n in range(STEPS):
                for q in (2 * n, 2 * n + 1):
                    for item in max_item(q):
                        maxima(*item)
                if n >= T and 1 <= n % T <= NR:
                    invert(n // T - 1, n % T - 1)
                if n >= T and n % T == NR + 1:
                    normalise(n // T - 1)
            for r in range(NR):
                invert(STEPS // T - 1, r)
            normalise(STEPS // T - 1)

            def add_attention(t):
                if t % 2 == 0:
                    v.wait_ge(s_o, t // 2 + 1)
                    v.wait_ge(s_xo, T)
                v.tensor_tensor(ht[0:rows(t), t, :], half(1 + t // 2, t)[0:rows(t), :], ht[0:rows(t), t, :], ALU.add).then_inc(s_u, 1)
                v.wait_ge(s_u, t + 1)
            ln_steps(v, ln4, ht, xn, before=add_attention)
            for t in range(T):
                ln4.wait_tile(v, t)
                v.tensor_tensor(xn[:, t, :], xn[:, t, :], g1_s[:], ALU.mult).then_inc(s_gain, 1)

            turn_copy(v, tx4, xT, (0, 1, 2, 3), 1)
            v.wait_ge(s_l1, 1)
            v.wait_ge(s_ew, 64)
            d = ps[:, 4, 0:E1 * T].rearrange("p (t e) -> p t e", e=E1)
            v.tensor_tensor(lg[:, 0:T - 1, :], d[:, 0:T - 1, :], bg_s[:].unsqueeze(1).to_broadcast([P, T - 1, E1]), ALU.add).then_inc(s_k, 1)
            v.tensor_tensor(lg[0:LAST, T - 1, :], d[0:LAST, T - 1, :], bg_s[0:LAST, :], ALU.add).then_inc(s_k, 1)
            v.wait_ge(s_k, 2)
            for t in range(T):
                v.max(top[:, t, :], lg[:, t, :]).then_inc(s_k2, 1)
            for t in range(T):
                v.wait_ge(s_k2, t + 1)
                v.max_index(topi[:, t, :], top[:, t, :], lg[:, t, :]).then_inc(s_k2, 1)
            v.wait_ge(s_k2, 2 * T)
            v.tensor_copy(best[:], topi[:, :, 0]).then_inc(s_k, 1)
            v.wait_ge(s_k, 3)
            v.wait_ge(s_c4, 9)
            v.tensor_tensor(oh[:], iota8[:].unsqueeze(1).to_broadcast([P, T, E1]), best[:].unsqueeze(2).to_broadcast([P, T, E1]),
                            ALU.is_equal).then_inc(s_k, 1)
            v.wait_ge(s_k, 4)
            v.tensor_tensor(oh[:], oh[:], valid[:].unsqueeze(2).to_broadcast([P, T, E1]), ALU.mult).then_inc(s_k, 1)
            v.wait_ge(s_k, 5)
            v.tensor_copy(ohb[:], oh[:]).then_inc(s_oh, 1)
            v.wait_ge(s_rank, 1)
            v.tensor_copy(rank[:], ps[:, 5, 0:E1 * (T + 1)].rearrange("p (t e) -> p t e", e=E1)).then_inc(s_k, 1)
            v.wait_ge(s_k, 6)
            v.tensor_scalar(cnt[:], rank[:, T, :], float(P - 1), None, ALU.add).then_inc(s_k, 1)
            v.wait_ge(s_k, 7)
            v.tensor_scalar(cnt[:], cnt[:], 7, 7, ALU.arith_shift_right, ALU.logical_shift_left).then_inc(s_k, 1)
            v.wait_ge(s_k, 8)
            v.tensor_copy(padded[:], cnt[:]).then_inc(s_k, 1)
            v.wait_ge(s_k, 9)
            v.tensor_tensor(prod[:], lower[:], padded[:].unsqueeze(1).to_broadcast([P, E1, E1]), ALU.mult).then_inc(s_k, 1)
            v.wait_ge(s_k, 10)
            v.tensor_reduce(base[:], prod[:], AX.X, ALU.add).then_inc(s_k, 1)
            v.wait_ge(s_k, 11)
            v.tensor_tensor(ends[:], base[:], padded[:], ALU.add).then_inc(s_k, 1)
            v.wait_ge(s_k, 12)
            v.tensor_tensor(past[:], ends[:].unsqueeze(1).to_broadcast([P, SLOTS, E1]),
                            starts[:].unsqueeze(2).to_broadcast([P, SLOTS, E1]), ALU.is_le).then_inc(s_k, 1)
            v.wait_ge(s_k, 13)
            v.tensor_reduce(slotf[:], past[:], AX.X, ALU.add).then_inc(s_k, 1)
            v.wait_ge(s_k, 14)
            v.tensor_scalar(sloti[:], slotf[:], float(E1 - 1), None, ALU.min).then_inc(s_sl, 1)
            v.tensor_tensor(rank[:, 0:T, :], rank[:, 0:T, :], base[:].unsqueeze(1).to_broadcast([P, T, E1]), ALU.add).then_inc(s_k, 1)
            v.wait_ge(s_k, 15)
            v.tensor_tensor(rank[:, 0:T, :], rank[:, 0:T, :], oh[:], ALU.mult).then_inc(s_k, 1)
            v.wait_ge(s_k, 16)
            v.tensor_reduce(pos[:], rank[:, 0:T, :], AX.X, ALU.add).then_inc(s_k, 1)
            v.wait_ge(s_k, 17)
            v.tensor_copy(posi[:], pos[:]).then_inc(s_pos, 1)

            for n in range(SLOTS + 1):
                if n < SLOTS:
                    v.wait_ge(s_gt, n + 1)
                    if n >= 2:
                        v.wait_ge(s_f1, 2 * (n - 1))
                    v.tensor_copy(xgT[:, n % 2, :, :], ps[:, n % 2, 0:D].rearrange("p (k c) -> p k c", k=H2)).then_inc(s_gc, 1)
                if n:
                    v.wait_ge(s_f2, n)
                    if n >= 3:
                        v.wait_ge(s_ys[(n - 1) % 2], 16 * ((n - 1) // 2))
                    v.tensor_tensor(yg[:, (n - 1) % 2, :], ps[:, 6 + (n - 1) % 2, 0:D], wexp[:, (n - 1) % NW, BLOB - D:BLOB], ALU.add)\
                        .then_inc(s_y, 1)

            def add_moe(t):
                v.wait_ge(s_ga2, 16 * T)
                v.tensor_tensor(ht[0:rows(t), t, :], moe[0:rows(t), t, :], xn[0:rows(t), t, :], ALU.add).then_inc(s_u2, 1)
                v.wait_ge(s_u2, t + 1)
            ln_steps(v, ln5, ht, ht, before=add_moe)
            for t in range(T):
                ln5.wait_tile(v, t)
                v.tensor_tensor(ht[:, t, :], ht[:, t, :], g2_s[:], ALU.mult).then_inc(s_gain2, 1)
                v.tensor_tensor(xt[0:rows(t), t, :], xt[0:rows(t), t, :], beta2_s[0:rows(t), :], ALU.add).then_inc(s_gain2, 1)



def layout(i):
    c = np.ascontiguousarray
    row = lambda a: c(a.reshape(1, -1))
    e1, d, hid = i["L1_ffn_W1"].shape
    w1 = i["L1_ffn_W1"].reshape(e1, H2, P, hid).transpose(0, 2, 1, 3).reshape(e1, P, -1)
    w2 = i["L1_ffn_W2"].reshape(e1, hid // P, P, d).transpose(0, 2, 1, 3).reshape(e1, P, -1)
    b1 = i["L1_ffn_b1"].reshape(e1, hid // P, P).transpose(0, 2, 1)
    b2 = np.broadcast_to(i["L1_ffn_b2"][:, None, :], (e1, P, d))
    pairs = lambda a: c(a.reshape(-1, PAIRS, 2, DH).transpose(0, 2, 1, 3).reshape(a.shape))
    halves = lambda a: c(a.reshape(-1, P).T)
    return dict(
        x=c(i["x"]), adjT=c(i["adj"].T), w_gnn=c(i["L0_gnn_weight"]), b_gnn=row(i["L0_gnn_bias"]),
        gate_wT=c(i["L0_ffn_gate_w"].T), w1=c(i["L0_ffn_w1"]), b1T=c(i["L0_ffn_b1"].T), w2=c(i["L0_ffn_w2"]), b2=c(i["L0_ffn_b2"]),
        sw1=c(i["L0_ffn_sw1"]), sb1T=c(i["L0_ffn_sb1"].reshape(-1, P).T), sw2=c(i["L0_ffn_sw2"]), sb2=row(i["L0_ffn_sb2"]),
        w_gnn1T=c(i["L1_gnn_W"].T),
        wq=pairs(i["L1_ffn_Wq"]), bqT=halves(pairs(i["L1_ffn_bq"])), wk=pairs(i["L1_ffn_Wk"]), bkT=halves(pairs(i["L1_ffn_bk"])),
        wv=c(i["L1_ffn_Wv"]), bv=row(i["L1_ffn_bv"]), wo=c(i["L1_ffn_Wo"]), bo=row(i["L1_ffn_bo"]),
        g1=row(i["L1_ffn_g1"]), beta1=row(i["L1_ffn_beta1"]), g2=row(i["L1_ffn_g2"]), beta2=row(i["L1_ffn_beta2"]),
        wg=c(i["L1_ffn_Wg"]), bg=row(i["L1_ffn_bg"]),
        blob=c(np.concatenate([w1, w2, b1, b2], axis=2)),
    )


def kernel(**inputs):
    import concourse.bacc as bacc
    from concourse.bass_utils import run_bass_kernel_spmd

    nc = bacc.Bacc("TRN2", target_bir_lowering=False, num_devices=1)
    arrays, args = {}, []
    for name, a in layout({k: np.asarray(v) for k, v in inputs.items()}).items():
        arrays[f"in_{name}"] = a
        args.append(nc.dram_tensor(f"in_{name}", a.shape, mybir.dt.from_np(a.dtype), kind="ExternalInput").ap())
    args.append(nc.dram_tensor("out_x", (R, D), F32, kind="ExternalOutput").ap())
    build(nc, *args)
    r = run_bass_kernel_spmd(nc, [arrays], core_ids=[0])
    return r.results[0]["out_x"]
```

```python
import numpy as np
import concourse.bass as bass
from concourse import mybir
from contextlib import ExitStack

F32 = mybir.dt.float32
F32R = mybir.dt.float32r
BF16 = mybir.dt.bfloat16
I32 = mybir.dt.int32
U32 = mybir.dt.uint32
ALU = mybir.AluOpType
ACT = mybir.ActivationFunctionType
AX = mybir.AxisListType

P = 128
R = 1354
D = 256
H2 = D // P
T = (R + P - 1) // P
LAST = R - (T - 1) * P
NC = 3
CW = 452
RW = NC * CW
G = (T + 1) // 2
E0, F0, S0 = 8, 128, 256
HEADS, DH = 8, 32
PAIRS = HEADS // 2
KA = 3 * DH
E1, HID = 8, 1024
FC = HID // P
SLOTS = (R + E1 * (P - 1)) // P
BLOB = 2 * H2 * HID + FC + D
NORM_EPS = 1e-8
LN_EPS = 1e-5


def rows(t):
    return P if t < T - 1 else LAST


def cols(t):
    return slice(t * P, t * P + rows(t))


def chunk(c):
    return slice(c * CW, (c + 1) * CW)


def build(nc, x, adjT, w_gnn, b_gnn, gate_wT, w1, b1T, w2, b2, sw1, sb1T, sw2, sb2, w_gnn1T,
          wq, bqT, wk, bkT, wv, bv, wo, bo, g1, beta1, g2, beta2, wg, bg, blob, out):
    ctx = ExitStack()
    with ctx:
        def sb(name, shape, dt=F32):
            return ctx.enter_context(nc.sbuf_tensor(name, shape, dt))

        def sem(name):
            return ctx.enter_context(nc.semaphore(name))

        def shared(home, name, shape):
            with nc.sbuf_tensor(name, shape, F32) as plain:
                pass
            return plain, home.enter_context(nc.sbuf_tensor(f"{name}_r", shape, F32R))

        ps = ctx.enter_context(nc.psum_tensor("ps", [P, 8, 512], F32))

        ident = sb("ident", [P, P])
        ones2 = sb("ones2", [P, 2])
        xt = sb("xt", [P, T, D])
        xn, xn_r = shared(ctx, "xn", [P, T, D])
        xT, xT_r = shared(ctx, "xT", [P, H2, RW])
        warm = sb("warm", [P, 5])
        st = sb("st", [P, T, 6])
        mv = sb("mv", [P, T, 2])
        rstd = sb("rstd", [P, T])
        std = sb("std", [P, T])
        eps_s = sb("eps_s", [P, 1])

        ht, ht_r = shared(ctx, "ht", [P, T, D])
        lg = sb("lg", [P, T, E0])
        top = sb("top", [P, T, 8])
        topi = sb("topi", [P, T, 8], U32)
        iota8 = sb("iota8", [P, E0])

        with ExitStack() as first:
            hn, hn_r = shared(first, "hn", [P, T, D])
            w_gnn_s, w_gnn_lo = shared(first, "w_gnn_s", [P, H2, D])
            b_gnn_s = first.enter_context(nc.sbuf_tensor("b_gnn_s", [P, D], F32))
        (wq_s, wq_lo), (wk_s, wk_lo), (wv_s, wv_lo) = (shared(ctx, f"w{n}_s", [P, H2, D]) for n in "qkv")
        wq_hi, wk_hi, wv_hi = (sb(f"w{n}_hi", [P, H2, D], F32R) for n in "qkv")
        wo_s = sb("wo_s", [P, H2, D])

        phase = ctx.enter_context(ExitStack())

        def sbp(name, shape, dt=F32):
            return phase.enter_context(nc.sbuf_tensor(name, shape, dt))

        adj, adj_r = shared(phase, "adj", [P, T, RW])
        w_gnn1_s = sbp("w_gnn1_s", [P, H2, D])
        dg = sbp("dg", [P, T])
        dgs = sbp("dgs", [P, T])
        dscale = sbp("dscale", [P, T])
        phase_ab = ctx.enter_context(ExitStack())

        def sbab(name, shape, dt=F32):
            return phase_ab.enter_context(nc.sbuf_tensor(name, shape, dt))

        fT_hi = sbab("fT_hi", [P, H2, RW], F32R)
        fT_lo = sbab("fT_lo", [P, H2, RW], F32R)
        EX = E0 + S0 // F0
        w1_s, w1_lo = shared(phase_ab, "w1_s", [P, EX, H2, F0])
        w2_s, w2_lo = shared(phase_ab, "w2_s", [P, EX, D])
        ss = sbab("ss", [P, T])
        norm = sbab("norm", [P, T])
        rnorm = sbab("rnorm", [P, T])
        NE = 2
        ex, ex_r = shared(phase_ab, "ex", [P, NE, RW])
        ee = sbab("ee", [P, NE, RW])
        ee_hi = sbab("ee_hi", [P, NE, RW], F32R)
        esum = sbab("esum", [P, RW])
        rden = sbab("rden", [P, T])
        w_gnn_hi = sbab("w_gnn_hi", [P, H2, D], F32R)
        sq = sbab("sq", [P, D])

        w1_hi = hn_r[:].rearrange("p t d -> p (t d)")[:, 0:EX * D].rearrange("p (e k f) -> p e k f", e=EX, k=H2)
        w2_hi = xT_r[:].rearrange("p k c -> p (k c)")[:, 0:EX * D].rearrange("p (e n) -> p e n", e=EX)
        gate_s, gate_lo = shared(phase_ab, "gate_s", [P, H2, E0])
        gate_hi = sbab("gate_hi", [P, H2, E0], F32R)
        b1_s = sbab("b1_s", [P, EX])
        b2_s = sbab("b2_s", [E0 + 1, D])
        mx = sbab("mx", [P, T])
        z = sbab("z", [P, T])
        topf = sbab("topf", [P, T, 2])
        pick = sbab("pick", [P, T, E0])
        comb = sbab("comb", [P, T, EX])
        combT = esum
        phase_ab.close()
        adj_hi = sbp("adj_hi", [P, T, RW], F32R)
        with nc.sbuf_tensor("gT", [P, H2, RW], F32) as gT:
            pass
        gy = sbp("gy", [P, T, D])

        phase.close()
        xT_lo = sbp("xT_lo", [P, H2, RW], F32R)
        bq_s, bk_s = (sbp(f"b{n}_s", [P, H2]) for n in "qk")
        bv_s, bo_s, g1_s, beta1_s = (sbp(f"{n}_s", [P, D]) for n in ("bv", "bo", "g1", "beta1"))
        hi = [sbp(f"{n}_hi", [P, H2, RW], F32R) for n in "qk"]
        lo = [sbp(f"{n}_lo", [P, H2, RW], F32R) for n in "qk"]
        NA = 3
        aug = [sbp(f"{n}_aug", [KA + 1, NA, 2, RW], F32R) for n in "qk"]
        va = sbp("va", [P, T, D])
        ones32 = sbp("ones32", [P, DH])
        NPT = 2
        pt = sbp("pt", [P, NPT, 2, CW])
        acc = sbp("acc", [P, 2, CW])
        rec = sbp("rec", [2 * DH, CW])
        mxp = sbp("mxp", [P, 2, 8, 2])
        nm = sbp("nm", [P, 2, 8])
        mT = sbp("mT", [8, 2, P], F32R)
        SW = 4
        spread = sbp("spread", [CW // SW, 2, SW])
        spread_inv = sbp("spread_inv", [CW // SW, 2, SW])
        inv_d = nc.dram_tensor("inverse_sums_scratch", [PAIRS * NC, 2, CW], F32).ap()
        cT = xT
        phase.close()
        wg_s = sbp("wg_s", [P, H2, E1])
        bg_s = sbp("bg_s", [P, E1])
        g2_s, beta2_s = (sbp(f"{n}_s", [P, D]) for n in ("g2", "beta2"))
        valid = sbp("valid", [P, T])
        lgT = sbp("lgT", [E1, RW])
        before = sbp("before", [P, P], BF16)
        onesb = sbp("onesb", [P, P], BF16)
        lower = sbp("lower", [P, E1, E1])
        starts = sbp("starts", [P, SLOTS])
        oh = sbp("oh", [P, T, E1])
        ohb = sbp("ohb", [P, T, E1], BF16)
        best = sbp("best", [P, T])
        rank = sbp("rank", [P, T + 1, E1])
        cnt = sbp("cnt", [P, E1], I32)
        padded = sbp("padded", [P, E1])
        prod = sbp("prod", [P, E1, E1])
        base = sbp("base", [P, E1])
        ends = sbp("ends", [P, E1])
        pos = sbp("pos", [P, T])
        posi = sbp("posi", [P, T], I32)
        place_i = sbp("place_i", [P, 2, T], I32)
        place = sbp("place", [P, 2, T])
        token = sbp("token", [P, T])
        iota = sbp("iota", [P, P])
        spare = sbp("spare", [P, SLOTS])
        in_row = sbp("in_row", [P, T, P], F32R)
        in_slot = sbp("in_slot", [P, T, 2 * SLOTS], F32R)
        unused = sbp("unused", [P, SLOTS])
        src_row = sbp("src_row", [P, SLOTS], U32)
        dst_row = sbp("dst_row", [P, SLOTS], U32)
        past = sbp("past", [P, SLOTS, E1])
        slotf = sbp("slotf", [P, SLOTS])
        sloti = sbp("sloti", [P, SLOTS], I32)
        NW = 4
        TG = 4

        def gathered(q):
            return range(q * TG, min((q + 1) * TG, T))

        NX = 6
        wexp = sbp("wexp", [P, NW, BLOB])
        xg = sbp("xg", [P, NX, D])
        xgT = sbp("xgT", [P, 2, H2, P])
        hid = sbp("hid", [P, 2, FC, P])
        yg = sbp("yg", [P, 2, D + 2])
        moe = sbp("moe", [P, T, D + 2])
        t_d = nc.dram_tensor("moe_input_scratch", [R, D], F32).ap()
        ys_d = nc.dram_tensor("moe_output_scratch", [R + SLOTS * P, D + 2], F32).ap()

        s_x = [sem(f"x_loaded_{n}") for n in range(2)]
        s_wgnn = sem("gnn_weights_loaded")
        s_adj = [sem(f"adj_loaded_{n}") for n in range(2)]
        s_pad = sem("pads_cleared")
        s_id = sem("identity_ready")
        s_xb = sem("x_bias_added")

        ln_stats, ln_mean, ln_dev, ln_inv, ln_done = (
            sem(f"layernorm_{s}") for s in ("stats", "mean", "deviation", "inverse", "done"))
        turn_turned, turn_copied = (sem(f"transposes_{s}") for s in ("turned", "copied"))

        class LN:
            def __init__(self, n):
                self.n, self.tiles = n, n * T

            def wait_tile(self, eng, t):
                eng.wait_ge(ln_done, self.tiles + t + 1)

        def chunk_of(t):
            return (min((t + 1) * P, R) - 1) // CW

        def chunk_group(c):
            return (min((c + 1) * CW, R) - 1) // (2 * P)

        class Turn:
            def __init__(self, n):
                self.groups = n * G

            def wait_group(self, eng, g):
                eng.wait_ge(turn_copied, g + 1)

        class Split:
            def __init__(self, n, m):
                self.groups, self.m = n * G, m

            def wait_group(self, eng, g):
                eng.wait_ge(split_lo, self.m * G + g + 1)

        split_hi, split_lo = (sem(f"transposes_{s}") for s in ("upper_part_copied", "low_part_ready"))
        ln0 = LN(0)
        tx = Split(0, 0)
        s_h = sem("h_projected")
        s_hc = sem("h_copied")
        s_ss = sem("h_squares_summed")
        s_nm = sem("h_norm_ready")
        s_rn = sem("h_norm_inverted")
        s_hn = sem("h_normalised")
        th = Split(1, 1)
        s_sim = sem("sim_ready")
        s_exp = sem("sim_exp_ready")
        s_e = sem("edge_weights_ready")
        s_eh = sem("edge_weights_upper_ready")
        s_el = sem("edge_weights_low_ready")
        s_hh = sem("h_upper_ready")
        s_hl = sem("h_low_ready")
        s_ws = sem("layer0_weights_split")
        s_hr = sem("hidden_upper_ready")
        s_hd = sem("hidden_low_ready")
        s_ah = sem("adj_upper_ready")
        s_al = sem("adj_low_ready")
        s_xh = sem("x2_upper_ready")
        s_xl = sem("x2_low_ready")
        s_tl = sem("temp_split")
        s_agg = sem("aggregated")
        s_es = sem("edge_sums_added")
        s_den = sem("denominators_ready")
        s_rd = sem("denominators_inverted")
        s_x1 = sem("x1_ready")
        ln1 = LN(1)
        tx1 = Split(2, 2)
        s_w0 = sem("layer0_expert_weights_loaded")
        s_init = sem("stage_b_constants_ready")
        s_lg = sem("gate_logits_ready")
        s_r = sem("routing_steps")
        s_er = sem("routing_exp_ready")
        s_top = sem("top_scores_ready")
        s_comb = sem("combine_weights_ready")
        s_ct = sem("combine_turned")
        s_cc = sem("combineT_copied")
        s_up = sem("expert_up_ready")
        s_dn = sem("expert_down_ready")
        s_x2 = sem("x2_parts_added")
        ln2 = LN(2)
        s_self = sem("self_loops_added")
        s_dg = sem("diagonal_ready")
        s_dgs = sem("diagonal_root_ready")
        s_ds = sem("degree_scale_ready")
        s_g = sem("graph_product_ready")
        s_ga = sem("graph_product_even_copied")
        s_gv = sem("graph_product_odd_copied")
        s_t1 = sem("temp_ready")
        s_ts = sem("temp_scaled")
        s_p2 = sem("second_product_ready")
        s_rl = sem("second_product_rectified")
        s_x3 = sem("x3_ready")
        s_aw = sem("attention_biases_loaded")
        s_wa = sem("attention_weights_loaded")
        s_was = sem("attention_weights_split")
        s_wgs = sem("gnn_weights_split")
        s_c3 = sem("stage_d_constants_ready")
        ln3 = LN(3)
        tx3 = Split(3, 3)
        s_dup = sem("pad_columns_doubled")
        s_pr = sem("projection_ready")
        s_hi = sem("hi_part_ready")
        s_lo = sem("lo_part_ready")
        s_vp = sem("v_projected")
        s_vc = sem("v_copied")
        s_vb = sem("v_biased")
        s_aug = [sem(f"pair_operands_{n}") for n in range(NA)]
        s_s1 = sem("scores_for_max_ready")
        s_mx = sem("score_maxima_ready")
        s_neg = sem("negated_maxima_ready")
        s_mt = sem("maxima_turned")
        s_mc = sem("maxima_copied")
        s_mr = [sem(f"maxima_rows_{n}") for n in range(NC)]
        s_sp = sem("row_sums_spread")
        s_si = sem("spread_sums_inverted")
        s_sd2 = sem("inverse_sums_stored")
        s_rb = sem("inverse_sums_repeated")
        s_s2 = sem("scores_ready")
        s_p = sem("probabilities_ready")
        s_pv = sem("values_weighted")
        s_ac = sem("head_outputs_copied")
        s_rc = sem("row_sums_inverted")
        s_cx = sem("head_outputs_normalised")
        s_xo = sem("attention_residual_biased")
        s_o = sem("output_projected")
        s_u = sem("attention_added")
        ln4 = LN(4)
        s_gain = sem("ln4_gain_applied")
        s_t = sem("moe_input_ready")
        s_ew = sem("moe_small_weights_loaded")
        s_c4 = sem("stage_e_constants_ready")
        s_td = sem("moe_input_stored")
        s_pl = sem("place_steps")
        s_sel = sem("selections_ready")
        s_inv = sem("slot_tokens_found")
        s_src = sem("source_rows_ready")
        s_dst = sem("target_rows_ready")
        tx4 = Turn(4)
        s_lc = sem("moe_logit_chunks_ready")
        s_lt = sem("moe_logit_chunks_copied")
        s_l1 = sem("moe_logits_ready")
        s_k = sem("dispatch_steps")
        s_k2 = sem("best_expert_steps")
        s_oh = sem("choices_ready")
        s_rank = sem("ranks_ready")
        s_sl = sem("slot_experts_ready")
        s_w = [sem(f"expert_loaded_{n}") for n in range(NW)]
        s_xg = [sem(f"slot_tokens_loaded_{n}") for n in range(NX)]
        s_gt = sem("slot_tokens_turned")
        s_gc = sem("slot_tokens_copied")
        s_f1 = sem("slot_up_ready")
        s_fg = sem("slot_gelu_ready")
        s_f2 = sem("slot_down_ready")
        s_y = sem("slot_output_ready")
        s_ys = [sem(f"slot_output_stored_{n}") for n in range(2)]
        s_ga2 = [sem(f"outputs_gathered_{n}") for n in range((T + TG - 1) // TG)]
        s_xb2 = sem("x3_offset_added")
        s_v = sem("slot_output_steps")
        s_sd = sem("deviations_ready")
        s_is = sem("deviations_inverted")
        s_x4 = sem("x4_parts")
        s_out = sem("output_stored")

        block = ctx.enter_context(nc.Block())

        CUT = 3
        BATCHES = ((0, CUT), (CUT, T))

        def ln_std(act, s, batches=(0, 1)):
            for n in batches:
                a, b = BATCHES[n]
                act.wait_ge(ln_mean, s.tiles + b)
                act.activation(std[:, a:b], mv[:, a:b, 1], ACT.Sqrt, bias=eps_s[:]).then_inc(ln_dev, 1)

        def preload(act, n, function):
            act.activation(warm[:, n:n + 1], eps_s[:], function)

        def ln_steps(v, s, src, dst, before=lambda t: None, arrived=lambda t: None, after=lambda t: None, ahead=CUT + 2,
                     gain=None):
            def moments(a, b):
                for t in range(a, b + 1):
                    if t < b:
                        if t + 1 < T:
                            before(t + 1)
                        arrived(t)
                        v.bn_stats(st[:, t, :], src[:, t, :]).then_inc(ln_stats, 1)
                    if t > a:
                        v.wait_ge(ln_stats, s.tiles + t)
                        v.bn_aggr(mv[:, t - 1, :], st[:, t - 1, :]).then_inc(ln_mean, 1)

            before(0)
            moments(0, CUT)
            moments(CUT, ahead)
            for n, (a, b) in enumerate(BATCHES):
                if gain:
                    v.wait_ge(ln_mean, s.tiles + b)
                    for t in range(a, b):
                        v.scalar_tensor_tensor(out=dst[:, t, :], in0=src[:, t, :], scalar=mv[:, t, 0:1], in1=gain[0][:],
                                               op0=ALU.subtract, op1=ALU.mult).then_inc(gain[2], 1)
                v.wait_ge(ln_dev, 2 * s.n + n + 1)
                v.reciprocal(rstd[:, a:b], std[:, a:b]).then_inc(ln_inv, 1)
                v.wait_ge(ln_inv, 2 * s.n + n + 1)
                for t in range(a, b):
                    if gain:
                        v.wait_ge(gain[2], t + 1)
                        v.scalar_tensor_tensor(out=dst[:, t, :], in0=dst[:, t, :], scalar=rstd[:, t:t + 1], in1=gain[1][:],
                                               op0=ALU.mult, op1=ALU.add).then_inc(gain[3], 1)
                    else:
                        v.tensor_scalar(dst[:, t, :], src[:, t, :], mv[:, t, 0:1], rstd[:, t:t + 1],
                                        ALU.subtract, ALU.mult).then_inc(ln_done, 1)
                    after(t)
                if n == 0:
                    moments(ahead, T)

        def turn_pe(pe, s, src, ready, banks, before=0, after=None):
            for g in range(G):
                pe.wait_ge(ready, before + min(2 * g + 2, T))
                if g >= len(banks):
                    s.wait_group(pe, g - len(banks))
                b = ps[:, banks[g % len(banks)], :].rearrange("p (k c) -> p k c", k=H2)
                for t in range(2 * g, min(2 * g + 2, T)):
                    for k in range(H2):
                        m = pe.transpose(b[:, k, (t - 2 * g) * P:(t - 2 * g) * P + rows(t)],
                                         src[0:rows(t), t, k * P:(k + 1) * P], ident[0:rows(t), 0:rows(t)])
                m.then_inc(turn_turned, 1)
                if after:
                    after(g)

        def turn_copy(act, s, dst, banks):
            for g in range(G):
                n = sum(rows(t) for t in group(g))
                act.wait_ge(turn_turned, s.groups + g + 1)
                b = ps[:, banks[g % len(banks)], :].rearrange("p (k c) -> p k c", k=H2)
                act.activation(dst[:, :, 2 * g * P:2 * g * P + n], b[:, :, 0:n], ACT.Copy).then_inc(turn_copied, 1)

        def split_copy(eng, s, dst_hi, dst_lo, banks):
            for g in range(G):
                n = sum(rows(t) for t in range(2 * g, min(2 * g + 2, T)))
                b = ps[:, banks[g % len(banks)], :].rearrange("p (k c) -> p k c", k=H2)[:, :, 0:n]
                own = slice(2 * g * P, 2 * g * P + n)
                if dst_lo is None:
                    eng.wait_ge(turn_turned, s.groups + g + 1)
                    eng.activation(dst_hi[:, :, own], b, ACT.Copy).then_inc(split_hi, 1)
                else:
                    eng.wait_ge(split_hi, s.m * G + g + 1)
                    eng.tensor_tensor(dst_lo[:, :, own], b, dst_hi[:, :, own].bitcast(F32), ALU.subtract).then_inc(split_lo, 1)

        def product3(pe, out, a, b, start, stop, skip=False):
            for n, (p, q) in enumerate(((0, 0), (0, 1), (1, 0))):
                m = pe.matmul(out, a[p], b[q], start=start and n == 0, stop=stop and n == 2, skip_group_check=skip)
            return m

        def group(g):
            return range(2 * g, min(2 * g + 2, T))

        def gshape(ap, g):
            return ap.rearrange("p (t d) -> p t d", t=2)[0:rows(2 * g), 0:len(group(g)), :]

        def project(pe, src, wait_group, w, done, banks, freed, per=2):
            for g in range(G):
                wait_group(pe, g)
                if g >= len(banks):
                    pe.wait_ge(freed, per * (g - len(banks) + 1))
                for t in group(g):
                    for k in range(H2):
                        m = pe.matmul(half(banks[g % len(banks)], t)[0:rows(t), :], src[:, k, cols(t)], w[:, k, :],
                                      start=(k == 0), stop=(k == H2 - 1))
                m.then_inc(done, 1)

        def token_product(pe, bank, t, x, w):
            for k in range(H2):
                m = product3(pe, half(bank, t)[0:rows(t), :], [f[:, k, cols(t)] for f in x], [f[:, k, :] for f in w], k == 0, k == H2 - 1)
            return m

        def half(bank, t):
            return ps[:, bank, (t % 2) * D:(t % 2 + 1) * D]

        CR = (T + 3) // 4

        STEPS = PAIRS * NC * T

        UNITS = PAIRS * NC
        UNIT_TILES = ((0, 4), (4, 8), (8, T))
        assert all(b * P >= min((q + 1) * CW, R) for q, (a, b) in enumerate(UNIT_TILES))

        def unit_scores(g):
            return [(g, h, i, part) for h in range(2) for i in range(*UNIT_TILES[g % NC]) for part in range(2)]

        def all_units():
            steps = unit_scores(0) + [(0, None, None, None)]
            for g in range(1, UNITS):
                own = unit_scores(g)
                steps += own[0:2] + ([(g - 1, None, None, None)] if g > 1 else []) + own[2:]
            return steps + [(UNITS - 1, None, None, None)]

        MAX_STEPS = all_units()
        MAX_PLACE = {m: k for k, m in enumerate(m for m in MAX_STEPS if m[1] is not None)}
        FIRST = len(unit_scores(0)) + 1
        AHEAD = FIRST + 4
        RATE = 90

        def max_items(q):
            return [m for k, m in enumerate(MAX_STEPS[AHEAD:]) if k * 100 // RATE == q]

        def max_set(g, i, h):
            return 1 if g == 0 and (h * UNIT_TILES[0][1] + i) % 2 else 5

        def rows_loaded(g):
            return (64 if g % NC == NC - 1 else 32) * (g // NC + 1)

        def route(v):
            v.wait_ge(s_lg, 1)
            v.wait_ge(s_init, 5)
            d = ps[:, 4, 0:E0 * T].rearrange("p (t e) -> p t e", e=E0)
            v.tensor_copy(lg[:, 0:T - 1, :], d[:, 0:T - 1, :])
            v.tensor_copy(lg[0:LAST, T - 1, :], d[0:LAST, T - 1, :]).then_inc(s_r, 1)
            v.wait_ge(s_r, 1)
            v.tensor_reduce(mx[:], lg[:], AX.X, ALU.max).then_inc(s_r, 1)
            v.wait_ge(s_r, 2)
            v.tensor_tensor(lg[:], lg[:], mx[:].unsqueeze(2).to_broadcast([P, T, E0]), ALU.subtract).then_inc(s_r, 1)
            v.wait_ge(s_er, 1)
            v.tensor_reduce(z[:], lg[:], AX.X, ALU.add).then_inc(s_r, 1)
            v.wait_ge(s_r, 4)
            v.reciprocal(z[:], z[:]).then_inc(s_r, 1)
            v.wait_ge(s_r, 5)
            v.tensor_tensor(lg[:], lg[:], z[:].unsqueeze(2).to_broadcast([P, T, E0]), ALU.mult).then_inc(s_r, 1)
            v.wait_ge(s_r, 6)
            for t in range(T):
                v.max(top[:, t, :], lg[:, t, :]).then_inc(s_top, 1)
            for t in range(T):
                v.wait_ge(s_top, t + 1)
                v.max_index(topi[:, t, :], top[:, t, :], lg[:, t, :]).then_inc(s_top, 1)
            v.tensor_reduce(z[:], top[:, :, 0:2], AX.X, ALU.add).then_inc(s_r, 1)
            v.wait_ge(s_r, 7)
            v.tensor_scalar(z[:], z[:], 1e-20, None, ALU.add).then_inc(s_r, 1)
            v.wait_ge(s_r, 8)
            v.reciprocal(z[:], z[:]).then_inc(s_r, 1)
            v.wait_ge(s_r, 9)
            v.tensor_tensor(top[:, :, 0:2], top[:, :, 0:2], z[:].unsqueeze(2).to_broadcast([P, T, 2]), ALU.mult).then_inc(s_r, 1)
            v.wait_ge(s_top, 2 * T)
            v.tensor_copy(topf[:], topi[:, :, 0:2]).then_inc(s_r, 1)
            v.wait_ge(s_r, 11)
            io = iota8[:].unsqueeze(1).to_broadcast([P, T, E0])
            first, second = (topf[:, :, a:a + 1].to_broadcast([P, T, E0]) for a in range(2))
            share1, share2 = (top[:, :, a:a + 1].to_broadcast([P, T, E0]) for a in range(2))
            cw = comb[:, :, 0:E0]
            v.tensor_tensor(cw, io, first, ALU.is_equal).then_inc(s_r, 1)
            v.tensor_tensor(pick[:], io, second, ALU.is_equal).then_inc(s_r, 1)
            v.wait_ge(s_r, 13)
            v.tensor_tensor(cw, cw, share1, ALU.mult).then_inc(s_r, 1)
            v.tensor_tensor(pick[:], pick[:], share2, ALU.mult).then_inc(s_r, 1)
            v.wait_ge(s_r, 15)
            v.tensor_tensor(cw, cw, pick[:], ALU.add).then_inc(s_comb, 1)
            v.wait_ge(s_comb, 1)

        @block.sync
        def _(sp):
            for n, (a, b) in enumerate(BATCHES):
                b = min(b, T - 1)
                sp.dma_start(xt[:, a:b, :], x[a * P:b * P, :].rearrange("(t p) d -> p t d", p=P)).then_inc(s_x[n], 16)
            sp.wait_ge(s_pad, 4)
            sp.dma_start(xt[0:LAST, T - 1, :], x[(T - 1) * P:R, :]).then_inc(s_x[1], 16)
            sp.dma_start(w_gnn_s[:], w_gnn.rearrange("(k p) o -> p k o", p=P)).then_inc(s_wgnn, 16)
            sp.dma_start(b_gnn_s[:], b_gnn.to_broadcast([P, D])).then_inc(s_wgnn, 16)
            for t in range(T):
                sp.dma_start(adj[0:rows(t), t, 0:R], adjT[t * P:t * P + rows(t), :]).then_inc(s_adj[t >= 2], 16)

            for e in range(E0):
                sp.dma_start(w1_s[:, e, :, :], w1[e].rearrange("(k p) f -> p k f", p=P)).then_inc(s_w0, 16)
            for e in range(E0, EX):
                sp.dma_start(w1_s[:, e, :, :], sw1[:, (e - E0) * F0:(e - E0 + 1) * F0].rearrange("(k p) f -> p k f", p=P)).then_inc(s_w0, 16)
            sp.dma_start(w2_s[:, 0:E0, :], w2.rearrange("e f h -> f e h")).then_inc(s_w0, 16)
            sp.dma_start(w2_s[:, E0:EX, :], sw2.rearrange("(c p) h -> p c h", p=P)).then_inc(s_w0, 16)
            sp.dma_start(b1_s[:, 0:E0], b1T).then_inc(s_w0, 16)
            sp.dma_start(b1_s[:, E0:EX], sb1T).then_inc(s_w0, 16)
            sp.dma_start(b2_s[0:E0, :], b2).then_inc(s_w0, 16)
            sp.dma_start(b2_s[E0:E0 + 1, :], sb2).then_inc(s_w0, 16)
            sp.dma_start(gate_s[:], gate_wT.rearrange("(k p) e -> p k e", p=P)).then_inc(s_w0, 16)
            sp.dma_start(w_gnn1_s[:], w_gnn1T.rearrange("(k p) o -> p k o", p=P)).then_inc(s_w0, 16)

            sp.wait_ge(s_up, NC * EX)
            for w_s, w in ((wq_s, wq), (wk_s, wk), (wv_s, wv), (wo_s, wo)):
                sp.dma_start(w_s[:], w.rearrange("(k p) o -> p k o", p=P)).then_inc(s_wa, 16)
            sp.wait_ge(s_p2, G)
            for b_s, b in ((bq_s, bqT), (bk_s, bkT)):
                sp.dma_start(b_s[:], b).then_inc(s_aw, 16)
            for b_s, b in ((bv_s, bv), (bo_s, bo), (g1_s, g1), (beta1_s, beta1)):
                sp.dma_start(b_s[:], b.to_broadcast([P, D])).then_inc(s_aw, 16)

            def pair_operands(p, which=(0, 1)):
                own = slice(p * DH, (p + 1) * DH)
                for a in which:
                    src = ((hi[0], hi[0], lo[0]), (hi[1], lo[1], hi[1]))[a]
                    for r in sorted(range(3), key=lambda r: src[r] is lo[a]):
                        if p == 0 and src[r] is lo[a]:
                            sp.wait_ge(s_lo, 2 * NC * (a + 1))
                        sp.dma_start(aug[a][r * DH:(r + 1) * DH, p % NA, :, :].bitcast(F32), src[r][own, :, :].bitcast(F32))\
                            .then_inc(s_aug[p % NA], 16)

            def maxima_rows(g):
                p, (a, b) = g // NC, UNIT_TILES[g % NC]
                sp.wait_ge(s_mc, g + 1)
                for h in range(2):
                    row = aug[0][KA:KA + 1, p % NA, h, :].bitcast(F32)
                    m = mT[h * (b - a):(h + 1) * (b - a), g % 2, :].bitcast(F32)
                    whole = min(b, T - 1) - a
                    sp.dma_start(row[:, a * P:(a + whole) * P].rearrange("a (t c) -> a t c", c=P), m[0:whole, :])\
                        .then_inc(s_mr[g % NC], 16)
                    if b == T:
                        sp.dma_start(row[:, (T - 1) * P:RW], m[whole:whole + 1, 0:RW - (T - 1) * P]).then_inc(s_mr[g % NC], 16)

            for a in range(2):
                sp.wait_ge(s_hi, 2 * NC * (a + 1))
                pair_operands(0, (a,))
            for p in range(1, NA):
                pair_operands(p)
            for g in range(UNITS):
                if g >= NC and g // NC + 2 < PAIRS and g % NC == 2:
                    p = g // NC + 2
                    sp.wait_ge(s_pv, NC * T * (p - NA + 1))
                    pair_operands(p)
                maxima_rows(g)

            sp.wait_ge(s_o, G)
            sp.dma_start(wg_s[:], wg.rearrange("(k p) e -> p k e", p=P)).then_inc(s_ew, 16)
            sp.dma_start(bg_s[:], bg.to_broadcast([P, E1])).then_inc(s_ew, 16)
            sp.dma_start(g2_s[:], g2.to_broadcast([P, D])).then_inc(s_ew, 16)
            sp.dma_start(beta2_s[:], beta2.to_broadcast([P, D])).then_inc(s_ew, 16)
            def by_tiles(move, q, sbuf, dram):
                own, whole = gathered(q), range(q * TG, min((q + 1) * TG, T - 1))
                move(sbuf[:, whole.start:whole.stop, :], dram[whole.start * P:whole.stop * P, :].rearrange("(t p) d -> p t d", p=P))
                if own.stop == T:
                    move(sbuf[0:LAST, T - 1, :], dram[(T - 1) * P:R, :])

            NG = len(s_ga2)
            for q in range(NG):
                sp.wait_ge(s_t, gathered(q).stop)
                by_tiles(lambda a, b: sp.dma_start(b, a).then_inc(s_td, 16), q, xn, t_d)

            def expert(n):
                e = sp.value_load(sloti[0:1, n:n + 1], min_val=0, max_val=E1 - 1)
                sp.dma_start(wexp[:, n % NW, :], blob[bass.ds(e, 1), :, :].rearrange("a p n -> (a p) n")).then_inc(s_w[n % NW], 16)

            sp.wait_ge(s_sl, 1)
            expert(0)
            sp.wait_ge(s_xg[0], 16)
            for n in range(1, NW):
                expert(n)
            for n in range(SLOTS - NW):
                sp.wait_ge(s_f2, n + 1)
                sp.wait_ge(s_v, 4 * n + 1)
                expert(n + NW)
            for q in range(2):
                sp.wait_ge(s_ys[q], 16 * (SLOTS // 2))
            sp.wait_ge(s_c4, 12)
            for q in range(NG):
                by_tiles(lambda a, b: sp.dma_start(a, b).then_inc(s_ga2[q], 16), q, moe, ys_d)
            for q in range(NG):
                sp.wait_ge(s_x4, gathered(q).stop)
                by_tiles(lambda a, b: sp.dma_start(b, a).then_inc(s_out, 16), q, xt, out)
            sp.wait_ge(s_out, 16 * (NG + 1))

        @block.gpsimd
        def _(pool):
            pool.memset(xt[:, T - 1, :], 0.0).then_inc(s_pad, 1)
            pool.memset(fT_hi[:, :, R:RW].bitcast(F32), 0.0).then_inc(s_pad, 1)
            pool.memset(adj[:, :, R:RW], 0.0).then_inc(s_pad, 1)
            pool.memset(fT_lo[:, :, R:RW].bitcast(F32), 0.0).then_inc(s_pad, 1)
            pool.memset(ht[:, T - 1, :], 0.0).then_inc(s_pad, 1)
            pool.memset(ss[:, :], 0.0).then_inc(s_pad, 1)
            pool.memset(ones2[:], 1.0).then_inc(s_pad, 1)
            pool.memset(eps_s[:], LN_EPS).then_inc(s_pad, 1)
            pool.memset(lg[:, T - 1, :], 0.0).then_inc(s_init, 1)
            pool.memset(comb[:, :, E0:EX], 1.0).then_inc(s_init, 1)
            pool.memset(dg[:], 1.0).then_inc(s_init, 1)
            pool.iota(iota8[:], [[1, E0]], base=0, channel_multiplier=0, allow_small_or_imprecise_dtypes=True).then_inc(s_init, 1)
            pool.memset(ident[:], 0.0).then_inc(s_id, 1)
            pool.wait_ge(s_id, 1)
            pool.affine_select(out=ident[:], in_=ident[:], compare_op=ALU.not_equal, fill=1.0, base=0,
                               pattern=[[-1, P]], channel_multiplier=1).then_inc(s_id, 1)
            pool.wait_ge(s_wgnn, 32)
            pool.tensor_copy(w_gnn_hi[:], w_gnn_s[:]).then_inc(s_wgs, 1)
            pool.wait_ge(s_wgs, 1)
            pool.tensor_tensor(w_gnn_lo[:], w_gnn_s[:], w_gnn_hi[:].bitcast(F32), ALU.subtract).then_inc(s_wgs, 1)
            for t in range(T):
                ln0.wait_tile(pool, t)
                pool.tensor_tensor(xt[0:rows(t), t, :], xt[0:rows(t), t, :], b_gnn_s[0:rows(t), :], ALU.add).then_inc(s_xb, 1)
            def split_weights(n):
                full, upper, low = ((gate_s[:], gate_hi[:], gate_lo[:]), (w1_s[:], w1_hi, w1_lo[:]), (w2_s[:], w2_hi, w2_lo[:]))[n]
                if n == 0:
                    pool.wait_ge(s_w0, 16 * (EX + 8))
                    pool.wait_ge(turn_turned, th.groups + G)
                    pool.wait_ge(s_ss, T)
                pool.tensor_copy(upper, full).then_inc(s_ws, 1)
                pool.wait_ge(s_ws, 2 * n + 1)
                pool.tensor_tensor(low, full, upper.bitcast(F32), ALU.subtract).then_inc(s_ws, 1)

            SPLITS = {2: 0, 3: 1, 6: 2}
            for j in range(T - 1):
                if j in SPLITS:
                    split_weights(SPLITS[j])
                pool.wait_ge(s_e, NC * (j + 1))
                if j == 0:
                    pool.tensor_copy(esum[:], ee[:, 0, :]).then_inc(s_es, 1)
                else:
                    pool.wait_ge(s_es, j)
                    pool.tensor_tensor(esum[:], esum[:], ee[:, j % NE, :], ALU.add).then_inc(s_es, 1)
            pool.wait_ge(s_den, 1)
            pool.memset(combT[0:E0 + 1, :], 1.0).then_inc(s_init, 1)
            pool.wait_ge(s_e, NC * T)
            for t in range(T):
                a = adj[0:rows(t), t, cols(t)]
                pool.tensor_tensor(a, a, ident[0:rows(t), 0:rows(t)], ALU.add).then_inc(s_self, 1)

            pool.wait_ge(s_dg, T)
            for j in range(T):
                pool.wait_ge(s_ah, j + 1)
                pool.tensor_tensor(adj_r[0:rows(j), j, :], adj[0:rows(j), j, :], adj_hi[0:rows(j), j, :].bitcast(F32), ALU.subtract).then_inc(s_al, 1)

            pool.wait_ge(s_wa, 16 * 4)
            for n, (full, upper, low) in enumerate(((wq_s, wq_hi, wq_lo), (wk_s, wk_hi, wk_lo), (wv_s, wv_hi, wv_lo))):
                pool.tensor_copy(upper[:], full[:]).then_inc(s_was, 1)
                pool.wait_ge(s_was, 2 * n + 1)
                pool.tensor_tensor(low[:], full[:], upper[:].bitcast(F32), ALU.subtract).then_inc(s_was, 1)

            pool.wait_ge(s_p2, G)
            pool.wait_ge(s_x3, T)
            pool.memset(ones32[:], 1.0).then_inc(s_c3, 1)
            pool.wait_ge(s_c3, 1)
            pool.memset(aug[1][KA:KA + 1, :, :, :].bitcast(F32), 1.0).then_inc(s_c3, 1)
            pool.wait_ge(s_c3, 2)
            pool.memset(mxp[:], 0.0).then_inc(s_c3, 1)
            pool.wait_ge(s_aw, 16 * 6)
            for t in range(T):
                ln3.wait_tile(pool, t)
                pool.tensor_tensor(ht[:, t, :], xn[:, t, :], bo_s[:], ALU.add).then_inc(s_xo, 1)
            for t in range(T):
                pool.wait_ge(s_vc, t // 2 + 1)
                pool.tensor_tensor(va[0:rows(t), t, :], va[0:rows(t), t, :], bv_s[0:rows(t), :], ALU.add).then_inc(s_vb, 1)

            pool.memset(valid[:], 1.0).then_inc(s_c4, 1)
            pool.memset(before[:], 1.0).then_inc(s_c4, 1)
            pool.memset(onesb[:], 1.0).then_inc(s_c4, 1)
            pool.memset(lower[:], 1.0).then_inc(s_c4, 1)
            pool.iota(starts[:], [[P, SLOTS]], base=0, channel_multiplier=0, allow_small_or_imprecise_dtypes=True).then_inc(s_c4, 1)
            pool.iota(token[:], [[P, T]], base=0, channel_multiplier=1, allow_small_or_imprecise_dtypes=True).then_inc(s_c4, 1)
            pool.iota(spare[:], [[P, SLOTS]], base=R, channel_multiplier=1, allow_small_or_imprecise_dtypes=True).then_inc(s_c4, 1)
            pool.iota(iota[:], [[1, P]], base=0, channel_multiplier=0, allow_small_or_imprecise_dtypes=True).then_inc(s_c4, 1)
            pool.wait_ge(s_c4, 8)
            pool.affine_select(out=valid[:], in_=valid[:], compare_op=ALU.is_ge, fill=0.0, base=R - 1, pattern=[[-P, T]],
                               channel_multiplier=-1).then_inc(s_c4, 1)
            pool.affine_select(out=before[:], in_=before[:], compare_op=ALU.is_ge, fill=0.0, base=-1, pattern=[[1, P]],
                               channel_multiplier=-1).then_inc(s_c4, 1)
            pool.affine_select(out=lower[:], in_=lower[:], compare_op=ALU.is_ge, fill=0.0, base=-1, pattern=[[1, E1], [-1, E1]],
                               channel_multiplier=0).then_inc(s_c4, 1)
            for m in range(STEPS // T - 1):
                p, c = m // NC, m % NC
                pool.wait_ge(s_ac, m + 1)
                for h in range(2):
                    o = (2 + h) * DH
                    pool.dma_start(spread[:, h, :], acc[o:o + 1, m % 2, :].rearrange("a (p w) -> a p w", w=SW)).then_inc(s_sp, 16)
                pool.wait_ge(s_si, m + 1)
                pool.dma_start(inv_d[m].rearrange("h (p w) -> p h w", w=SW), spread_inv[:]).then_inc(s_sd2, 16)
                pool.wait_ge(s_sd2, 16 * (m + 1))
                if m:
                    pool.wait_ge(s_cx, m)
                for h in range(2):
                    pool.dma_start(rec[h * DH:(h + 1) * DH, :], inv_d[m, h:h + 1, :].to_broadcast([DH, CW])).then_inc(s_rb, 16)
                pool.wait_ge(s_rb, 32 * (m + 1))
                o = p % 2 * 2 * DH
                pool.tensor_tensor(cT[o:o + 2 * DH, p // 2, chunk(c)], acc[0:2 * DH, m % 2, :], rec[:], ALU.mult).then_inc(s_cx, 1)

            pool.wait_ge(s_ew, 64)
            for t in range(T):
                pool.tensor_tensor(xt[0:rows(t), t, :], xt[0:rows(t), t, :], beta2_s[0:rows(t), :], ALU.add).then_inc(s_xb2, 1)

            def gather(n):
                pool.indirect_dma_start(xg[:, n % NX, :], None, t_d, bass.IndirectOffsetOnAxis(ap=src_row[:, n:n + 1], axis=0))\
                    .then_inc(s_xg[n % NX], 16)

            pool.wait_ge(s_td, 16 * (len(s_ga2) + 1))
            pool.wait_ge(s_src, 1)
            for n in range(NX):
                gather(n)
            pool.memset(moe[:, T - 1, D:D + 2], 0.0).then_inc(s_c4, 1)
            pool.wait_ge(s_dst, 1)
            for n in range(SLOTS):
                pool.wait_ge(s_y, n + 1)
                if n + NX < SLOTS:
                    gather(n + NX)
                pool.indirect_dma_start(ys_d, bass.IndirectOffsetOnAxis(ap=dst_row[:, n:n + 1], axis=0), yg[:, n % 2, :], None)\
                    .then_inc(s_ys[n % 2], 16)

        HB = (4, 5, 6, 7)
        SIMB = (6, 7)

        @block.tensor
        def _(pe):
            pe.wait_ge(s_id, 2)
            turn_pe(pe, tx, xn, ln_done, (0, 1, 2, 3), ln0.tiles)
            pe.wait_ge(s_wgs, 2)
            for g in range(G):
                tx.wait_group(pe, g)
                if g >= len(HB):
                    pe.wait_ge(s_ss, 2 * (g - len(HB) + 1))
                for t in group(g):
                    m = token_product(pe, HB[g % len(HB)], t, (xT_r, fT_lo), (w_gnn_hi, w_gnn_lo))
                m.then_inc(s_h, 1)
            turn_pe(pe, th, hn, s_hn, (0, 1, 2, 3))

            def sim(j):
                for c in range(NC):
                    n = NC * j + c
                    if n >= 2:
                        pe.wait_ge(s_exp, n - 1)
                    else:
                        pe.wait_ge(s_ss, T)
                    for k in range(H2):
                        m = product3(pe, ps[0:rows(j), SIMB[n % 2], 0:CW], [f[:, k, cols(j)] for f in (fT_hi, fT_lo)],
                                     [f[:, k, chunk(c)] for f in (fT_hi, fT_lo)], k == 0, k == H2 - 1)
                    m.then_inc(s_sim, 1)

            def denominators():
                pe.wait_ge(s_es, T)
                pe.wait_ge(s_exp, NC * T)
                for i in range(T):
                    m = pe.matmul(ps[0:rows(i), SIMB[0], 2 * i:2 * i + 2], esum[:, cols(i)], ones2[:], start=(i == 0), stop=(i == T - 1),
                                  skip_group_check=True)
                m.then_inc(s_den, 1)

            th.wait_group(pe, G - 1)
            pe.wait_ge(s_pad, 8)
            sim(0)
            for j in range(T):
                if j + 1 < T:
                    sim(j + 1)
                else:
                    denominators()
                pe.wait_ge(s_el, j + 1)
                if j == 0:
                    pe.wait_ge(s_hl, 1)
                for i in range(T):
                    m = product3(pe, half(i // 2, i)[0:rows(i), :], [e[0:rows(j), j % NE, cols(i)] for e in (ee_hi, ex_r)],
                                 [h[0:rows(j), j, :] for h in (xn_r, ht_r)], j == 0 and i % 2 == 0, j == T - 1, True)
                    if j == T - 1 and (i % 2 or i == T - 1):
                        m.then_inc(s_agg, 1)
                if j < T - 1:
                    m.then_inc(s_agg, 1)

            turn_pe(pe, tx1, xn, ln_done, (0, 1, 2, 3), ln1.tiles)
            tx1.wait_group(pe, G - 1)
            pe.wait_ge(s_w0, 16 * (EX + 8))
            pe.wait_ge(s_ws, 2)
            for t in range(T):
                for k in range(H2):
                    m = product3(pe, ps[0:rows(t), 4, E0 * t:E0 * (t + 1)], [f[:, k, cols(t)] for f in (fT_hi, fT_lo)],
                                 [g[:, k, :] for g in (gate_hi, gate_lo)], k == 0, k == H2 - 1)
            m.then_inc(s_lg, 1)

            def up(e):
                for c in range(NC):
                    if e:
                        pe.wait_ge(s_hr, NC * (e - 1) + c + 1)
                    else:
                        pe.wait_ge(s_ws, 4)
                    for k in range(H2):
                        m = product3(pe, ps[:, c, 0:CW], [w[:, e, k, :] for w in (w1_hi, w1_lo)],
                                     [f[:, k, chunk(c)] for f in (fT_hi, fT_lo)], k == 0, k == H2 - 1)
                    m.then_inc(s_up, 1)

            def down(e):
                pe.wait_ge(s_hd, e + 1)
                if e == 0:
                    pe.wait_ge(s_ws, 6)
                for g in range(G):
                    n = G * e + g
                    if n >= 4:
                        pe.wait_ge(s_x2, T * ((n - 4) // G) + min(2 * ((n - 4) % G) + 2, T))
                    else:
                        pe.wait_ge(s_r, 1)
                    for t in group(g):
                        m = product3(pe, half(4 + n % 4, t)[0:rows(t), :], [h[:, e % 2, cols(t)] for h in (ee_hi, ex_r)],
                                     [w[:, e, :] for w in (w2_hi, w2_lo)], True, e < EX - 1)
                        if e == EX - 1:
                            m = pe.matmul(half(4 + n % 4, t)[0:rows(t), :], combT[0:E0 + 1, cols(t)], b2_s[:], start=False, stop=True)
                    m.then_inc(s_dn, 1)

            up(0)
            def turn_combine(r):
                if r:
                    pe.wait_ge(s_cc, r)
                else:
                    pe.wait_ge(s_comb, 1)
                for t in range(4 * r, min(4 * r + 4, T)):
                    m = pe.transpose(ps[0:E0, 3, t % 4 * P:t % 4 * P + rows(t)], comb[0:rows(t), t, 0:E0], ident[0:rows(t), 0:rows(t)])
                m.then_inc(s_ct, 1)

            for e in range(EX - 1):
                up(e + 1)
                if 1 <= e <= CR:
                    turn_combine(e - 1)
                down(e)
            pe.wait_ge(s_cc, CR)
            down(EX - 1)

            pe.wait_ge(s_x2, T * (EX - 1) + 8)
            for j in range(T):
                pe.wait_ge(s_xl, j + 1)
                pe.wait_ge(s_al, j + 1)
                for k in range(H2):
                    for c in range(NC):
                        m = product3(pe, ps[:, NC * k + c, 0:CW], [x[0:rows(j), j, k * P:(k + 1) * P] for x in (ht_r, xn_r)],
                                     [a[0:rows(j), j, chunk(c)] for a in (adj_hi, adj_r)], j == 0, j == T - 1)
            m.then_inc(s_g, 1)

            def both_copied(eng, g):
                eng.wait_ge(s_ga, 1)
                eng.wait_ge(s_gv, 1)
            project(pe, gT, both_copied, w_gnn1_s, s_t1, (6, 7), s_ts)
            for j in range(T):
                pe.wait_ge(s_tl, 2 * (j + 1))
                for i in range(T):
                    m = product3(pe, half(i // 2, i)[0:rows(i), :], [a[0:rows(j), j, cols(i)] for a in (adj_hi, adj_r)],
                                 [x[0:rows(j), j, :] for x in (xn_r, ht_r)], j == 0 and i % 2 == 0, j == T - 1, True)
                    if j == T - 1 and (i % 2 or i == T - 1):
                        m.then_inc(s_p2, 1)

            def project_qk(u, c):
                w, k2 = ((wq_hi, wq_lo), (wk_hi, wk_lo))[u // 2], u % 2
                if u >= 2:
                    pe.wait_ge(s_lo, NC * (u - 2) + c + 1)
                for k in range(H2):
                    m = product3(pe, ps[:, 3 * (u % 2) + c, 0:CW], [f[:, k, k2 * P:(k2 + 1) * P] for f in w],
                                 [f[:, k, chunk(c)] for f in (xT_r, xT_lo)], k == 0, k == H2 - 1)
                m.then_inc(s_pr, 1)

            turn_pe(pe, tx3, xn, ln_done, (6, 7), ln3.tiles)
            pe.wait_ge(s_was, 6)
            pe.wait_ge(s_rl, T)
            pe.wait_ge(s_aw, 16 * 6)
            for u, c in [(u, c) for u in range(4) for c in range(NC)]:
                tx3.wait_group(pe, chunk_group(c))
                if c == NC - 1:
                    pe.wait_ge(s_dup, 2)
                project_qk(u, c)

            def project_v(g):
                if g == 0:
                    pe.wait_ge(s_lo, 4 * NC)
                if g >= 2:
                    pe.wait_ge(s_vc, g - 1)
                for t in group(g):
                    m = token_product(pe, 4 * (g % 2), t, (xT_r, xT_lo), (wv_hi, wv_lo))
                m.then_inc(s_vp, 1)

            def rows2(i):
                return slice(i * P, min((i + 1) * P, RW))

            def max_scores(g, h, i, part):
                k = MAX_STEPS.index((g, h, i, part))
                if h is None:
                    pe.wait_ge(s_neg, g + 1)
                    if g:
                        last = [m for m in MAX_STEPS[:k] if m[3] == 0][-1]
                        pe.wait_ge(s_mx, MAX_PLACE[last] + 1)
                    w = 2 * (UNIT_TILES[g % NC][1] - UNIT_TILES[g % NC][0])
                    pe.transpose(ps[0:w, 5, 0:P], nm[:, g % 2, 0:w], ident[:]).then_inc(s_mt, 1)
                    return
                p, place, b = g // NC, MAX_PLACE[(g, h, i, part)], max_set(g, i, h)
                if g % NC == 0 and place == MAX_PLACE[unit_scores(g)[0]]:
                    pe.wait_ge(s_aug[p % NA], 16 * 6 * (p // NA + 1))
                    if p == 0:
                        pe.wait_ge(s_lo, 4 * NC)
                if g == 0:
                    if place >= 4 and part == 0:
                        pe.wait_ge(s_mx, place - 2)
                else:
                    pe.wait_ge(s_mx, place - 1)
                    turned = [m for m in MAX_STEPS[:k] if m[1] is None]
                    if part == 0:
                        pe.wait_ge(s_mc, len(turned))
                w = rows2(i)
                for c in ((0, 1), (2,))[part]:
                    m = pe.matmul(ps[0:w.stop - w.start, b + c, 0:CW], aug[0][0:KA, p % NA, h, w], aug[1][0:KA, p % NA, h, chunk(c)],
                                  start=True, stop=True)
                m.then_inc(s_s1, 1)

            def scores(n):
                p, c, k = n // (NC * T), n // T % NC, n % T
                if n % T == 0:
                    pe.wait_ge(s_mr[c], rows_loaded(n // T))
                    pe.wait_ge(s_c3, 3)
                    if n == 0:
                        pe.wait_ge(s_vc, G)
                if n >= 2:
                    pe.wait_ge(s_p, n - 1)
                for h in range(2):
                    m = pe.matmul(ps[0:rows(k), 1 + 2 * (n % 2) + h, 0:CW], aug[1][:, p % NA, h, cols(k)], aug[0][:, p % NA, h, chunk(c)],
                                  start=True, stop=True)
                m.then_inc(s_s2, 1)

            def values(n):
                p, k = n // (NC * T), n % T
                if n == 0:
                    pe.wait_ge(s_vb, T)
                pe.wait_ge(s_p, n + 1)
                if k == 0 and n:
                    pe.wait_ge(s_ac, n // T)
                for a in range(4):
                    w = va[0:rows(k), k, (2 * p + a) * DH:(2 * p + a + 1) * DH] if a < 2 else ones32[0:rows(k), :]
                    m = pe.matmul(ps[DH * a:DH * (a + 1), 0, 0:CW], w, pt[0:rows(k), n % NPT, a % 2, :],
                                  start=(k == 0), stop=(k == T - 1))
                m.then_inc(s_pv, 1)

            project_v(0)
            project_v(1)
            for k, step in enumerate(MAX_STEPS[0:AHEAD]):
                max_scores(*step)
                if k % 4 == 1 and 2 + k // 4 < G:
                    project_v(2 + k // 4)
            scores(0)
            for n in range(STEPS):
                if n + 1 < STEPS:
                    scores(n + 1)
                for item in max_items(2 * n):
                    max_scores(*item)
                values(n)
                for item in max_items(2 * n + 1):
                    max_scores(*item)

            def heads_ready(eng, g):
                eng.wait_ge(s_cx, NC * (PAIRS - 1) + (min((2 * g + 2) * P, R) - 1) // CW + 1)
            project(pe, cT, heads_ready, wo_s, s_o, (1, 2, 3, 4, 5, 6), s_u)

            def gate(g):
                for c in range(NC):
                    if chunk_group(c) == g:
                        tx4.wait_group(pe, g)
                        for k in range(H2):
                            m = pe.matmul(ps[0:E1, 4 + c, 0:CW], wg_s[:, k, :], xT[:, k, chunk(c)], start=(k == 0), stop=(k == H2 - 1))
                        m.then_inc(s_lc, 1)

            pe.wait_ge(s_ew, 64)
            pe.wait_ge(s_u, T)
            turn_pe(pe, tx4, xn, s_t, (0, 1, 2, 3), after=lambda g: gate(g - 1) if g else None)
            gate(G - 1)
            for t in range(T):
                pe.wait_ge(s_lt, chunk_of(t) + 1)
                m = pe.transpose(ps[0:rows(t), 7, E1 * t:E1 * (t + 1)], lgT[:, cols(t)], ident[0:E1, 0:E1])
            m.then_inc(s_l1, 1)
            pe.wait_ge(s_oh, 1)
            pe.wait_ge(s_c4, 11)
            for t in range(T + 1):
                o = ps[:, 5, E1 * t:E1 * (t + 1)]
                for j in range(t):
                    m = pe.matmul(o, onesb[:], ohb[:, j, :], start=(j == 0), stop=(t == T and j == T - 1))
                if t < T:
                    m = pe.matmul(o, before[:], ohb[:, t, :], start=(t == 0), stop=True)
            m.then_inc(s_rank, 1)

            for t in range(T):
                pe.wait_ge(s_sel, t // TG + 2)
                m = pe.matmul(ps[:, 6, 0:2 * SLOTS], in_row[0:rows(t), t, :], in_slot[0:rows(t), t, :], start=(t == 0), stop=(t == T - 1))
            m.then_inc(s_inv, 1)

            def slot_turn(n):
                pe.wait_ge(s_xg[n % NX], 16 * (n // NX + 1))
                if n >= 2:
                    pe.wait_ge(s_gc, n - 1)
                for k in range(H2):
                    m = pe.transpose(ps[:, n % 2, k * P:(k + 1) * P], xg[:, n % NX, k * P:(k + 1) * P], ident[:])
                m.then_inc(s_gt, 1)

            def slot_up(n):
                pe.wait_ge(s_w[n % NW], 16 * (n // NW + 1))
                pe.wait_ge(s_gc, n + 1)
                w = wexp[:, n % NW, 0:H2 * HID].rearrange("p (k f) -> p k f", k=H2)
                for b in range(2):
                    if n >= 2:
                        pe.wait_ge(s_fg, FC * (n - 2) + FC // 2 * (b + 1))
                    for f in range(FC // 2):
                        for k in range(H2):
                            fc = b * FC // 2 + f
                            m = pe.matmul(ps[:, 2 + 2 * (n % 2) + b, f * P:(f + 1) * P], w[:, k, fc * P:(fc + 1) * P],
                                          xgT[:, n % 2, k, :], start=(k == 0), stop=(k == H2 - 1))
                    m.then_inc(s_f1, 1)

            def slot_down(n):
                if n >= 2:
                    pe.wait_ge(s_y, n - 1)
                w = wexp[:, n % NW, H2 * HID:2 * H2 * HID].rearrange("p (c d) -> p c d", c=FC)
                for f in range(FC):
                    pe.wait_ge(s_fg, FC * n + f + 1)
                    m = pe.matmul(ps[:, 6 + n % 2, 0:D], hid[:, n % 2, f, :], w[:, f, :], start=(f == 0), stop=(f == FC - 1))
                m.then_inc(s_f2, 1)

            slot_turn(0)
            slot_turn(1)
            slot_up(0)
            for n in range(SLOTS):
                if n + 2 < SLOTS:
                    slot_turn(n + 2)
                if n + 1 < SLOTS:
                    slot_up(n + 1)
                slot_down(n)

        @block.scalar
        def _(act):
            act.wait_ge(s_pad, 8)
            preload(act, 0, ACT.Sqrt)
            ln_std(act, ln0)
            split_copy(act, tx, xT_r, None, (0, 1, 2, 3))
            for g in range(G):
                act.wait_ge(s_h, g + 1)
                bank = ps[:, HB[g % 4], :]
                act.activation(ht[0:rows(2 * g), 2 * g:2 * g + len(group(g)), :], gshape(bank, g), ACT.Copy).then_inc(s_hc, 1)
                for t in group(g):
                    if t:
                        act.wait_ge(s_ss, t)
                    act.activation(sq[0:rows(t), :], half(HB[g % 4], t)[0:rows(t), :], ACT.Square,
                                   accum_out=ss[0:rows(t), t:t + 1]).then_inc(s_ss, 1)
            act.wait_ge(s_ss, T)
            act.activation(norm[:], ss[:], ACT.Sqrt).then_inc(s_nm, 1)
            split_copy(act, th, fT_hi, None, (0, 1, 2, 3))
            for j in range(T):
                for c in range(NC):
                    n = NC * j + c
                    act.wait_ge(s_sim, n + 1)
                    if j >= NE and c == 0:
                        act.wait_ge(s_agg, j - NE + 1)
                    act.activation(ex[0:rows(j), j % NE, chunk(c)], ps[0:rows(j), SIMB[n % 2], 0:CW], ACT.Exp)\
                        .then_inc(s_exp, 1)
                act.wait_ge(s_e, NC * (j + 1))
                act.activation(ee_hi[0:rows(j), j % NE, :], ee[0:rows(j), j % NE, :], ACT.Copy).then_inc(s_eh, 1)

            preload(act, 1, ACT.Sqrt)
            ln_std(act, ln1)
            preload(act, 2, ACT.Exp)
            split_copy(act, tx1, fT_hi, None, (0, 1, 2, 3))
            act.wait_ge(s_r, 3)
            act.activation(lg[:], lg[:], ACT.Exp).then_inc(s_er, 1)
            for e in range(EX):
                for c in range(NC):
                    act.wait_ge(s_up, NC * e + c + 1)
                    if e >= 2 and c == 0:
                        act.wait_ge(s_dn, G * (e - 1))
                    act.activation(ee[:, e % 2, chunk(c)], ps[:, c, 0:CW], ACT.Relu, bias=b1_s[:, e:e + 1])
                    act.activation(ee_hi[:, e % 2, chunk(c)], ps[:, c, 0:CW], ACT.Relu, bias=b1_s[:, e:e + 1]).then_inc(s_hr, 1)
                if 2 <= e <= CR + 1:
                    r = e - 2
                    n = min(4 * P, R - 4 * P * r)
                    act.wait_ge(s_init, 5)
                    act.wait_ge(s_ct, r + 1)
                    act.activation(combT[0:E0, 4 * P * r:4 * P * r + n], ps[0:E0, 3, 0:n], ACT.Copy).then_inc(s_cc, 1)

            def upper_graph(j):
                act.activation(adj_hi[0:rows(j), j, :], adj[0:rows(j), j, :], ACT.Copy).then_inc(s_ah, 1)

            AH = 5
            preload(act, 3, ACT.Sqrt)
            act.wait_ge(s_dg, T)
            act.wait_ge(s_up, NC * EX)
            for j in range(AH):
                upper_graph(j)
            act.activation(dgs[:], dg[:], ACT.Sqrt).then_inc(s_dgs, 1)
            ln_std(act, ln2, (0,))
            for t in range(T):
                if t == CUT:
                    ln_std(act, ln2, (1,))
                    act.wait_ge(s_dn, G * EX)
                ln2.wait_tile(act, t)
                act.activation(ht_r[:, t, :], xn[:, t, :], ACT.Copy).then_inc(s_xh, 1)
                if t >= CUT and AH + t - CUT < T:
                    upper_graph(AH + t - CUT)
            act.wait_ge(s_g, 1)
            act.activation(gT[:, 0, :].rearrange("p (c w) -> p c w", c=NC), ps[:, 0:NC, 0:CW], ACT.Copy).then_inc(s_ga, 1)
            act.wait_ge(s_ds, 1)
            for t in range(T):
                act.wait_ge(s_t1, t // 2 + 1)
                act.activation(ht[0:rows(t), t, :], half(6 + t // 2 % 2, t)[0:rows(t), :], ACT.Copy,
                               scale=dscale[0:rows(t), t:t + 1]).then_inc(s_ts, 1)
            for t in range(T):
                act.wait_ge(s_p2, t // 2 + 1)
                act.activation(gy[0:rows(t), t, :], half(t // 2, t)[0:rows(t), :], ACT.Relu,
                               scale=dscale[0:rows(t), t:t + 1]).then_inc(s_rl, 1)

            ln_std(act, ln3)
            split_copy(act, tx3, xT_r, None, (6, 7))
            for u in range(4):
                for c in range(NC):
                    act.wait_ge(s_pr, NC * u + c + 1)
                    act.activation(hi[u // 2][:, u % 2, chunk(c)], ps[:, 3 * (u % 2) + c, 0:CW], ACT.Identity,
                                   bias=(bq_s, bk_s)[u // 2][:, u % 2:u % 2 + 1]).then_inc(s_hi, 1)
            for g in range(G):
                act.wait_ge(s_vp, g + 1)
                act.activation(va[0:rows(2 * g), 2 * g:2 * g + len(group(g)), :], gshape(ps[:, 4 * (g % 2), :], g), ACT.Copy).then_inc(s_vc, 1)
            for n in range(STEPS + 1):
                if n < STEPS:
                    act.wait_ge(s_s2, n + 1)
                    if n >= NPT:
                        act.wait_ge(s_pv, n - NPT + 1)
                    k = n % T
                    b = 1 + 2 * (n % 2)
                    act.activation(pt[0:rows(k), n % NPT, :, :], ps[0:rows(k), b:b + 2, 0:CW], ACT.Exp, scale=DH ** -0.5).then_inc(s_p, 1)
                if n and n % T == 0:
                    m = n // T - 1
                    act.wait_ge(s_pv, n)
                    if m >= 2:
                        act.wait_ge(s_cx, m - 1)
                    act.activation(acc[:, m % 2, :], ps[:, 0, 0:CW], ACT.Copy).then_inc(s_ac, 1)
            preload(act, 4, ACT.Sqrt)
            ln_std(act, ln4)

            turn_copy(act, tx4, xT, (0, 1, 2, 3))
            for c in range(NC):
                act.wait_ge(s_lc, c + 1)
                act.activation(lgT[:, chunk(c)], ps[0:E1, 4 + c, 0:CW], ACT.Copy).then_inc(s_lt, 1)
            for n in range(SLOTS):
                bias = wexp[:, n % NW, 2 * H2 * HID:2 * H2 * HID + FC]
                for f in range(FC):
                    if f % (FC // 2) == 0:
                        act.wait_ge(s_f1, 2 * n + f // (FC // 2) + 1)
                        if n >= 2:
                            act.wait_ge(s_f2, n - 1)
                    act.activation(hid[:, n % 2, f, :], ps[:, 2 + 2 * (n % 2) + f // (FC // 2), f % (FC // 2) * P:(f % (FC // 2) + 1) * P],
                                   ACT.Gelu, bias=bias[:, f:f + 1]).then_inc(s_fg, 1)
            for q in range(len(s_ga2)):
                own = gathered(q)
                act.wait_ge(s_ga2[q], 32 if own.stop == T else 16)
                act.activation(std[:, own.start:own.stop], moe[:, own.start:own.stop, D + 1], ACT.Sqrt, bias=eps_s[:]).then_inc(s_sd, 1)

        @block.vector
        def _(v):
            ln_steps(v, ln0, xt, xn, arrived=lambda t: v.wait_ge(s_x[t >= CUT], 16 * (1 + (t >= CUT))))
            split_copy(v, tx, xT_r, fT_lo, (0, 1, 2, 3))
            for g in range(G):
                own = slice(2 * g, 2 * g + len(group(g)))
                v.wait_ge(s_hc, g + 1)
                v.tensor_copy(xn_r[:, own, :], ht[:, own, :]).then_inc(s_hh, 1)
            v.wait_ge(s_nm, 1)
            v.tensor_scalar(norm[:], norm[:], NORM_EPS, None, ALU.max).then_inc(s_rn, 1)
            v.wait_ge(s_rn, 1)
            v.reciprocal(rnorm[:], norm[:]).then_inc(s_rn, 1)
            v.wait_ge(s_rn, 2)
            for t in range(T):
                v.tensor_scalar(hn[:, t, :], ht[:, t, :], rnorm[:, t:t + 1], None, ALU.mult).then_inc(s_hn, 1)
            split_copy(v, th, fT_hi, fT_lo, (0, 1, 2, 3))
            v.wait_ge(s_hh, G)
            v.tensor_tensor(ht_r[:], ht[:], xn_r[:].bitcast(F32), ALU.subtract).then_inc(s_hl, 1)
            for j in range(T):
                if j < 3:
                    v.wait_ge(s_adj[j >= 2], 16 * (T - 2) if j >= 2 else 32)
                if j >= NE:
                    v.wait_ge(s_agg, j - NE + 1)
                    v.wait_ge(s_es, j - NE + 1)
                for c in range(NC):
                    v.wait_ge(s_exp, NC * j + c + 1)
                    v.scalar_tensor_tensor(out=ee[0:rows(j), j % NE, chunk(c)], in0=adj[0:rows(j), j, chunk(c)], scalar=NORM_EPS,
                                           in1=ex[0:rows(j), j % NE, chunk(c)], op0=ALU.add, op1=ALU.mult).then_inc(s_e, 1)
                if j == T - 1:
                    v.wait_ge(s_e, NC * T)
                    v.wait_ge(s_es, j)
                    v.tensor_tensor(esum[0:LAST, :], esum[0:LAST, :], ee[0:LAST, j % NE, :], ALU.add).then_inc(s_es, 1)
                v.wait_ge(s_eh, j + 1)
                v.tensor_tensor(ex_r[0:rows(j), j % NE, :], ee[0:rows(j), j % NE, :], ee_hi[0:rows(j), j % NE, :].bitcast(F32),
                                ALU.subtract).then_inc(s_el, 1)
            v.wait_ge(s_den, 1)
            d = ps[:, SIMB[0], 0:2 * T].rearrange("p (t a) -> p t a", a=2)
            v.reciprocal(rden[:, 0:T - 1], d[:, 0:T - 1, 0]).then_inc(s_rd, 1)
            v.reciprocal(rden[0:LAST, T - 1:T], d[0:LAST, T - 1, 0:1]).then_inc(s_rd, 1)
            v.wait_ge(s_rd, 2)
            v.wait_ge(s_xb, T)
            def add_graph(t):
                v.wait_ge(s_agg, T + t // 2)
                v.scalar_tensor_tensor(out=xt[0:rows(t), t, :], in0=half(t // 2, t)[0:rows(t), :], scalar=rden[0:rows(t), t:t + 1],
                                       in1=xt[0:rows(t), t, :], op0=ALU.mult, op1=ALU.add).then_inc(s_x1, 1)

            ln_steps(v, ln1, xt, xn, add_graph, lambda t: v.wait_ge(s_x1, t + 1))
            split_copy(v, tx1, fT_hi, fT_lo, (0, 1, 2, 3))
            route(v)

            def hidden_low(e):
                v.wait_ge(s_hr, NC * (e + 1))
                v.tensor_tensor(ex_r[:, e % 2, :], ee[:, e % 2, :], ee_hi[:, e % 2, :].bitcast(F32), ALU.subtract).then_inc(s_hd, 1)

            def add_expert(e, t):
                g = t // 2
                v.wait_ge(s_dn, G * e + g + 1)
                if e:
                    v.wait_ge(s_x2, T * (e - 1) + t + 1)
                v.scalar_tensor_tensor(out=xt[0:rows(t), t, :], in0=half(4 + (G * e + g) % 4, t)[0:rows(t), :],
                                       scalar=comb[0:rows(t), t, e:e + 1], in1=xt[0:rows(t), t, :],
                                       op0=ALU.mult, op1=ALU.add).then_inc(s_x2, 1)

            hidden_low(0)
            for e in range(EX):
                if e == EX // 2:
                    v.wait_ge(s_self, T)
                    for t in range(T):
                        if t:
                            v.wait_ge(s_dg, t)
                        v.tensor_tensor_reduce(sq[0:rows(t), 0:rows(t)], adj[0:rows(t), t, cols(t)], ident[0:rows(t), 0:rows(t)],
                                               1.0, 0.0, ALU.mult, ALU.add, dg[0:rows(t), t:t + 1]).then_inc(s_dg, 1)
                if e < EX - 1:
                    for t in range(T):
                        add_expert(e, t)
                    hidden_low(e + 1)

            def x2_low(t):
                if t:
                    v.wait_ge(s_xh, t)
                    v.tensor_tensor(xn_r[:, t - 1, :], xn[:, t - 1, :], ht_r[:, t - 1, :].bitcast(F32), ALU.subtract).then_inc(s_xl, 1)

            ln_steps(v, ln2, xt, xn, lambda t: add_expert(EX - 1, t), lambda t: v.wait_ge(s_x2, T * (EX - 1) + t + 1), x2_low, 7)
            x2_low(T)
            v.wait_ge(s_dgs, 1)
            v.reciprocal(dscale[:], dgs[:]).then_inc(s_ds, 1)
            v.wait_ge(s_g, 1)
            v.tensor_copy(gT[:, 1, :].rearrange("p (c w) -> p c w", c=NC), ps[:, NC:2 * NC, 0:CW]).then_inc(s_gv, 1)
            for t in range(T):
                v.wait_ge(s_ts, t + 1)
                v.tensor_copy(xn_r[0:rows(t), t, :], ht[0:rows(t), t, :]).then_inc(s_tl, 1)
                v.wait_ge(s_tl, 2 * t + 1)
                v.tensor_tensor(ht_r[0:rows(t), t, :], ht[0:rows(t), t, :], xn_r[0:rows(t), t, :].bitcast(F32), ALU.subtract).then_inc(s_tl, 1)
            def add_second(t):
                v.wait_ge(s_rl, t + 1)
                v.tensor_tensor(xt[0:rows(t), t, :], xt[0:rows(t), t, :], gy[0:rows(t), t, :], ALU.add).then_inc(s_x3, 1)


            ln_steps(v, ln3, xt, xn, add_second, lambda t: v.wait_ge(s_x3, t + 1))
            split_copy(v, tx3, xT_r, xT_lo, (6, 7))
            v.wait_ge(split_lo, (tx3.m + 1) * G)
            for part in (xT_r, xT_lo):
                v.tensor_copy(part[:, :, R:RW], part[:, :, R - 1:R].bitcast(F32).to_broadcast([P, H2, RW - R])).then_inc(s_dup, 1)
            for u in range(4):
                for c in range(NC):
                    v.wait_ge(s_hi, NC * u + c + 1)
                    v.scalar_tensor_tensor(out=lo[u // 2][:, u % 2, chunk(c)], in0=ps[:, 3 * (u % 2) + c, 0:CW],
                                           scalar=(bq_s, bk_s)[u // 2][:, u % 2:u % 2 + 1], in1=hi[u // 2][:, u % 2, chunk(c)].bitcast(F32),
                                           op0=ALU.add, op1=ALU.subtract).then_inc(s_lo, 1)

            def maxima(g, h, i, part):
                if h is None:
                    w = 2 * (UNIT_TILES[g % NC][1] - UNIT_TILES[g % NC][0])
                    v.wait_ge(s_mt, g + 1)
                    if g >= 2:
                        v.wait_ge(s_mr[(g - 2) % NC], rows_loaded(g - 2))
                    v.tensor_copy(mT[0:w, g % 2, :], ps[0:w, 5, 0:P]).then_inc(s_mc, 1)
                    return
                place, first, last = (MAX_PLACE[m] for m in ((g, h, i, part), unit_scores(g)[0], unit_scores(g)[-1]))
                w, b = min((i + 1) * P, RW) - i * P, max_set(g, i, h)
                own = mxp[0:w, g % 2, (place - first) // 2, :]
                if place == first:
                    v.wait_ge(s_c3, 3)
                    if g >= 2:
                        v.wait_ge(s_neg, g - 1)
                v.wait_ge(s_s1, place + 1)
                if g == 0:
                    if part == 1:
                        v.tensor_reduce(own[:, 0:1], ps[0:w, b:b + 3, 0:CW], AX.XY, ALU.max).then_inc(s_mx, 2)
                elif part == 0:
                    v.tensor_reduce(own[:, 0:1], ps[0:w, b:b + 2, 0:CW], AX.XY, ALU.max).then_inc(s_mx, 1)
                else:
                    v.tensor_reduce(own[:, 1:2], ps[0:w, b + 2, 0:CW], AX.X, ALU.max).then_inc(s_mx, 1)
                if place == last:
                    v.wait_ge(s_mx, last + 1)
                    if g >= 2:
                        v.wait_ge(s_mt, g - 1)
                    w = (last + 1 - first) // 2
                    v.tensor_reduce(nm[:, g % 2, 0:w], mxp[:, g % 2, 0:w, 0:(2 if g else 1)], AX.X, ALU.max, negate=True).then_inc(s_neg, 1)

            for step in MAX_STEPS[0:AHEAD]:
                maxima(*step)
            for n in range(STEPS):
                for q in (2 * n, 2 * n + 1):
                    for step in max_items(q):
                        maxima(*step)
                if n >= T and n % T == 6:
                    m = n // T - 1
                    v.wait_ge(s_sp, 32 * (m + 1))
                    if m:
                        v.wait_ge(s_sd2, 16 * m)
                    v.reciprocal(spread_inv[:], spread[:]).then_inc(s_si, 1)
            m = STEPS // T - 1
            o = (PAIRS - 1) % 2 * 2 * DH
            v.wait_ge(s_ac, m + 1)
            v.wait_ge(s_cx, m)
            v.reciprocal(rec[:], acc[2 * DH:4 * DH, m % 2, :]).then_inc(s_rc, 1)
            v.wait_ge(s_rc, 1)
            v.tensor_tensor(cT[o:o + 2 * DH, (PAIRS - 1) // 2, chunk(NC - 1)], acc[0:2 * DH, m % 2, :], rec[:], ALU.mult).then_inc(s_cx, 1)

            def add_attention(t):
                if t % 2 == 0:
                    v.wait_ge(s_o, t // 2 + 1)
                    v.wait_ge(s_xo, T)
                v.tensor_tensor(ht[0:rows(t), t, :], half(1 + t // 2, t)[0:rows(t), :], ht[0:rows(t), t, :], ALU.add).then_inc(s_u, 1)
            ln_steps(v, ln4, ht, xn, add_attention, lambda t: v.wait_ge(s_u, t + 1), gain=(g1_s, beta1_s, s_gain, s_t))

            v.wait_ge(s_l1, 1)
            v.wait_ge(s_ew, 64)
            d = ps[:, 7, 0:E1 * T].rearrange("p (t e) -> p t e", e=E1)
            v.tensor_tensor(lg[:, 0:T - 1, :], d[:, 0:T - 1, :], bg_s[:].unsqueeze(1).to_broadcast([P, T - 1, E1]), ALU.add).then_inc(s_k, 1)
            v.tensor_tensor(lg[0:LAST, T - 1, :], d[0:LAST, T - 1, :], bg_s[0:LAST, :], ALU.add).then_inc(s_k, 1)
            v.wait_ge(s_k, 2)
            for t in range(T):
                v.max(top[:, t, :], lg[:, t, :]).then_inc(s_k2, 1)
            for t in range(T):
                v.wait_ge(s_k2, t + 1)
                v.max_index(topi[:, t, :], top[:, t, :], lg[:, t, :]).then_inc(s_k2, 1)
            v.wait_ge(s_k2, 2 * T)
            v.tensor_copy(best[:], topi[:, :, 0]).then_inc(s_k, 1)
            v.wait_ge(s_k, 3)
            v.wait_ge(s_c4, 11)
            v.tensor_tensor(oh[:], iota8[:].unsqueeze(1).to_broadcast([P, T, E1]), best[:].unsqueeze(2).to_broadcast([P, T, E1]),
                            ALU.is_equal).then_inc(s_k, 1)
            v.wait_ge(s_k, 4)
            v.tensor_tensor(oh[:], oh[:], valid[:].unsqueeze(2).to_broadcast([P, T, E1]), ALU.mult).then_inc(s_k, 1)
            v.wait_ge(s_k, 5)
            v.tensor_copy(ohb[:], oh[:]).then_inc(s_oh, 1)
            v.wait_ge(s_rank, 1)
            v.tensor_copy(rank[:], ps[:, 5, 0:E1 * (T + 1)].rearrange("p (t e) -> p t e", e=E1)).then_inc(s_k, 1)
            v.wait_ge(s_k, 6)
            v.tensor_scalar(cnt[:], rank[:, T, :], float(P - 1), None, ALU.add).then_inc(s_k, 1)
            v.wait_ge(s_k, 7)
            v.tensor_scalar(cnt[:], cnt[:], 7, 7, ALU.arith_shift_right, ALU.logical_shift_left).then_inc(s_k, 1)
            v.wait_ge(s_k, 8)
            v.tensor_copy(padded[:], cnt[:]).then_inc(s_k, 1)
            v.wait_ge(s_k, 9)
            v.tensor_tensor(prod[:], lower[:], padded[:].unsqueeze(1).to_broadcast([P, E1, E1]), ALU.mult).then_inc(s_k, 1)
            v.wait_ge(s_k, 10)
            v.tensor_reduce(base[:], prod[:], AX.X, ALU.add).then_inc(s_k, 1)
            v.wait_ge(s_k, 11)
            v.tensor_tensor(ends[:], base[:], padded[:], ALU.add).then_inc(s_k, 1)
            v.wait_ge(s_k, 12)
            v.tensor_tensor(past[:], ends[:].unsqueeze(1).to_broadcast([P, SLOTS, E1]),
                            starts[:].unsqueeze(2).to_broadcast([P, SLOTS, E1]), ALU.is_le).then_inc(s_k, 1)
            v.wait_ge(s_k, 13)
            v.tensor_reduce(slotf[:], past[:], AX.X, ALU.add).then_inc(s_k, 1)
            v.wait_ge(s_k, 14)
            v.tensor_scalar(sloti[:], slotf[:], float(E1 - 1), None, ALU.min).then_inc(s_sl, 1)
            v.tensor_tensor(rank[:, 0:T, :], rank[:, 0:T, :], base[:].unsqueeze(1).to_broadcast([P, T, E1]), ALU.add).then_inc(s_k, 1)
            v.wait_ge(s_k, 15)
            v.tensor_tensor(rank[:, 0:T, :], rank[:, 0:T, :], oh[:], ALU.mult).then_inc(s_k, 1)
            v.wait_ge(s_k, 16)
            v.tensor_reduce(pos[:], rank[:, 0:T, :], AX.X, ALU.add).then_inc(s_k, 1)
            v.wait_ge(s_k, 17)
            v.tensor_copy(posi[:], pos[:]).then_inc(s_pl, 1)
            v.wait_ge(s_pl, 1)
            v.tensor_scalar(place_i[:, 0, :], posi[:], 7, None, ALU.arith_shift_right).then_inc(s_pl, 1)
            v.tensor_scalar(place_i[:, 1, :], posi[:], P - 1, None, ALU.bitwise_and).then_inc(s_pl, 1)
            v.wait_ge(s_pl, 3)
            v.tensor_copy(place[:], place_i[:]).then_inc(s_pl, 1)
            v.wait_ge(s_pl, 4)
            v.tensor_tensor(in_slot[:, :, 0:SLOTS], iota[:, 0:SLOTS].unsqueeze(1).to_broadcast([P, T, SLOTS]),
                            place[:, 0, :].unsqueeze(2).to_broadcast([P, T, SLOTS]), ALU.is_equal).then_inc(s_pl, 1)
            v.wait_ge(s_pl, 5)
            v.tensor_tensor(in_slot[:, :, SLOTS:2 * SLOTS], in_slot[:, :, 0:SLOTS].bitcast(F32),
                            token[:].unsqueeze(2).to_broadcast([P, T, SLOTS]), ALU.mult).then_inc(s_sel, 1)
            for a in range(0, T, TG):
                n = min(TG, T - a)
                v.tensor_tensor(in_row[:, a:a + n, :], iota[:].unsqueeze(1).to_broadcast([P, n, P]),
                                place[:, 1, a:a + n].unsqueeze(2).to_broadcast([P, n, P]), ALU.is_equal).then_inc(s_sel, 1)
            v.wait_ge(s_inv, 1)
            v.tensor_copy(src_row[:], ps[:, 6, SLOTS:2 * SLOTS]).then_inc(s_src, 1)
            v.scalar_tensor_tensor(out=unused[:], in0=ps[:, 6, 0:SLOTS], scalar=1.0, in1=spare[:], op0=ALU.subtract, op1=ALU.mult)\
                .then_inc(s_pl, 1)
            v.wait_ge(s_pl, 6)
            v.tensor_tensor(dst_row[:], ps[:, 6, SLOTS:2 * SLOTS], unused[:], ALU.subtract).then_inc(s_dst, 1)

            def slot_output(n):
                y = yg[:, n % 2, :]
                v.wait_ge(s_w[n % NW], 16 * (n // NW + 1))
                v.wait_ge(s_xg[n % NX], 16 * (n // NX + 1))
                if n >= 2:
                    v.wait_ge(s_ys[n % 2], 16 * (n // 2))
                v.tensor_tensor(y[:, 0:D], xg[:, n % NX, :], wexp[:, n % NW, BLOB - D:BLOB], ALU.add).then_inc(s_v, 1)
                v.wait_ge(s_v, 4 * n + 1)
                v.wait_ge(s_f2, n + 1)
                v.tensor_tensor(y[:, 0:D], ps[:, 6 + n % 2, 0:D], y[:, 0:D], ALU.add).then_inc(s_v, 1)
                v.wait_ge(s_v, 4 * n + 2)
                v.bn_stats(st[:, n % 2, :], y[:, 0:D]).then_inc(s_v, 1)
                v.wait_ge(s_v, 4 * n + 3)
                v.bn_aggr(y[:, D:D + 2], st[:, n % 2, :]).then_inc(s_v, 1)
                v.wait_ge(s_v, 4 * n + 4)
                v.scalar_tensor_tensor(out=y[:, 0:D], in0=y[:, 0:D], scalar=y[:, D:D + 1], in1=g2_s[:], op0=ALU.subtract, op1=ALU.mult)\
                    .then_inc(s_y, 1)

            def slot_copy(n):
                v.wait_ge(s_gt, n + 1)
                if n >= 2:
                    v.wait_ge(s_f1, 2 * (n - 1))
                v.tensor_copy(xgT[:, n % 2, :, :], ps[:, n % 2, 0:D].rearrange("p (k c) -> p k c", k=H2)).then_inc(s_gc, 1)

            slot_copy(0)
            slot_copy(1)
            for n in range(SLOTS):
                if n + 2 < SLOTS:
                    slot_copy(n + 2)
                slot_output(n)

            v.wait_ge(s_xb2, T)
            for q in range(len(s_ga2)):
                own = gathered(q)
                v.wait_ge(s_sd, q + 1)
                v.reciprocal(rstd[:, own.start:own.stop], std[:, own.start:own.stop]).then_inc(s_is, 1)
                v.wait_ge(s_is, q + 1)
                v.wait_ge(s_ga2[q], 32 if own.stop == T else 16)
                for t in own:
                    x = xt[0:rows(t), t, :]
                    v.scalar_tensor_tensor(out=x, in0=moe[0:rows(t), t, 0:D], scalar=rstd[0:rows(t), t:t + 1], in1=x,
                                           op0=ALU.mult, op1=ALU.add).then_inc(s_x4, 1)


def layout(i):
    c = np.ascontiguousarray
    row = lambda a: c(a.reshape(1, -1))
    e1, d, hid = i["L1_ffn_W1"].shape
    w1 = i["L1_ffn_W1"].reshape(e1, H2, P, hid).transpose(0, 2, 1, 3).reshape(e1, P, -1)
    w2 = i["L1_ffn_W2"].reshape(e1, hid // P, P, d).transpose(0, 2, 1, 3).reshape(e1, P, -1)
    b1 = i["L1_ffn_b1"].reshape(e1, hid // P, P).transpose(0, 2, 1)
    b2 = np.broadcast_to(i["L1_ffn_b2"][:, None, :], (e1, P, d))
    pairs = lambda a: c(a.reshape(-1, PAIRS, 2, DH).transpose(0, 2, 1, 3).reshape(a.shape))
    halves = lambda a: c(a.reshape(-1, P).T)
    return dict(
        x=c(i["x"]), adjT=c(i["adj"].T), w_gnn=c(i["L0_gnn_weight"]), b_gnn=row(i["L0_gnn_bias"]),
        gate_wT=c(i["L0_ffn_gate_w"].T), w1=c(i["L0_ffn_w1"]), b1T=c(i["L0_ffn_b1"].T), w2=c(i["L0_ffn_w2"]), b2=c(i["L0_ffn_b2"]),
        sw1=c(i["L0_ffn_sw1"]), sb1T=c(i["L0_ffn_sb1"].reshape(-1, P).T), sw2=c(i["L0_ffn_sw2"]), sb2=row(i["L0_ffn_sb2"]),
        w_gnn1T=c(i["L1_gnn_W"].T),
        wq=pairs(i["L1_ffn_Wq"]), bqT=halves(pairs(i["L1_ffn_bq"])), wk=pairs(i["L1_ffn_Wk"]), bkT=halves(pairs(i["L1_ffn_bk"])),
        wv=c(i["L1_ffn_Wv"]), bv=row(i["L1_ffn_bv"]), wo=c(i["L1_ffn_Wo"]), bo=row(i["L1_ffn_bo"]),
        g1=row(i["L1_ffn_g1"]), beta1=row(i["L1_ffn_beta1"]), g2=row(i["L1_ffn_g2"]), beta2=row(i["L1_ffn_beta2"]),
        wg=c(i["L1_ffn_Wg"]), bg=row(i["L1_ffn_bg"]),
        blob=c(np.concatenate([w1, w2, b1, b2], axis=2)),
    )


def kernel(**inputs):
    import concourse.bacc as bacc
    from concourse.bass_utils import run_bass_kernel_spmd

    nc = bacc.Bacc("TRN2", target_bir_lowering=False, num_devices=1)
    arrays, args = {}, []
    for name, a in layout({k: np.asarray(v) for k, v in inputs.items()}).items():
        arrays[f"in_{name}"] = a
        args.append(nc.dram_tensor(f"in_{name}", a.shape, mybir.dt.from_np(a.dtype), kind="ExternalInput").ap())
    args.append(nc.dram_tensor("out_x", (R, D), F32, kind="ExternalOutput").ap())
    build(nc, *args)
    r = run_bass_kernel_spmd(nc, [arrays], core_ids=[0])
    return r.results[0]["out_x"]
```
